# Optimizing a Trainium2 kernel written in Bass

```python
import numpy as np
import jax
import jax.numpy as jnp

def _softmax(x, axis=-1):
    return jax.nn.softmax(x, axis=axis)

def _gelu(x):
    return jax.nn.gelu(x, approximate=True)

def _silu(x):
    return jax.nn.silu(x)

def _sigmoid(x):
    return jax.nn.sigmoid(x)

def _layernorm(x, axis=-1, eps=1e-05):
    m = jnp.mean(x, axis=axis, keepdims=True)
    v = jnp.var(x, axis=axis, keepdims=True)
    return (x - m) / jnp.sqrt(v + eps)

def _scatter_add(tgt, idx, src, axis=0):
    return tgt.at[idx].add(src)

def _segment_sum(src, seg, n):
    return jax.ops.segment_sum(src, seg, n)
kernel_name = 'mk_sandwich_d4_jaxref_r8_04775e'

def setup_inputs(seed: int=0):
    np.random.seed(seed)
    _w = jnp.asarray

    def _L0_attn_setup():
        import jax, jax.numpy as jnp
        import numpy as np
        NEG_FILL = jnp.finfo(jnp.float32).min
        key = jax.random.key(seed)
        k0, k1, k2, k3, k4 = jax.random.split(key, 5)
        B, N, E, D = (4, 512, 128, 32)
        STD = 0.05
        inputs = jax.random.normal(k0, (B, N, E), dtype=jnp.float32)
        Wq = STD * jax.random.normal(k1, (E, D), dtype=jnp.float32)
        Wk = STD * jax.random.normal(k2, (E, D), dtype=jnp.float32)
        Wvdown = STD * jax.random.normal(k3, (E, D), dtype=jnp.float32)
        Wvup = STD * jax.random.normal(k4, (D, E), dtype=jnp.float32)
        return {'inputs': inputs, 'Wq': Wq, 'Wk': Wk, 'Wvdown': Wvdown, 'Wvup': Wvup}
    _L0_attn_in = _L0_attn_setup()

    def _L0_ffn_setup():
        import jax, jax.numpy as jnp
        import numpy as np
        DIM = 128
        HIDDEN = 384
        SCALE = 1.0 / 127.0

        def _dequant(w_int, dtype):
            return w_int.astype(dtype) * jnp.asarray(SCALE, dtype)
        key = jax.random.key(seed)
        k_x, k_g, k_u, k_d = jax.random.split(key, 4)
        x = jax.random.normal(k_x, (4, 256, DIM), dtype=jnp.float32)
        w_gate = jax.random.randint(k_g, (HIDDEN, DIM), -127, 128, dtype=jnp.int32)
        w_up = jax.random.randint(k_u, (HIDDEN, DIM), -127, 128, dtype=jnp.int32)
        w_down = jax.random.randint(k_d, (DIM, HIDDEN), -127, 128, dtype=jnp.int32)
        return {'x': x, 'w_gate': w_gate, 'w_up': w_up, 'w_down': w_down}
    _L0_ffn_in = _L0_ffn_setup()

    def _L1_attn_setup():
        import jax, jax.numpy as jnp
        import numpy as np
        B, T, DIM = (2, 512, 128)
        DEPTH, HEADS = (4, 8)
        DH = DIM // HEADS
        NLOCAL, WINDOW, BUCKET = (4, 128, 64)
        MULT = 4

        def layer_norm(x, g, b, eps=1e-05):
            m = jnp.mean(x, -1, keepdims=True)
            v = jnp.mean(jnp.square(x - m), -1, keepdims=True)
            return (x - m) * jax.lax.rsqrt(v + eps) * g + b

        def causal_linear_attn(q, k, v):
            b, h, n, e = q.shape
            u = n // BUCKET
            q = jax.nn.softmax(q, axis=-1)
            k = jax.nn.elu(k) + 1.0
            bq = q.reshape(b, h, u, BUCKET, e)
            bk = k.reshape(b, h, u, BUCKET, e)
            bv = v.reshape(b, h, u, BUCKET, e)
            k_cum = jnp.cumsum(bk.sum(axis=-2), axis=-2)
            ctx = jnp.einsum('bhund,bhune->bhude', bk, bv)
            ctx = jnp.cumsum(ctx, axis=2)
            ctx = ctx / (k_cum[..., None] + 1e-06)
            ctx = jnp.pad(ctx, ((0, 0), (0, 0), (1, 0), (0, 0), (0, 0)))[:, :, :-1]
            out = jnp.einsum('bhund,bhude->bhune', bq, ctx)
            return out.reshape(b, h, n, e)

        def local_attn(q, k, v):
            b, lh, t, e = q.shape
            bh = b * lh
            nb = t // WINDOW
            bq = q.reshape(bh, nb, WINDOW, e)
            bk = k.reshape(bh, nb, WINDOW, e)
            bv = v.reshape(bh, nb, WINDOW, e)

            def look_around(x):
                padded = jnp.pad(x, ((0, 0), (1, 0), (0, 0), (0, 0)))
                return jnp.concatenate([padded[:, :-1], padded[:, 1:]], axis=2)
            bk2 = look_around(bk)
            bv2 = look_around(bv)
            tix = jnp.arange(t).reshape(1, nb, WINDOW)
            tpad = jnp.pad(tix, ((0, 0), (1, 0), (0, 0)), constant_values=-1)
            kix = jnp.concatenate([tpad[:, :-1], tpad[:, 1:]], axis=2)
            dots = jnp.einsum('bwie,bwje->bwij', bq, bk2) * e ** (-0.5)
            mask_value = -jnp.finfo(dots.dtype).max
            causal_mask = tix[:, :, :, None] < kix[:, :, None, :]
            pad_mask = (kix == -1)[:, :, None, :]
            dots = jnp.where(causal_mask | pad_mask, mask_value, dots)
            attn = jax.nn.softmax(dots, axis=-1)
            out = jnp.einsum('bwij,bwje->bwie', attn, bv2)
            return out.reshape(b, lh, t, e)

        def self_attention(x, Wq, Wk, Wv, Wo, bo):
            b, t, _ = x.shape
            mh = lambda z: z.reshape(b, t, HEADS, DH).transpose(0, 2, 1, 3)
            q, k, v = (mh(x @ Wq), mh(x @ Wk), mh(x @ Wv))
            lo = local_attn(q[:, :NLOCAL], k[:, :NLOCAL], v[:, :NLOCAL])
            go = causal_linear_attn(q[:, NLOCAL:], k[:, NLOCAL:], v[:, NLOCAL:])
            out = jnp.concatenate([lo, go], axis=1)
            out = out.transpose(0, 2, 1, 3).reshape(b, t, DIM)
            return out @ Wo + bo
        key = jax.random.key(seed)
        ks = jax.random.split(key, 8)
        s = 0.02
        rn = lambda k, shape: jax.random.normal(k, shape, dtype=jnp.float32) * s
        return {'x': jax.random.normal(ks[0], (B, T, DIM), dtype=jnp.float32), 'Wq': rn(ks[1], (DEPTH, DIM, DIM)), 'Wk': rn(ks[2], (DEPTH, DIM, DIM)), 'Wv': rn(ks[3], (DEPTH, DIM, DIM)), 'Wo': rn(ks[4], (DEPTH, DIM, DIM)), 'bo': jnp.zeros((DEPTH, DIM), jnp.float32), 'ln1_g': jnp.ones((DEPTH, DIM), jnp.float32), 'ln1_b': jnp.zeros((DEPTH, DIM), jnp.float32), 'W1': rn(ks[5], (DEPTH, DIM, DIM * MULT)), 'b1': jnp.zeros((DEPTH, DIM * MULT), jnp.float32), 'W2': rn(ks[6], (DEPTH, DIM * MULT, DIM)), 'b2': jnp.zeros((DEPTH, DIM), jnp.float32), 'ln2_g': jnp.ones((DEPTH, DIM), jnp.float32), 'ln2_b': jnp.zeros((DEPTH, DIM), jnp.float32)}
    _L1_attn_in = _L1_attn_setup()

    def _L1_ffn_setup():
        import jax, jax.numpy as jnp
        import numpy as np
        B, M, D = (4, 256, 128)
        N, P = (64, 32)
        key = jax.random.key(seed)
        k1, k2, k3, k4 = jax.random.split(key, 4)
        x = jax.random.normal(k1, (B, M, D), dtype=jnp.float32)
        phi = jax.random.normal(k2, (D, N, P), dtype=jnp.float32) * (1.0 / np.sqrt(D))
        W = jax.random.normal(k3, (N, D, D), dtype=jnp.float32) * (1.0 / np.sqrt(D))
        b = jax.random.normal(k4, (N, D), dtype=jnp.float32) * 0.01
        return {'x': x, 'phi': phi, 'W': W, 'b': b}
    _L1_ffn_in = _L1_ffn_setup()

    def _L2_attn_setup():
        import jax, jax.numpy as jnp
        import numpy as np
        EMB = 128
        HEADS = 16
        ATT = EMB // HEADS
        key = jax.random.key(seed)
        ks = jax.random.split(key, 5)
        s = 1.0 / np.sqrt(EMB)
        return {'x': jax.random.normal(ks[0], (4, 256, EMB), dtype=jnp.float32), 'Wq': jax.random.uniform(ks[1], (EMB, HEADS * ATT), jnp.float32, -s, s), 'Wk': jax.random.uniform(ks[2], (EMB, HEADS * ATT), jnp.float32, -s, s), 'Wv': jax.random.uniform(ks[3], (EMB, HEADS * ATT), jnp.float32, -s, s), 'Wo': jax.random.uniform(ks[4], (HEADS * ATT, EMB), jnp.float32, -s, s)}
    _L2_attn_in = _L2_attn_setup()

    def _L2_ffn_setup():
        import jax, jax.numpy as jnp
        import numpy as np
        N_EMBD = 128
        N_STATE = 512
        key = jax.random.key(seed)
        k_x, k_w1, k_b1, k_w2, k_b2 = jax.random.split(key, 5)
        x = jax.random.normal(k_x, (4, 256, N_EMBD), dtype=jnp.float32)
        w1 = jax.random.normal(k_w1, (N_EMBD, N_STATE), dtype=jnp.float32) * (1.0 / np.sqrt(N_EMBD))
        b1 = jax.random.normal(k_b1, (N_STATE,), dtype=jnp.float32) * 0.02
        w2 = jax.random.normal(k_w2, (N_STATE, N_EMBD), dtype=jnp.float32) * (1.0 / np.sqrt(N_STATE))
        b2 = jax.random.normal(k_b2, (N_EMBD,), dtype=jnp.float32) * 0.02
        return {'x': x, 'w1': w1, 'b1': b1, 'w2': w2, 'b2': b2}
    _L2_ffn_in = _L2_ffn_setup()

    def _L3_attn_setup():
        import jax, jax.numpy as jnp
        import numpy as np
        D = 128
        DI = 256
        HS = 16
        PS = DI // HS
        NS = 64
        KC = 4
        CHUNK = 64
        HA = 16
        HKV = 4
        PA = D // HA
        MLP_MULT = 4
        ROPE_BASE = 10000.0
        B_SZ = 2
        L_SEQ = 256

        def rms_norm(x):
            eps = jnp.asarray(jnp.finfo(x.dtype).eps, x.dtype)
            return x * jax.lax.rsqrt(jnp.mean(jnp.square(x), axis=-1, keepdims=True) + eps)

        def silu(x):
            return x * jax.nn.sigmoid(x)

        def apply_rope(x, cos, sin):
            half = x.shape[-1] // 2
            x1, x2 = (x[..., :half], x[..., half:])
            return jnp.concatenate([x1 * cos + x2 * sin, -x1 * sin + x2 * cos], axis=-1)

        def selective_scan(x, A, Bm, Cm, dt, chunk):
            Bb, L, H, P = x.shape
            N = Bm.shape[-1]
            decay = jnp.exp(A * dt)
            nc = L // chunk
            xp = x.reshape(Bb, nc, chunk, H, P).transpose(0, 1, 3, 2, 4)
            Bp = Bm.reshape(Bb, nc, chunk, H, N).transpose(0, 1, 3, 2, 4)
            Cp = Cm.reshape(Bb, nc, chunk, H, N).transpose(0, 1, 3, 2, 4)
            x_dt = xp * dt[None, None, :, None, None]
            idx = jnp.arange(chunk)
            diff = idx[:, None] - idx[None, :]
            Lm = jnp.where(diff >= 0, decay[:, None, None] ** jnp.maximum(diff, 0), 0.0)
            CB = jnp.einsum('bchqn,bchkn->bchqk', Cp, Bp)
            y_diag = jnp.einsum('bchqk,bchkp->bchqp', CB * Lm[None, None], x_dt)
            decay_rev = decay[:, None] ** (chunk - 1 - idx)[None, :]
            states = jnp.einsum('bchtn,bchtp->bchnp', Bp * decay_rev[None, None, :, :, None], x_dt)
            ci = jnp.arange(nc)
            shift = ci[:, None] - ci[None, :] - 1
            cdec = decay ** chunk
            M = jnp.where(shift >= 0, cdec[:, None, None] ** jnp.maximum(shift, 0), 0.0)
            h_carry = jnp.einsum('hij,bjhnp->bihnp', M, states)
            decay_out = decay[:, None] ** (idx + 1)[None, :]
            y_off = jnp.einsum('bchtn,bchnp->bchtp', Cp, h_carry) * decay_out[None, None, :, :, None]
            y = (y_diag + y_off).transpose(0, 1, 3, 2, 4).reshape(Bb, L, H, P)
            return y

        def mlp(n, fc_w, proj_w):
            h = jax.nn.relu(n @ fc_w)
            return jnp.square(h) @ proj_w
        key = jax.random.key(seed)
        ks = jax.random.split(key, 24)
        w = lambda k, shp, s=0.02: jax.random.normal(k, shp, jnp.float32) * s
        dt_init = jax.random.uniform(ks[0], (HS,), jnp.float32, 0.001, 0.1)
        dt_bias = dt_init + jnp.log(-jnp.expm1(-dt_init))
        return {'x': jax.random.normal(ks[1], (B_SZ, L_SEQ, D), jnp.float32), 'in_proj_w': w(ks[2], (D, 2 * DI)), 'conv_w': w(ks[3], (DI, KC), 0.2), 'conv_b': jnp.zeros((DI,), jnp.float32), 'B_proj_w': w(ks[4], (D, HS * NS)), 'C_proj_w': w(ks[5], (D, HS * NS)), 'dt_bias': dt_bias, 'A_log': jnp.log(jnp.arange(1, HS + 1, dtype=jnp.float32)), 'D_param': jnp.ones((HS,), jnp.float32), 'out_proj_w': w(ks[6], (DI, D)), 'resid_mix_m': jnp.stack([jnp.ones(D), jnp.zeros(D)]).astype(jnp.float32), 'mamba_scale': jnp.ones((D,), jnp.float32), 'm_fc_w': w(ks[7], (D, MLP_MULT * D)), 'm_proj_w': w(ks[8], (MLP_MULT * D, D)), 'm_mlp_scale': jnp.ones((D,), jnp.float32), 'resid_mix_a': jnp.stack([jnp.ones(D), jnp.zeros(D)]).astype(jnp.float32), 'q_w': w(ks[9], (D, D)), 'k_w': w(ks[10], (D, HKV * PA)), 'v_w': w(ks[11], (D, HKV * PA)), 'o_w': w(ks[12], (D, D)), 'q_gain': jnp.full((HA,), 1.0, jnp.float32), 'attn_scale': jnp.ones((D,), jnp.float32), 'a_fc_w': w(ks[13], (D, MLP_MULT * D)), 'a_proj_w': w(ks[14], (MLP_MULT * D, D)), 'a_mlp_scale': jnp.ones((D,), jnp.float32)}
    _L3_attn_in = _L3_attn_setup()

    def _L3_ffn_setup():
        import jax, jax.numpy as jnp
        import numpy as np
        N, T, D = (4, 512, 128)
        NUM_EXPERTS = 8
        EXPERT_CAP = 2.0
        MLP_RATIO = 4
        HIDDEN = MLP_RATIO * D
        key = jax.random.key(seed)
        k1, k2, k3, k4 = jax.random.split(key, 4)
        x = jax.random.normal(k1, (N, T, D), dtype=jnp.float32)
        gate_w = jax.random.truncated_normal(k2, -2.0, 2.0, (D, NUM_EXPERTS), dtype=jnp.float32) * 0.02
        w1 = jax.random.normal(k3, (NUM_EXPERTS, D, HIDDEN), dtype=jnp.float32) * 0.02
        w2 = jax.random.normal(k4, (NUM_EXPERTS, HIDDEN, D), dtype=jnp.float32) * 0.02
        return {'x': x, 'gate_w': gate_w, 'w1': w1, 'w2': w2}
    _L3_ffn_in = _L3_ffn_setup()
    _d = {'L0_attn_inputs': _L0_attn_in['inputs'], 'L0_attn_Wq': _L0_attn_in['Wq'], 'L0_attn_Wk': _L0_attn_in['Wk'], 'L0_attn_Wvdown': _L0_attn_in['Wvdown'], 'L0_attn_Wvup': _L0_attn_in['Wvup'], 'L0_ffn_w_gate': _L0_ffn_in['w_gate'], 'L0_ffn_w_up': _L0_ffn_in['w_up'], 'L0_ffn_w_down': _L0_ffn_in['w_down'], 'L1_attn_Wq': _L1_attn_in['Wq'], 'L1_attn_Wk': _L1_attn_in['Wk'], 'L1_attn_Wv': _L1_attn_in['Wv'], 'L1_attn_Wo': _L1_attn_in['Wo'], 'L1_attn_bo': _L1_attn_in['bo'], 'L1_attn_ln1_g': _L1_attn_in['ln1_g'], 'L1_attn_ln1_b': _L1_attn_in['ln1_b'], 'L1_attn_W1': _L1_attn_in['W1'], 'L1_attn_b1': _L1_attn_in['b1'], 'L1_attn_W2': _L1_attn_in['W2'], 'L1_attn_b2': _L1_attn_in['b2'], 'L1_attn_ln2_g': _L1_attn_in['ln2_g'], 'L1_attn_ln2_b': _L1_attn_in['ln2_b'], 'L1_ffn_phi': _L1_ffn_in['phi'], 'L1_ffn_W': _L1_ffn_in['W'], 'L1_ffn_b': _L1_ffn_in['b'], 'L2_attn_Wq': _L2_attn_in['Wq'], 'L2_attn_Wk': _L2_attn_in['Wk'], 'L2_attn_Wv': _L2_attn_in['Wv'], 'L2_attn_Wo': _L2_attn_in['Wo'], 'L2_ffn_w1': _L2_ffn_in['w1'], 'L2_ffn_b1': _L2_ffn_in['b1'], 'L2_ffn_w2': _L2_ffn_in['w2'], 'L2_ffn_b2': _L2_ffn_in['b2'], 'L3_attn_in_proj_w': _L3_attn_in['in_proj_w'], 'L3_attn_conv_w': _L3_attn_in['conv_w'], 'L3_attn_conv_b': _L3_attn_in['conv_b'], 'L3_attn_B_proj_w': _L3_attn_in['B_proj_w'], 'L3_attn_C_proj_w': _L3_attn_in['C_proj_w'], 'L3_attn_dt_bias': _L3_attn_in['dt_bias'], 'L3_attn_A_log': _L3_attn_in['A_log'], 'L3_attn_D_param': _L3_attn_in['D_param'], 'L3_attn_out_proj_w': _L3_attn_in['out_proj_w'], 'L3_attn_resid_mix_m': _L3_attn_in['resid_mix_m'], 'L3_attn_mamba_scale': _L3_attn_in['mamba_scale'], 'L3_attn_m_fc_w': _L3_attn_in['m_fc_w'], 'L3_attn_m_proj_w': _L3_attn_in['m_proj_w'], 'L3_attn_m_mlp_scale': _L3_attn_in['m_mlp_scale'], 'L3_attn_resid_mix_a': _L3_attn_in['resid_mix_a'], 'L3_attn_q_w': _L3_attn_in['q_w'], 'L3_attn_k_w': _L3_attn_in['k_w'], 'L3_attn_v_w': _L3_attn_in['v_w'], 'L3_attn_o_w': _L3_attn_in['o_w'], 'L3_attn_q_gain': _L3_attn_in['q_gain'], 'L3_attn_attn_scale': _L3_attn_in['attn_scale'], 'L3_attn_a_fc_w': _L3_attn_in['a_fc_w'], 'L3_attn_a_proj_w': _L3_attn_in['a_proj_w'], 'L3_attn_a_mlp_scale': _L3_attn_in['a_mlp_scale'], 'L3_ffn_gate_w': _L3_ffn_in['gate_w'], 'L3_ffn_w1': _L3_ffn_in['w1'], 'L3_ffn_w2': _L3_ffn_in['w2']}
    _x0 = _d['L0_attn_inputs']
    _d['L0_attn_inputs'] = jax.random.normal(jax.random.fold_in(jax.random.key(seed), 1), (16, 256, 128), dtype=_x0.dtype)
    del _x0
    return _d

def reference(L0_attn_inputs, L0_attn_Wq, L0_attn_Wk, L0_attn_Wvdown, L0_attn_Wvup, L0_ffn_w_gate, L0_ffn_w_up, L0_ffn_w_down, L1_attn_Wq, L1_attn_Wk, L1_attn_Wv, L1_attn_Wo, L1_attn_bo, L1_attn_ln1_g, L1_attn_ln1_b, L1_attn_W1, L1_attn_b1, L1_attn_W2, L1_attn_b2, L1_attn_ln2_g, L1_attn_ln2_b, L1_ffn_phi, L1_ffn_W, L1_ffn_b, L2_attn_Wq, L2_attn_Wk, L2_attn_Wv, L2_attn_Wo, L2_ffn_w1, L2_ffn_b1, L2_ffn_w2, L2_ffn_b2, L3_attn_in_proj_w, L3_attn_conv_w, L3_attn_conv_b, L3_attn_B_proj_w, L3_attn_C_proj_w, L3_attn_dt_bias, L3_attn_A_log, L3_attn_D_param, L3_attn_out_proj_w, L3_attn_resid_mix_m, L3_attn_mamba_scale, L3_attn_m_fc_w, L3_attn_m_proj_w, L3_attn_m_mlp_scale, L3_attn_resid_mix_a, L3_attn_q_w, L3_attn_k_w, L3_attn_v_w, L3_attn_o_w, L3_attn_q_gain, L3_attn_attn_scale, L3_attn_a_fc_w, L3_attn_a_proj_w, L3_attn_a_mlp_scale, L3_ffn_gate_w, L3_ffn_w1, L3_ffn_w2):

    def _L0_attn_ref(inputs, Wq, Wk, Wvdown, Wvup):
        import jax, jax.numpy as jnp
        import numpy as np
        NEG_FILL = jnp.finfo(jnp.float32).min
        B, N, E = inputs.shape
        D = Wq.shape[1]
        Q = inputs @ Wq
        K = inputs @ Wk
        score = jnp.einsum('bqd,bkd->bqk', Q, K)
        score = score / jnp.sqrt(jnp.float32(D))
        causal = jnp.tril(jnp.ones((N, N), dtype=bool))
        score = jnp.where(causal, score, 0.0)
        score = jnp.where(score != 0, score, NEG_FILL)
        attn = jax.nn.softmax(score, axis=-1)
        V = inputs @ (Wvdown @ Wvup)
        return attn @ V

    def _L0_ffn_ref(x, w_gate, w_up, w_down):
        import jax, jax.numpy as jnp
        import numpy as np
        DIM = 128
        HIDDEN = 384
        SCALE = 1.0 / 127.0

        def _dequant(w_int, dtype):
            return w_int.astype(dtype) * jnp.asarray(SCALE, dtype)
        wg = _dequant(w_gate, x.dtype)
        wu = _dequant(w_up, x.dtype)
        wd = _dequant(w_down, x.dtype)
        gate = jnp.einsum('bsd,hd->bsh', x, wg)
        up = jnp.einsum('bsd,hd->bsh', x, wu)
        h = jax.nn.silu(gate) * up
        return jnp.einsum('bsh,dh->bsd', h, wd)

    def _L1_attn_ref(x, Wq, Wk, Wv, Wo, bo, ln1_g, ln1_b, W1, b1, W2, b2, ln2_g, ln2_b):
        import jax, jax.numpy as jnp
        import numpy as np
        B, T, DIM = (2, 512, 128)
        DEPTH, HEADS = (4, 8)
        DH = DIM // HEADS
        NLOCAL, WINDOW, BUCKET = (4, 128, 64)
        MULT = 4

        def layer_norm(x, g, b, eps=1e-05):
            m = jnp.mean(x, -1, keepdims=True)
            v = jnp.mean(jnp.square(x - m), -1, keepdims=True)
            return (x - m) * jax.lax.rsqrt(v + eps) * g + b

        def causal_linear_attn(q, k, v):
            b, h, n, e = q.shape
            u = n // BUCKET
            q = jax.nn.softmax(q, axis=-1)
            k = jax.nn.elu(k) + 1.0
            bq = q.reshape(b, h, u, BUCKET, e)
            bk = k.reshape(b, h, u, BUCKET, e)
            bv = v.reshape(b, h, u, BUCKET, e)
            k_cum = jnp.cumsum(bk.sum(axis=-2), axis=-2)
            ctx = jnp.einsum('bhund,bhune->bhude', bk, bv)
            ctx = jnp.cumsum(ctx, axis=2)
            ctx = ctx / (k_cum[..., None] + 1e-06)
            ctx = jnp.pad(ctx, ((0, 0), (0, 0), (1, 0), (0, 0), (0, 0)))[:, :, :-1]
            out = jnp.einsum('bhund,bhude->bhune', bq, ctx)
            return out.reshape(b, h, n, e)

        def local_attn(q, k, v):
            b, lh, t, e = q.shape
            bh = b * lh
            nb = t // WINDOW
            bq = q.reshape(bh, nb, WINDOW, e)
            bk = k.reshape(bh, nb, WINDOW, e)
            bv = v.reshape(bh, nb, WINDOW, e)

            def look_around(x):
                padded = jnp.pad(x, ((0, 0), (1, 0), (0, 0), (0, 0)))
                return jnp.concatenate([padded[:, :-1], padded[:, 1:]], axis=2)
            bk2 = look_around(bk)
            bv2 = look_around(bv)
            tix = jnp.arange(t).reshape(1, nb, WINDOW)
            tpad = jnp.pad(tix, ((0, 0), (1, 0), (0, 0)), constant_values=-1)
            kix = jnp.concatenate([tpad[:, :-1], tpad[:, 1:]], axis=2)
            dots = jnp.einsum('bwie,bwje->bwij', bq, bk2) * e ** (-0.5)
            mask_value = -jnp.finfo(dots.dtype).max
            causal_mask = tix[:, :, :, None] < kix[:, :, None, :]
            pad_mask = (kix == -1)[:, :, None, :]
            dots = jnp.where(causal_mask | pad_mask, mask_value, dots)
            attn = jax.nn.softmax(dots, axis=-1)
            out = jnp.einsum('bwij,bwje->bwie', attn, bv2)
            return out.reshape(b, lh, t, e)

        def self_attention(x, Wq, Wk, Wv, Wo, bo):
            b, t, _ = x.shape
            mh = lambda z: z.reshape(b, t, HEADS, DH).transpose(0, 2, 1, 3)
            q, k, v = (mh(x @ Wq), mh(x @ Wk), mh(x @ Wv))
            lo = local_attn(q[:, :NLOCAL], k[:, :NLOCAL], v[:, :NLOCAL])
            go = causal_linear_attn(q[:, NLOCAL:], k[:, NLOCAL:], v[:, NLOCAL:])
            out = jnp.concatenate([lo, go], axis=1)
            out = out.transpose(0, 2, 1, 3).reshape(b, t, DIM)
            return out @ Wo + bo
        for i in range(DEPTH):
            x = x + self_attention(layer_norm(x, ln1_g[i], ln1_b[i]), Wq[i], Wk[i], Wv[i], Wo[i], bo[i])
            h = layer_norm(x, ln2_g[i], ln2_b[i])
            x = x + (jax.nn.gelu(h @ W1[i] + b1[i], approximate=False) @ W2[i] + b2[i])
        return x

    def _L1_ffn_ref(x, phi, W, b):
        import jax, jax.numpy as jnp
        import numpy as np
        B, M, D = (4, 256, 128)
        N, P = (64, 32)
        logits = jnp.einsum('bmd,dnp->bmnp', x, phi)
        dispatch = jax.nn.softmax(logits, axis=0)
        bsz, m, n, p = logits.shape
        combine = jax.nn.softmax(logits.reshape(bsz, m, n * p), axis=-1).reshape(bsz, m, n, p)
        slots = jnp.einsum('bmd,bmnp->bnpd', x, dispatch)
        y = jnp.einsum('bnpd,nde->bnpe', slots, W) + b[None, :, None, :]
        out = jnp.einsum('bnpd,bmnp->bmd', y, combine)
        return out

    def _L2_attn_ref(x, Wq, Wk, Wv, Wo):
        import jax, jax.numpy as jnp
        import numpy as np
        EMB = 128
        HEADS = 16
        ATT = EMB // HEADS
        b, t, _ = x.shape
        h, d = (HEADS, ATT)
        scale = d ** (-0.25)
        q = (x @ Wq).reshape(b, t, h, d) * scale
        k = (x @ Wk).reshape(b, t, h, d) * scale
        v = (x @ Wv).reshape(b, t, h, d)
        dot = jnp.einsum('bqhd,bkhd->bhqk', q, k)
        causal = jnp.tril(jnp.ones((t, t), dtype=bool))
        dot = jnp.where(causal[None, None], dot, -jnp.inf)
        attn = jax.nn.softmax(dot, axis=-1)
        out = jnp.einsum('bhqk,bkhd->bqhd', attn, v).reshape(b, t, h * d)
        return out @ Wo

    def _L2_ffn_ref(x, w1, b1, w2, b2):
        import jax, jax.numpy as jnp
        import numpy as np
        N_EMBD = 128
        N_STATE = 512
        h = jax.nn.gelu(jnp.einsum('bse,eh->bsh', x, w1) + b1, approximate=False)
        return jnp.einsum('bsh,he->bse', h, w2) + b2

    def _L3_attn_ref(x, in_proj_w, conv_w, conv_b, B_proj_w, C_proj_w, dt_bias, A_log, D_param, out_proj_w, resid_mix_m, mamba_scale, m_fc_w, m_proj_w, m_mlp_scale, resid_mix_a, q_w, k_w, v_w, o_w, q_gain, attn_scale, a_fc_w, a_proj_w, a_mlp_scale):
        import jax, jax.numpy as jnp
        import numpy as np
        D = 128
        DI = 256
        HS = 16
        PS = DI // HS
        NS = 64
        KC = 4
        CHUNK = 64
        HA = 16
        HKV = 4
        PA = D // HA
        MLP_MULT = 4
        ROPE_BASE = 10000.0
        B_SZ = 2
        L_SEQ = 256

        def rms_norm(x):
            eps = jnp.asarray(jnp.finfo(x.dtype).eps, x.dtype)
            return x * jax.lax.rsqrt(jnp.mean(jnp.square(x), axis=-1, keepdims=True) + eps)

        def silu(x):
            return x * jax.nn.sigmoid(x)

        def apply_rope(x, cos, sin):
            half = x.shape[-1] // 2
            x1, x2 = (x[..., :half], x[..., half:])
            return jnp.concatenate([x1 * cos + x2 * sin, -x1 * sin + x2 * cos], axis=-1)

        def selective_scan(x, A, Bm, Cm, dt, chunk):
            Bb, L, H, P = x.shape
            N = Bm.shape[-1]
            decay = jnp.exp(A * dt)
            nc = L // chunk
            xp = x.reshape(Bb, nc, chunk, H, P).transpose(0, 1, 3, 2, 4)
            Bp = Bm.reshape(Bb, nc, chunk, H, N).transpose(0, 1, 3, 2, 4)
            Cp = Cm.reshape(Bb, nc, chunk, H, N).transpose(0, 1, 3, 2, 4)
            x_dt = xp * dt[None, None, :, None, None]
            idx = jnp.arange(chunk)
            diff = idx[:, None] - idx[None, :]
            Lm = jnp.where(diff >= 0, decay[:, None, None] ** jnp.maximum(diff, 0), 0.0)
            CB = jnp.einsum('bchqn,bchkn->bchqk', Cp, Bp)
            y_diag = jnp.einsum('bchqk,bchkp->bchqp', CB * Lm[None, None], x_dt)
            decay_rev = decay[:, None] ** (chunk - 1 - idx)[None, :]
            states = jnp.einsum('bchtn,bchtp->bchnp', Bp * decay_rev[None, None, :, :, None], x_dt)
            ci = jnp.arange(nc)
            shift = ci[:, None] - ci[None, :] - 1
            cdec = decay ** chunk
            M = jnp.where(shift >= 0, cdec[:, None, None] ** jnp.maximum(shift, 0), 0.0)
            h_carry = jnp.einsum('hij,bjhnp->bihnp', M, states)
            decay_out = decay[:, None] ** (idx + 1)[None, :]
            y_off = jnp.einsum('bchtn,bchnp->bchtp', Cp, h_carry) * decay_out[None, None, :, :, None]
            y = (y_diag + y_off).transpose(0, 1, 3, 2, 4).reshape(Bb, L, H, P)
            return y

        def mlp(n, fc_w, proj_w):
            h = jax.nn.relu(n @ fc_w)
            return jnp.square(h) @ proj_w
        Bb, L, _ = x.shape
        x0 = x
        xm = resid_mix_m[0][None, None] * x + resid_mix_m[1][None, None] * x0
        n = rms_norm(xm)
        vg = n @ in_proj_w
        value, gate = (vg[..., :DI], vg[..., DI:])
        v_t = value.transpose(0, 2, 1)
        v_conv = jax.lax.conv_general_dilated(v_t, conv_w[:, None, :], (1,), [(KC - 1, 0)], feature_group_count=DI, dimension_numbers=('NCH', 'OIH', 'NCH')) + conv_b[None, :, None]
        value = silu(v_conv).transpose(0, 2, 1).reshape(Bb, L, HS, PS)
        Bm = (xm @ B_proj_w).reshape(Bb, L, HS, NS)
        Cm = (xm @ C_proj_w).reshape(Bb, L, HS, NS)
        dt = jax.nn.softplus(dt_bias)
        A = -jnp.exp(A_log)
        y = selective_scan(value, A, Bm, Cm, dt, CHUNK)
        y = y + D_param[None, None, :, None] * value
        y = y.reshape(Bb, L, DI) * silu(gate) @ out_proj_w
        xm = xm + mamba_scale[None, None] * y
        xm = xm + m_mlp_scale[None, None] * mlp(rms_norm(xm), m_fc_w, m_proj_w)
        xa = resid_mix_a[0][None, None] * xm + resid_mix_a[1][None, None] * x0
        n = rms_norm(xa)
        q = (n @ q_w).reshape(Bb, L, HA, PA).transpose(0, 2, 1, 3)
        k = (n @ k_w).reshape(Bb, L, HKV, PA).transpose(0, 2, 1, 3)
        v = (n @ v_w).reshape(Bb, L, HKV, PA).transpose(0, 2, 1, 3)
        q = rms_norm(q)
        k = rms_norm(k)
        inv_freq = 1.0 / ROPE_BASE ** (jnp.arange(0, PA, 2, dtype=jnp.float32) / PA)
        f = jnp.outer(jnp.arange(L, dtype=jnp.float32), inv_freq)
        cos, sin = (jnp.cos(f)[None, None], jnp.sin(f)[None, None])
        q = apply_rope(q, cos, sin) * q_gain[None, :, None, None]
        k = apply_rope(k, cos, sin)
        G = HA // HKV
        k = jnp.repeat(k, G, axis=1)
        v = jnp.repeat(v, G, axis=1)
        s = jnp.einsum('bhqd,bhkd->bhqk', q, k) / np.float32(np.sqrt(PA))
        mask = jnp.tril(jnp.ones((L, L), bool))
        s = jnp.where(mask[None, None], s, jnp.asarray(-jnp.inf, s.dtype))
        att = jax.nn.softmax(s, axis=-1)
        y = jnp.einsum('bhqk,bhkd->bhqd', att, v).transpose(0, 2, 1, 3).reshape(Bb, L, D)
        xa = xa + attn_scale[None, None] * (y @ o_w)
        xa = xa + a_mlp_scale[None, None] * mlp(rms_norm(xa), a_fc_w, a_proj_w)
        return xa

    def _L3_ffn_ref(x, gate_w, w1, w2):
        import jax, jax.numpy as jnp
        import numpy as np
        N, T, D = (4, 512, 128)
        NUM_EXPERTS = 8
        EXPERT_CAP = 2.0
        MLP_RATIO = 4
        HIDDEN = MLP_RATIO * D
        x = x.astype(jnp.float32)
        n, t, d = x.shape
        k = int(EXPERT_CAP * t / NUM_EXPERTS)
        scores = jnp.einsum('ntd,de->nte', x, gate_w)
        probs = jax.nn.softmax(scores, axis=-1)
        probs = jnp.transpose(probs, (0, 2, 1))
        g, m = jax.lax.top_k(probs, k)
        xin = jax.vmap(lambda xb, mb: xb[mb])(x, m)
        h = jax.nn.gelu(jnp.einsum('nekd,edf->nekf', xin, w1))
        h = jnp.einsum('nekf,efd->nekd', h, w2)
        weighted = g[..., None] * h
        flat_idx = (m + jnp.arange(n, dtype=m.dtype)[:, None, None] * t).reshape(-1)
        out = jnp.zeros((n * t, d), dtype=jnp.float32).at[flat_idx].add(weighted.reshape(-1, d))
        out = out.reshape(n, t, d)
        return out.astype(jnp.bfloat16)
    x = L0_attn_inputs
    x = x + _layernorm(_L0_attn_ref(_layernorm(x, axis=-1), L0_attn_Wq, L0_attn_Wk, L0_attn_Wvdown, L0_attn_Wvup), axis=-1)
    x = x + _layernorm(_L0_ffn_ref(_layernorm(x, axis=-1), L0_ffn_w_gate, L0_ffn_w_up, L0_ffn_w_down), axis=-1)
    x = x + _layernorm(_L1_attn_ref(_layernorm(x, axis=-1), L1_attn_Wq, L1_attn_Wk, L1_attn_Wv, L1_attn_Wo, L1_attn_bo, L1_attn_ln1_g, L1_attn_ln1_b, L1_attn_W1, L1_attn_b1, L1_attn_W2, L1_attn_b2, L1_attn_ln2_g, L1_attn_ln2_b), axis=-1)
    x = x + _layernorm(_L1_ffn_ref(_layernorm(x, axis=-1), L1_ffn_phi, L1_ffn_W, L1_ffn_b), axis=-1)
    x = x + _layernorm(_L2_attn_ref(_layernorm(x, axis=-1), L2_attn_Wq, L2_attn_Wk, L2_attn_Wv, L2_attn_Wo), axis=-1)
    x = x + _layernorm(_L2_ffn_ref(_layernorm(x, axis=-1), L2_ffn_w1, L2_ffn_b1, L2_ffn_w2, L2_ffn_b2), axis=-1)
    x = x + _layernorm(_L3_attn_ref(_layernorm(x, axis=-1), L3_attn_in_proj_w, L3_attn_conv_w, L3_attn_conv_b, L3_attn_B_proj_w, L3_attn_C_proj_w, L3_attn_dt_bias, L3_attn_A_log, L3_attn_D_param, L3_attn_out_proj_w, L3_attn_resid_mix_m, L3_attn_mamba_scale, L3_attn_m_fc_w, L3_attn_m_proj_w, L3_attn_m_mlp_scale, L3_attn_resid_mix_a, L3_attn_q_w, L3_attn_k_w, L3_attn_v_w, L3_attn_o_w, L3_attn_q_gain, L3_attn_attn_scale, L3_attn_a_fc_w, L3_attn_a_proj_w, L3_attn_a_mlp_scale), axis=-1)
    x = x + _layernorm(_L3_ffn_ref(_layernorm(x, axis=-1), L3_ffn_gate_w, L3_ffn_w1, L3_ffn_w2), axis=-1)
    return x

_drawn_inputs = setup_inputs


def setup_inputs(seed=0):
    import zlib

    import numpy as np

    out = dict(_drawn_inputs(seed))
    spreads = {'L1_attn_bo': (0.0, 0.1),
     'L1_attn_ln1_g': (1.0, 0.6),
     'L1_attn_ln1_b': (0.0, 0.559),
     'L1_attn_b1': (0.0, 0.1),
     'L1_attn_b2': (0.0, 0.1),
     'L1_attn_ln2_g': (1.0, 0.6),
     'L1_attn_ln2_b': (0.0, 0.523),
     'L3_attn_conv_b': (0.0, 0.8),
     'L3_attn_D_param': (1.0, 0.6),
     'L3_attn_mamba_scale': (1.0, 0.6),
     'L3_attn_m_mlp_scale': (1.0, 0.6),
     'L3_attn_q_gain': (1.0, 0.6),
     'L3_attn_attn_scale': (1.0, 0.6),
     'L3_attn_a_mlp_scale': (1.0, 0.6)}
    factors = {'L1_attn_Wq': 8.0,
     'L1_attn_Wk': 8.0,
     'L1_ffn_b': 8.0,
     'L2_ffn_b1': 3.321,
     'L2_ffn_b2': 4.058,
     'L3_attn_in_proj_w': 8.0,
     'L3_attn_conv_w': 8.0,
     'L3_attn_B_proj_w': 8.0,
     'L3_attn_C_proj_w': 8.0,
     'L3_attn_dt_bias': 8.0,
     'L3_attn_A_log': 8.0,
     'L3_attn_out_proj_w': 8.0,
     'L3_attn_m_fc_w': 2.929,
     'L3_attn_m_proj_w': 3.311,
     'L3_attn_resid_mix_a': 4.092,
     'L3_attn_q_w': 5.16,
     'L3_attn_k_w': 4.928,
     'L3_attn_v_w': 4.266,
     'L3_attn_o_w': 3.781,
     'L3_attn_a_fc_w': 3.132,
     'L3_attn_a_proj_w': 3.123}
    for name, (base, spread) in spreads.items():
        noise = np.random.default_rng([zlib.crc32(name.encode()), seed]).standard_normal(out[name].shape)
        drawn = base * np.exp(spread * noise) if base else spread * noise
        out[name] = jnp.asarray(drawn.astype(out[name].dtype))
    for name, factor in factors.items():
        out[name] = (out[name] * factor).astype(out[name].dtype)
    return out
```

```python
from contextlib import ExitStack

import numpy as np

import concourse.bass as bass
from concourse import mybir

F32 = mybir.dt.float32
BF16 = mybir.dt.bfloat16
I32 = mybir.dt.int32
ALU = mybir.AluOpType
ACT = mybir.ActivationFunctionType
X_AX = mybir.AxisListType.X
NEG = -3.0e38
FMIN = float(np.finfo(np.float32).min)
EPSB = 1.0013580322265625e-05


def layout(pieces):
    at, off = {}, 0
    for name, n in pieces:
        at[name] = (off, n)
        off += n
    return at, off


WA, NA = layout([("wq0", 32), ("wk0", 32), ("wvd", 128), ("wvu", 128)]
                + [(f"{n}{i}", w) for i in range(4)
                   for n, w in (("l1q", 128), ("l1k", 128), ("l1vqk", 256), ("l1o", 128), ("l1w1", 512), ("l1w2", 512))]
                + [("bo", 512), ("b2", 512)])
WB, NB = layout([("phi", 2048), ("W", 8192)])
WM, NM = layout([("mfc", 512), ("mpj", 512), ("afc", 512), ("apj", 512)])
WC, NC = layout([("l2q", 128), ("l2k", 128), ("l2v", 128), ("l2o", 128), ("l2w1", 512), ("l2w2", 512),
                 ("inp", 512), ("bp", 1024), ("cp", 1024), ("outp", 256),
                 ("qkv", 192), ("ow", 128)])
WD, ND = layout([(f"{n}{e}", 512) for e in range(8) for n in ("w1", "w2")])
WI, NI = layout([("wg", 384), ("wu", 384), ("wd", 384)])
VE, NV = layout([("ln1g", 4), ("ln1b", 4), ("ln2g", 4), ("ln2b", 4), ("b1", 16), ("l2b1", 4), ("convw", 8),
                 ("convb", 2), ("dpar", 2), ("mb", 64), ("dt", 16), ("al", 16),
                 ("qg", 16), ("gate", 8), ("l2b2", 128), ("rm0", 128), ("rm1", 128),
                 ("msc", 128), ("mmsc", 128), ("ra0", 128), ("ra1", 128), ("asc", 128), ("amsc", 128)])
CO, NCO = layout([("ident", 128), ("cmask", 128), ("dif", 128), ("tri", 128), ("qp1", 1),
                  ("rev", 1), ("cos", 8), ("sin", 8), ("hm8", 16), ("hm16", 4), ("bm64", 32), ("bm16", 64)])


class Tok:
    __slots__ = ("eng", "idx")

    def __init__(self, eng, idx):
        self.eng, self.idx = eng, idx


class DmaTok:
    __slots__ = ("sem", "val")

    def __init__(self, sem, val):
        self.sem, self.val = sem, val


def flat(deps):
    for d in deps:
        if d is None:
            continue
        if isinstance(d, (list, tuple)):
            yield from flat(d)
        else:
            yield d


class Queues:

    def __init__(self):
        self.q = {e: [] for e in ("pe", "act", "dve", "pool", "sp")}
        self.pending = {e: [] for e in self.q}

    def op(self, eng, fn, *deps):
        d = list(flat(deps)) + self.pending[eng]
        self.pending[eng] = []
        self.q[eng].append((d, fn))
        return Tok(eng, len(self.q[eng]) - 1)

    def pe(self, fn, *deps):
        return self.op("pe", fn, *deps)

    def act(self, fn, *deps):
        return self.op("act", fn, *deps)

    def dve(self, fn, *deps):
        return self.op("dve", fn, *deps)

    def pool(self, fn, *deps):
        return self.op("pool", fn, *deps)

    def fence(self):
        last = [Tok(e, len(self.q[e]) - 1) for e in ("pe", "act", "dve", "pool") if self.q[e]]
        for e in ("pe", "act", "dve", "pool"):
            self.pending[e] = [t for t in last]
        return last


class Ring:

    def __init__(self, bufs):
        self.free = [(b, []) for b in bufs]

    def take(self):
        assert self.free, "no buffer has been given back"
        return self.free.pop(0)

    def give(self, buf, *toks):
        self.free.append((buf, list(flat(toks))))


def pipe(gens):
    active = []
    gens = list(gens)
    while gens or active:
        for g in list(active):
            try:
                next(g)
            except StopIteration:
                active.remove(g)
        if gens:
            g = gens.pop(0)
            try:
                next(g)
                active.append(g)
            except StopIteration:
                pass


def build(nc, wa, wb, wc, wd, wm, wi, ve, co, step, xin, out):
    ctx = ExitStack()
    with ctx:
        def sb(name, shape, dt=F32):
            return ctx.enter_context(nc.sbuf_tensor(name, shape, dt))

        XA = sb("XA", [128, 32, 128])
        ZX = sb("ZX", [128, 32, 128])
        Z, XN = ZX[:, 0:16, :], ZX[:, 16:32, :]
        AR = sb("AR", [128, 20480])
        wAB = sb("wAB", [128, 8192])
        wCs = sb("wCs", [128, NC])
        vecs = sb("vecs", [128, NV])
        cons = sb("cons", [128, NCO])
        identb = sb("identb", [128, 128], BF16)
        cmaskb = sb("cmaskb", [128, 128], BF16)
        MISC = sb("MISC", [128, 512])
        R8 = sb("R8", [128, 2, 2048])
        R2 = sb("R2", [128, 8, 512])
        RS = sb("RS", [128, 8, 64])
        psum = [ctx.enter_context(nc.psum_tensor(f"ps{i}", [128, 512], F32)) for i in range(8)]

        P = Queues()
        PS = Ring(psum)
        S8 = Ring([R8[:, i, :] for i in range(2)])
        S2 = Ring([R2[:, i, :] for i in range(8)])
        SS = Ring([RS[:, i, :] for i in range(8)])
        sems = []

        def dma(dst, src, *deps):
            s = ctx.enter_context(nc.semaphore(f"s_dma{len(sems)}"))
            sems.append(s)
            P.op("sp", lambda e: (e.dma_start(dst, src).then_inc(s, 16), None)[1], *deps)
            return DmaTok(s, 16)

        def wv(name):
            for tab, t, base in ((WA, wAB, 0), (WM, wAB, 4096), (WC, wCs, 0), (VE, vecs, 0), (CO, cons, 0)):
                if name in tab:
                    o, n = tab[name]
                    return t[:, base + o:base + o + n]
            raise KeyError(name)

        XT = AR[:, 0:2048]
        O = AR[:, 2048:4096].rearrange("p (t c) -> p t c", c=128)
        R0 = AR[:, 4096:20480]
        ident = wv("ident")

        d_co = dma(cons[:, :], co)
        xrows = xin.rearrange("b (t p) d -> p (b t) d", p=128)
        d_x = [dma(XA[:, 8 * i:8 * i + 8, :], xrows[:, 8 * i:8 * i + 8, :]) for i in range(4)]
        d_wa0 = dma(wAB[:, 0:320], wa[:, 0:320])
        wi_s = R0[:, 9216:9216 + NI].bitcast(I32)
        d_wi = dma(wi_s, wi)
        STEPM = R0[:, 8192:8576]
        d_st = dma(STEPM, step)
        d_ve = dma(vecs[:, :], ve)
        d_wa = dma(wAB[:, 320:NA], wa[:, 320:NA])
        d_wc = dma(wCs[:, :], wc)
        t_cb = P.act(lambda e: e.copy(identb[:, :], ident), d_co)
        t_cb = [t_cb, P.act(lambda e: e.copy(cmaskb[:, :], wv("cmask")), d_co)]
        mhalf = MISC[:, 0:4]
        t_mh = P.dve(lambda e: e.memset(mhalf, -0.5))

        def mm(out, lhsT, rhs, start, stop, *deps):
            return P.pe(lambda e: e.matmul(out, lhsT, rhs, start=start, stop=stop), *deps)

        def tr(out, in_, *deps):
            k = in_.shape[0]
            return P.pe(lambda e: e.transpose(out, in_, ident[0:k, 0:k]), d_co, *deps)

        flip = [0]

        def evac(out, in_, *deps):
            flip[0] ^= 1
            if flip[0]:
                return P.act(lambda e: e.copy(out, in_), *deps)
            return P.dve(lambda e: e.tensor_copy(out, in_), *deps)

        def tt(out, a, b, op, *deps):
            return P.dve(lambda e: e.tensor_tensor(out, a, b, op), *deps)

        def ts(out, a, s1, s2, op0, op1, *deps):
            if op1 is None:
                return P.dve(lambda e: e.tensor_scalar(out, a, s1, None, op0), *deps)
            return P.dve(lambda e: e.tensor_scalar(out, a, s1, s2, op0, op1), *deps)

        def norm(src, dst, deps, rms=False, eps=1e-5):
            out = [None] * 16

            def group(g):
                buf, w = SS.take()
                st = [None] * 4
                for i in range(4):
                    st[i] = P.dve(lambda e, i=i, x=src(4 * g + i): e.bn_stats(buf[:, 6 * i:6 * i + 6], x),
                                  w, deps[4 * g + i])
                ag = [P.dve(lambda e, i=i: e.bn_aggr(buf[:, 24 + 2 * i:26 + 2 * i], buf[:, 6 * i:6 * i + 6]), st[i])
                      for i in range(4)]
                mv = buf[:, 24:32].rearrange("p (i c) -> p i c", c=2)
                if rms:
                    a = tt(buf[:, 32:36], mv[:, :, 0], mv[:, :, 0], ALU.mult, ag)
                    b = P.dve(lambda e: e.scalar_tensor_tensor(buf[:, 36:40], buf[:, 32:36], eps, mv[:, :, 1],
                                                               ALU.add, ALU.add), a, ag)
                else:
                    b = ts(buf[:, 36:40], mv[:, :, 1], eps, None, ALU.add, None, ag)
                r = P.pool(lambda e: e.tensor_tensor(buf[:, 40:44], buf[:, 36:40], mhalf, ALU.pow), b, t_mh)
                yield
                last = []
                for i in range(4):
                    t = 4 * g + i
                    rs = buf[:, 40 + i:41 + i]
                    if rms:
                        k = ts(dst(t), src(t), rs, None, ALU.mult, None, r)
                    else:
                        k = ts(dst(t), src(t), buf[:, 24 + 2 * i:25 + 2 * i], rs, ALU.subtract, ALU.mult, r, ag[i])
                    out[t] = k
                    last.append(k)
                SS.give(buf, last)

            pipe(group(g) for g in range(4))
            return out

        def to_T(src, dstT, deps, g_=None, b_=None):
            out = [None] * 16
            for g in range(4):
                ps, w = PS.take()
                for i in range(4):
                    k = tr(ps[:, i * 128:(i + 1) * 128], src(4 * g + i), w, deps[4 * g + i])
                d = dstT[:, g * 512:(g + 1) * 512]
                if g_ is None:
                    v = evac(d, ps[:, :], k)
                else:
                    v = ts(d, ps[:, :], g_, b_, ALU.mult, ALU.add, k, d_ve)
                PS.give(ps, v)
                out[4 * g:4 * g + 4] = [v] * 4
            return out

        def proj_T(dst, w_, srcT, deps, scale=None, wdep=None):
            m = w_.shape[1]
            out = [None] * 16
            for g in range(4):
                ps, w = PS.take()
                k = mm(ps[0:m, :], w_, srcT[:, g * 512:(g + 1) * 512], True, True, w, wdep, deps[4 * g:4 * g + 4])
                d = dst[:, g * 512:(g + 1) * 512]
                if scale is None:
                    v = evac(d, ps[0:m, :], k)
                else:
                    v = ts(d, ps[0:m, :], scale, None, ALU.mult, None, k)
                PS.give(ps, v)
                out[4 * g:4 * g + 4] = [v] * 4
            return out

        def proj_tok(dst, w_, srcT, deps, wdep=None, fin=None):
            out = [None] * 16
            for g in range(4):
                ps, w = PS.take()
                for i in range(4):
                    t = 4 * g + i
                    k = mm(ps[:, i * 128:(i + 1) * 128], srcT[:, t * 128:(t + 1) * 128], w_, True, True,
                           w, wdep, deps[t])
                if fin is None:
                    v = evac(dst[:, 4 * g:4 * g + 4, :], ps[:, :].rearrange("p (t c) -> p t c", c=128), k)
                else:
                    v = fin(ps, g, k)
                PS.give(ps, v)
                out[4 * g:4 * g + 4] = [v] * 4
            return out

        def post(X, Y, deps):
            n = norm(lambda t: Y[:, t, :], lambda t: Y[:, t, :], deps)
            out = []
            for g in range(4):
                s = slice(4 * g, 4 * g + 4)
                k = tt(X[:, s, :], X[:, s, :], Y[:, s, :], ALU.add, n[s])
                out += [k] * 4
            return out

        def pre(X, deps):
            n = norm(lambda t: X[:, t, :], lambda t: XN[:, t, :], deps)
            return n, to_T(lambda t: XN[:, t, :], XT, n)

        def mlp(srcT, deps, w1, b1, nh, kind, w2, fin, wdep, w1b=None):
            out = [None] * 16

            def chunk(g):
                h, hw = S8.take()
                h = h.rearrange("p (j n) -> p j n", n=512)
                xs = srcT[:, g * 512:(g + 1) * 512]
                hk = []
                for j in range(nh):
                    ps, w = PS.take()
                    k = mm(ps[:, :], w1[:, j * 128:(j + 1) * 128], xs, True, True, w, wdep, deps[4 * g:4 * g + 4])
                    if kind == "silu":
                        p2, w_2 = PS.take()
                        k2 = mm(p2[:, :], w1b[:, j * 128:(j + 1) * 128], xs, True, True, w_2, wdep)
                        a = P.act(lambda e, ps=ps, j=j: e.activation(h[:, j, :], ps[:, :], ACT.Silu), hw, k)
                        v = tt(h[:, j, :], h[:, j, :], p2[:, :], ALU.mult, a, k2)
                        PS.give(ps, a)
                        PS.give(p2, v)
                    elif kind == "relu2":
                        a = P.act(lambda e, ps=ps, j=j: e.activation(h[:, j, :], ps[:, :], ACT.Relu), hw, k)
                        v = P.pool(lambda e, j=j: e.tensor_tensor(h[:, j, :], h[:, j, :], h[:, j, :], ALU.mult), a)
                        PS.give(ps, a)
                    else:
                        b = 0.0 if b1 is None else b1[:, j:j + 1]
                        v = P.act(lambda e, ps=ps, j=j, b=b: e.activation(h[:, j, :], ps[:, :], kind, bias=b), hw, k, d_ve)
                        PS.give(ps, v)
                    hk.append(v)
                yield
                ps, w = PS.take()
                for i in range(4):
                    for j in range(nh):
                        k = mm(ps[:, i * 128:(i + 1) * 128], h[:, j, i * 128:(i + 1) * 128], w2[:, j, :],
                               j == 0, j == nh - 1, w, hk)
                S8.give(h.rearrange("p j n -> p (j n)"), k)
                v = fin(ps, g, k)
                PS.give(ps, v)
                out[4 * g:4 * g + 4] = [v] * 4

            pipe(chunk(g) for g in range(4))
            return out

        def v4(ps):
            return ps[:, :].rearrange("p (t c) -> p t c", c=128)

        def add_rep(dst, rep):
            def fin(ps, g, k):
                s = slice(4 * g, 4 * g + 4)
                a = tt(dst[:, s, :], dst[:, s, :], v4(ps), ALU.add, k)
                return tt(dst[:, s, :], dst[:, s, :], rep.unsqueeze(1).to_broadcast([128, 4, 128]), ALU.add, a, d_ve)
            return fin

        def add_scaled(dst, rep):
            def fin(ps, g, k):
                s = slice(4 * g, 4 * g + 4)
                tmp, w = S2.take()
                a = tt(v4(tmp), v4(ps), rep.unsqueeze(1).to_broadcast([128, 4, 128]), ALU.mult, k, w, d_ve)
                b = tt(dst[:, s, :], dst[:, s, :], v4(tmp), ALU.add, a)
                S2.give(tmp, b)
                return [a, b]
            return fin

        def attn_item(q, kT, v0, v1, po0, po1, rs0, rs1, deps, kdeps, done):
            ps, w = PS.take()
            mm(ps[:, 0:128], q[:, 0:128], kT[:, 0:128], True, False, w, deps, kdeps)
            mm(ps[:, 0:128], identb[:, :], cmaskb[:, :], False, True, t_cb)
            mm(ps[:, 128:384], q[:, 128:256], kT[:, 0:256], True, False)
            k = mm(ps[:, 256:384], identb[:, :], cmaskb[:, :], False, True)
            done.append(k)
            st, sw = SS.take()
            m0 = P.dve(lambda e: e.tensor_reduce(st[:, 0:1], ps[:, 0:128], X_AX, ALU.max, negate=True), k, sw)
            m1 = P.dve(lambda e: e.tensor_reduce(st[:, 1:2], ps[:, 128:384], X_AX, ALU.max, negate=True), k, sw)
            p_, pw = S2.take()
            x0 = P.act(lambda e: e.activation(p_[:, 0:128], ps[:, 0:128], ACT.Exp, bias=st[:, 0:1], accum_out=rs0),
                       m0, m1, pw, kdeps)
            x1 = P.act(lambda e: e.activation(p_[:, 128:384], ps[:, 128:384], ACT.Exp, bias=st[:, 1:2],
                                              accum_out=rs1), m1)
            PS.give(ps, x1)
            SS.give(st, x1)
            yield
            pt, w = PS.take()
            for j in range(3):
                k = tr(pt[:, j * 128:(j + 1) * 128], p_[:, j * 128:(j + 1) * 128], w, x0, x1)
            S2.give(p_, k)
            pT, pw = S2.take()
            v = evac(pT[:, 0:384], pt[:, 0:384], k, pw)
            PS.give(pt, v)
            yield
            mm(po0, pT[:, 0:128], v0, True, True, v, deps, kdeps)
            mm(po1, pT[:, 128:256], v0, True, False)
            k = mm(po1, pT[:, 256:384], v1, False, True)
            S2.give(pT, k)
            done.append([k, x0, x1])

        def heads_attn(QT, KT, V, nh, hd, hm, dq, dk, dv):
            out = [None] * 16
            prev = [None]
            for g in range(4):
                RSUM = MISC[:, 64 + 64 * (g % 2):128 + 64 * (g % 2)].rearrange("p (t h) -> p t h", t=4)
                po, pow_ = PS.take()
                done = []
                qm = {}

                def item(h, b, g=g, po=po, pow_=pow_, RSUM=RSUM, done=done, qm=qm):
                    if b == 0:
                        q, qw = S2.take()
                        a = P.pool(lambda e: e.tensor_scalar(q, QT[:, g * 512:(g + 1) * 512], hm[:, h:h + 1], None,
                                                             ALU.mult), dq[4 * g:4 * g + 4], qw, d_co)
                        qm[h] = (q, a, [])
                    q, a, rd = qm[h]
                    t0 = 4 * g + 2 * b
                    c0, c1 = (2 * b) * nh * hd + h * hd, (2 * b + 1) * nh * hd + h * hd
                    it = attn_item(q[:, b * 256:(b + 1) * 256], KT[:, t0 * 128:(t0 + 2) * 128], V(t0, h),
                                   V(t0 + 1, h), po[:, c0:c0 + hd], po[:, c1:c1 + hd],
                                   RSUM[:, 2 * b, h:h + 1], RSUM[:, 2 * b + 1, h:h + 1],
                                   [a, pow_], [dk[t0:t0 + 2], dv[t0:t0 + 2], prev[0]], done)
                    next(it)
                    rd.append(done[-1])
                    if b == 1:
                        S2.give(q, rd)
                    yield
                    yield from it

                pipe(item(h, b) for h in range(nh) for b in range(2))
                r = P.dve(lambda e, RSUM=RSUM: e.reciprocal(RSUM[:, :, 0:nh], RSUM[:, :, 0:nh]), done)
                po4 = po[:, 0:4 * nh * hd].rearrange("p (t h d) -> p t h d", t=4, d=hd)
                for t in range(4):
                    k = tt(O[:, 4 * g + t, 0:nh * hd].rearrange("p (h d) -> p h d", d=hd), po4[:, t, :, :],
                           RSUM[:, t, 0:nh].unsqueeze(2).to_broadcast([128, nh, hd]), ALU.mult, r, done)
                    out[4 * g + t] = k
                PS.give(po, k)
                prev[0] = k
            return out

        d_outs = []
        def l0_attn(X, dx0, dwv):
            n0, x0T = pre(X, dx0)
            QT0, KT0 = R0[0:32, 0:2048], R0[0:32, 2048:4096]
            V0 = R0[:, 4096:6144].rearrange("p (t c) -> p t c", c=128)
            dq = proj_T(QT0, wv("wq0"), XT, x0T, scale=float(32.0 ** -0.5), wdep=d_wa0)
            dk = proj_T(KT0, wv("wk0"), XT, x0T, wdep=d_wa0)
            dv = proj_tok(V0, WV, XT, x0T, wdep=dwv)
            y0 = [None] * 16

            def item(b, qt):
                t = 2 * b + qt
                ps, w = PS.take()
                k = mm(ps[:, 0:256], QT0[:, t * 128:(t + 1) * 128], KT0[:, b * 256:(b + 1) * 256], True, True,
                       w, dq[t], dk[2 * b:2 * b + 2])
                s_, sw = S2.take()
                sc, zz = s_[:, 0:256], s_[:, 256:512]
                o = 128 - 128 * qt
                a = tt(sc, ps[:, 0:256], STEPM[:, o:o + 256], ALU.mult, k, sw, d_st)
                PS.give(ps, a)
                c = ts(zz, sc, 0.0, FMIN, ALU.is_equal, ALU.mult, a)
                d = tt(sc, sc, zz, ALU.add, c)
                st, sw = SS.take()
                m = P.dve(lambda e: e.tensor_reduce(st[:, 0:1], sc, X_AX, ALU.max, negate=True), d, sw)
                x = P.act(lambda e: e.activation(sc, sc, ACT.Exp, bias=st[:, 0:1], accum_out=st[:, 1:2]), m)
                r = P.dve(lambda e: e.reciprocal(st[:, 2:3], st[:, 1:2]), x)
                yield
                pt, w = PS.take()
                for j in range(2):
                    k = tr(pt[:, j * 128:(j + 1) * 128], sc[:, j * 128:(j + 1) * 128], w, x)
                S2.give(s_, k)
                pT, pw = S2.take()
                v = evac(pT[:, 0:256], pt[:, 0:256], k, pw)
                PS.give(pt, v)
                yield
                po, w = PS.take()
                for j in range(2):
                    k = mm(po[:, 0:128], pT[:, j * 128:(j + 1) * 128], V0[:, 2 * b + j, :], j == 0, j == 1,
                           w, v, dv[2 * b + j])
                S2.give(pT, k)
                y0[t] = ts(O[:, t, :], po[:, 0:128], st[:, 2:3], None, ALU.mult, None, k, r)
                PS.give(po, y0[t])
                SS.give(st, y0[t])

            pipe(item(b, qt) for b in range(8) for qt in range(2))
            return post(X, O, y0)

        def fin_O(ps, g, k):
            return evac(O[:, 4 * g:4 * g + 4, :], v4(ps), k)

        def l0_ffn(X, dx, wgu, t_wi):
            n, xT = pre(X, dx)
            y = mlp(XT, xT, wgu[:, 0:384], None, 3, "silu", wgu[:, 768:1152].rearrange("p (j c) -> p j c", c=128),
                    fin_O, t_wi, w1b=wgu[:, 384:768])
            return post(X, O, y)

        halves = [XA[:, 0:16, :], XA[:, 16:32, :]]
        WV = R0[:, 6144:6272]
        ps, w = PS.take()
        k = mm(ps[:, 0:128], wv("wvd")[0:32, :], wv("wvu")[0:32, :], True, True, w, d_wa0)
        dwv = evac(WV, ps[:, 0:128], k)
        PS.give(ps, dwv)
        wgu = R0[:, 10368:10368 + NI]
        t_wi = ts(wgu, wi_s, float(np.float32(1.0 / 127.0)), None, ALU.mult, None, d_wi)
        dxh = []
        for hf in range(2):
            d = l0_attn(halves[hf], [d_x[(16 * hf + t) // 8] for t in range(16)], dwv)
            P.fence()
            dxh.append(l0_ffn(halves[hf], d, wgu, t_wi))
            P.fence()

        QT, KT = R0[:, 0:2048], R0[:, 2048:4096]
        VQ = R0[:, 4096:4096 + 16 * 272].rearrange("p (t c) -> p t c", c=272)
        QG = R0[0:64, 8448:10496]
        CTX = R0[0:64, 10496:10496 + 8 * 3 * 65].rearrange("p (b u c) -> p b u c", b=8, c=65)
        CN = R0[0:64, 12416:12416 + 8 * 3 * 64].rearrange("p (b u c) -> p b u c", b=8, c=64)
        CR = R0[0:64, 14400:14424].rearrange("p (b u) -> p b u", b=8)
        GS = R0[:, 14464:14464 + 64]
        EK = R0[:, 14592:14592 + 1024].rearrange("p (t c) -> p t c", c=64)

        def linear_attn(dv):
            out = [None] * 16
            dctx, dqg = [], []
            for g in range(4):
                s = slice(4 * g, 4 * g + 4)
                q4 = VQ[:, s, 144:208].rearrange("p t (h d) -> p t h d", d=16)
                kk = VQ[:, s, 208:272]
                gs = GS[:, 16 * g:16 * g + 16].rearrange("p (t h) -> p t h", t=4)
                gb = gs.unsqueeze(3).to_broadcast([128, 4, 4, 16])
                a = P.dve(lambda e, q4=q4, gs=gs: e.tensor_reduce(gs, q4, X_AX, ALU.max), dv[s])
                a = tt(q4, q4, gb, ALU.subtract, a)
                a = P.act(lambda e, s=s: e.activation(VQ[:, s, 144:208], VQ[:, s, 144:208], ACT.Exp), a)
                a = P.dve(lambda e, q4=q4, gs=gs: e.tensor_reduce(gs, q4, X_AX, ALU.add), a)
                a = P.dve(lambda e, gs=gs: e.reciprocal(gs, gs), a)
                a = tt(q4, q4, gb, ALU.mult, a)
                ek = EK[:, s, :]
                c = ts(ek, kk, 0.0, None, ALU.min, None, dv[s])
                c = P.act(lambda e, ek=ek: e.activation(ek, ek, ACT.Exp), c)
                c = P.dve(lambda e, ek=ek, kk=kk: e.scalar_tensor_tensor(kk, kk, 0.0, ek, ALU.max, ALU.add), c)
                ps, w = PS.take()
                for j in range(4):
                    k = tr(ps[0:64, j * 128:(j + 1) * 128], VQ[:, 4 * g + j, 144:208], w, a)
                v = evac(QG[:, g * 512:(g + 1) * 512], ps[0:64, :], k)
                PS.give(ps, v)
                dqg.append(v)
                for us in ((0, 2), (1,)):
                    ps, w = PS.take()
                    nu = len(us)
                    for bb in range(2):
                        for n, u in enumerate(us):
                            t, r, c_ = 4 * g + 2 * bb + u // 2, 64 * (u % 2), (nu * bb + n) * 65
                            k = mm(ps[0:64, c_:c_ + 65], VQ[r:r + 64, t, 208:272], VQ[r:r + 64, t, 64:129],
                                   True, True, w, c)
                    v = evac(CTX[:, 2 * g:2 * g + 2, us[0]:3:2, :],
                             ps[0:64, 0:130 * nu].rearrange("p (b u c) -> p b u c", b=2, c=65), k)
                    PS.give(ps, v)
                    dctx.append(v)
            c = dctx
            for u in (1, 2):
                c = tt(CTX[:, :, u, :], CTX[:, :, u, :], CTX[:, :, u - 1, :], ALU.add, c)
            c = ts(CR, CTX[:, :, :, 64], 1e-6, None, ALU.add, None, c)
            c = P.dve(lambda e: e.reciprocal(CR, CR), c)
            a = tt(CN, CTX[:, :, :, 0:64], CR.unsqueeze(3).to_broadcast([64, 8, 3, 64]), ALU.mult, c)
            CNf = CN.rearrange("p b u c -> p (b u) c")
            a = tt(CNf, CNf, wv("bm16")[0:64, :].unsqueeze(1).to_broadcast([64, 24, 64]), ALU.mult, a, d_co)
            for g in range(4):
                ps, w = PS.take()
                for bb in range(2):
                    b = 2 * g + bb
                    for u in range(1, 4):
                        j, r = 2 * bb + u // 2, 64 * (u % 2)
                        k = mm(ps[r:r + 64, j * 64:(j + 1) * 64],
                               QG[:, b * 256 + u * 64:b * 256 + (u + 1) * 64], CN[:, b, u - 1, :], True, True,
                               w, a, dqg[g])
                p3 = ps[:, 0:256].rearrange("p (t c) -> p t c", c=64)
                o3 = O[:, 4 * g:4 * g + 4, 64:128]
                pz = P.dve(lambda e, o3=o3: e.memset(o3[0:64, 0:4:2, :], 0.0))
                v1 = P.act(lambda e, o3=o3, p3=p3: e.copy(o3[64:128, 0:4:2, :], p3[64:128, 0:4:2, :]), k)
                v2 = P.act(lambda e, o3=o3, p3=p3: e.copy(o3[:, 1:4:2, :], p3[:, 1:4:2, :]), k)
                PS.give(ps, v2)
                for j in range(4):
                    out[4 * g + j] = [pz, v1, v2]
            return out

        def l1_attn(X, dx):
            dz = norm(lambda t: X[:, t, :], lambda t: Z[:, t, :], dx)
            for i in range(4):
                def col(n, i=i):
                    return wv(n)[:, i:i + 1]
                n = norm(lambda t: Z[:, t, :], lambda t: XN[:, t, :], dz)
                hT = to_T(lambda t: XN[:, t, :], XT, n, col("ln1g"), col("ln1b"))
                dq = proj_T(QT, wv(f"l1q{i}"), XT, hT, scale=0.25, wdep=d_wa)
                dk = proj_T(KT, wv(f"l1k{i}"), XT, hT, wdep=d_wa)
                dv = [None] * 16
                for g in range(8):
                    ps, w = PS.take()
                    for j in range(2):
                        t = 2 * g + j
                        k = mm(ps[:, j * 256:(j + 1) * 256], XT[:, t * 128:(t + 1) * 128], wv(f"l1vqk{i}"),
                               True, True, w, hT[t], d_wa)
                    p2 = ps[:, :].rearrange("p (t c) -> p t c", c=256)
                    a = P.act(lambda e, g=g, p2=p2: e.copy(VQ[:, 2 * g:2 * g + 2, 0:128], p2[:, :, 0:128]), k)
                    c = P.act(lambda e, g=g, p2=p2: e.copy(VQ[:, 2 * g:2 * g + 2, 144:272], p2[:, :, 128:256]), k)
                    PS.give(ps, c)
                    dv[2 * g] = dv[2 * g + 1] = [a, c, t_one]
                ka = heads_attn(QT, KT, lambda t, h: VQ[:, t, 16 * h:16 * h + 16], 4, 16, wv("hm16"), dq, dk, dv)
                kl = linear_attn(dv)
                oT = to_T(lambda t: O[:, t, :], XT, [[ka[t], kl[t], hT, dq, dk, dv] for t in range(16)])
                dz = proj_tok(None, wv(f"l1o{i}"), XT, oT, wdep=d_wa,
                              fin=add_rep(Z, wv("bo")[:, i * 128:(i + 1) * 128]))
                n = norm(lambda t: Z[:, t, :], lambda t: XN[:, t, :], dz)
                P.fence()
                hT = to_T(lambda t: XN[:, t, :], XT, n, col("ln2g"), col("ln2b"))
                dz = mlp(XT, hT, wv(f"l1w1{i}"), wv("b1")[:, 4 * i:4 * i + 4], 4, ACT.Gelu,
                         wv(f"l1w2{i}").rearrange("p (j c) -> p j c", c=128),
                         add_rep(Z, wv("b2")[:, i * 128:(i + 1) * 128]), d_wa)
                P.fence()
            return post(X, Z, dz)

        t_one = P.dve(lambda e: e.memset(VQ[:, :, 128:129], 1.0))
        for hf in range(2):
            dxh[hf] = l1_attn(halves[hf], dxh[hf])
            last = P.fence()

        phi = wAB[:, 0:2048]
        d_phi = dma(phi, wb[:, 0:2048], last)
        d_wm = dma(wAB[:, 4096:4096 + NM], wm, last)
        XTA = AR[:, 0:4096]
        LR = Ring([AR[:, 4096 + 2048 * i:6144 + 2048 * i] for i in range(3)])
        DR = Ring([AR[:, 10240 + 2048 * i:12288 + 2048 * i] for i in range(2)])
        YA = AR[:, 14336:18432].rearrange("p (b m e) -> p b m e", b=16, m=2)
        SL = AR[:, 18432:20480].rearrange("p (b s) -> p b s", b=16)
        WR = Ring([wAB[:, 2048 + 512 * i:2560 + 512 * i] for i in range(4)])
        XN4 = ZX[:, :, :].rearrange("p (b m) d -> p b m d", m=2)
        xTh = []
        for hf in range(2):
            n = norm(lambda t: halves[hf][:, t, :], lambda t: ZX[:, 16 * hf + t, :], dxh[hf])
            xTh += to_T(lambda t: ZX[:, 16 * hf + t, :], XTA[:, 2048 * hf:2048 * hf + 2048], n)
        MR = MISC[:, 64:96].rearrange("p (m b) -> p m b", m=2)
        LS = MISC[:, 96:128].rearrange("p (m b) -> p m b", m=2)
        smoe = {"acc": None, "stat": [None, None]}

        def wload(q):
            b_, w = WR.take()
            return b_, dma(b_, wb[:, 2048 + 512 * q:2560 + 512 * q], w, last)

        wch = {q: wload(q) for q in range(3)}

        def unit(q, mt):
            L, lw = LR.take()
            L3 = L.rearrange("p (b s) -> p b s", b=16)
            ev = []
            for g in range(4):
                ps, w = PS.take()
                for i in range(4):
                    t = 2 * (4 * g + i) + mt
                    k = mm(ps[:, i * 128:(i + 1) * 128], XTA[:, t * 128:(t + 1) * 128],
                           phi[:, q * 128:(q + 1) * 128], True, True, w, xTh[t], d_phi)
                v = evac(L3[:, 4 * g:4 * g + 4, :], v4(ps), k, lw)
                PS.give(ps, v)
                ev.append(v)
            D, dw = DR.take()
            D3 = D.rearrange("p (b s) -> p b s", b=16)
            Ds = D.rearrange("p (b s) -> p s b", b=16)
            tmp, tw = S2.take()
            m1 = tmp[:, 0:128]
            mb = m1.unsqueeze(1).to_broadcast([128, 16, 128])
            a = P.dve(lambda e: e.tensor_reduce(m1, L.rearrange("p (b s) -> p s b", b=16), X_AX, ALU.max), ev, tw)
            a0 = tt(D3, L3, mb, ALU.subtract, a, dw)
            x = P.act(lambda e: e.activation(D, D, ACT.Exp), a0)
            st, sw = SS.take()
            tm, al, rs, nm = st[:, 0:16], st[:, 16:32], st[:, 32:48], st[:, 48:64]
            mr, ls = MR[:, mt, :], LS[:, mt, :]
            pst = smoe["stat"][mt]
            b1 = P.dve(lambda e: e.tensor_reduce(tm, L3, X_AX, ALU.max), ev, sw)
            if q == 0:
                b2 = P.dve(lambda e: e.tensor_copy(mr, tm), b1)
                ax = None
            else:
                b2 = tt(tm, tm, mr, ALU.max, b1, pst)
                b3 = tt(al, mr, tm, ALU.subtract, b2)
                ax = P.act(lambda e: e.activation(al, al, ACT.Exp), b3)
                b2 = P.dve(lambda e: e.tensor_copy(mr, tm), b3)
            b4 = ts(nm, mr, -1.0, None, ALU.mult, None, b2)
            ex = None
            for b in range(16):
                ex = P.act(lambda e, b=b: e.activation(L3[:, b, :], L3[:, b, :], ACT.Exp, bias=nm[:, b:b + 1],
                                                       accum_out=rs[:, b:b + 1]), b4, a0)
            if q == 0:
                c = P.dve(lambda e: e.tensor_copy(ls, rs), ex)
            else:
                c = tt(ls, ls, al, ALU.mult, ax, pst)
                c = tt(ls, ls, rs, ALU.add, c, ex)
            smoe["stat"][mt] = [c, b2]
            a = P.dve(lambda e: e.tensor_reduce(m1, Ds, X_AX, ALU.add), x)
            a = P.dve(lambda e: e.reciprocal(m1, m1), a)
            a = tt(D3, D3, mb, ALU.mult, a)
            S2.give(tmp, a)
            yield
            if mt == 0:
                smoe["acc"] = [PS.take() for _ in range(4)]
            acc = smoe["acc"]
            for b in range(16):
                k = P.pe(lambda e, b=b: e.matmul(acc[b // 4][0][:, (b % 4) * 128:(b % 4 + 1) * 128],
                                                 XN4[:, b, mt, :], D3[:, b, :], start=(mt == 0 and b % 4 == 0),
                                                 stop=(mt == 1), skip_group_check=True), acc[b // 4][1], a)
            DR.give(D, k)
            smoe[("E", q, mt)] = (L, L3, st, al, [ex, ax], c)
            if mt == 0:
                return
            sl = []
            for g in range(4):
                v = evac(SL[:, 4 * g:4 * g + 4, :], v4(acc[g][0]), k, smoe.get("slread"))
                PS.give(acc[g][0], v)
                sl.append(v)
            yield
            yt, yw = S8.take()
            yt3 = yt.rearrange("p (b s) -> p b s", b=16)
            W, dW = wch[q]
            kk = []
            for i in range(4):
                ps, w = PS.take()
                k = mm(ps[:, :].rearrange("p (b s) -> p b s", b=16), W[:, i * 128:(i + 1) * 128],
                       SL[:, :, i * 32:(i + 1) * 32], True, True, w, sl, dW)
                bb = wv("mb")[:, 4 * q + i:4 * q + i + 1]
                v = ts(yt3[:, :, i * 32:(i + 1) * 32], ps[:, :].rearrange("p (b s) -> p b s", b=16), bb, None,
                       ALU.add, None, k, yw, d_ve)
                PS.give(ps, v)
                kk.append(v)
            smoe["slread"] = k
            WR.give(W, k)
            if q + 3 < 16:
                wch[q + 3] = wload(q + 3)
            ym, mw = S8.take()
            ym3 = ym.rearrange("p (b e) -> p b e", b=16)
            ky = []
            for g in range(4):
                pt, w = PS.take()
                for i in range(4):
                    b = 4 * g + i
                    k = tr(pt[:, i * 128:(i + 1) * 128], yt3[:, b, :], w, kk)
                v = evac(ym3[:, 4 * g:4 * g + 4, :], v4(pt), k, mw)
                PS.give(pt, v)
                ky.append(v)
            S8.give(yt, k)
            for m_ in range(2):
                L_, E3, st_, al_, kx, kc = smoe.pop(("E", q, m_))
                for g in range(4):
                    pt, w = PS.take()
                    for i in range(4):
                        k = tr(pt[:, i * 128:(i + 1) * 128], E3[:, 4 * g + i, :], w, kx)
                    eT, ew = S2.take()
                    v = evac(eT, pt[:, :], k, ew)
                    PS.give(pt, v)
                    if g == 3:
                        LR.give(L_, k)
                    po, w = PS.take()
                    for i in range(4):
                        b = 4 * g + i
                        k = mm(po[:, i * 128:(i + 1) * 128], eT[:, i * 128:(i + 1) * 128], ym3[:, b, :], True, True,
                               w, v, ky[g])
                    S2.give(eT, k)
                    for i in range(4):
                        b = 4 * g + i
                        pi = po[:, i * 128:(i + 1) * 128]
                        if q == 0:
                            v = P.dve(lambda e, b=b, pi=pi, m_=m_: e.tensor_copy(YA[:, b, m_, :], pi), k)
                        else:
                            v = P.dve(lambda e, b=b, pi=pi, m_=m_, al_=al_: e.scalar_tensor_tensor(
                                YA[:, b, m_, :], YA[:, b, m_, :], al_[:, b:b + 1], pi, ALU.mult, ALU.add),
                                k, kx, smoe.get(("ya", b, m_)))
                        smoe[("ya", b, m_)] = v
                    PS.give(po, [smoe[("ya", 4 * g + i, m_)] for i in range(4)])
                SS.give(st_, v, kc)
            S8.give(ym, k)

        pipe(unit(q, mt) for q in range(16) for mt in range(2))
        rl = P.dve(lambda e: e.reciprocal(LS, LS), smoe["stat"])
        P.fence()
        kya = []
        for b in range(16):
            for m_ in range(2):
                kya.append(ts(YA[:, b, m_, :], YA[:, b, m_, :], LS[:, m_, b:b + 1], None, ALU.mult, None, rl))
        YT_ = YA.rearrange("p b m e -> p (b m) e")
        for hf in range(2):
            dxh[hf] = post(halves[hf], YT_[:, 16 * hf:16 * hf + 16, :], kya[16 * hf:16 * hf + 16])
        P.fence()

        V2 = R0[:, 4096:6144].rearrange("p (t c) -> p t c", c=128)

        def l2_attn(X, dx):
            n, xT = pre(X, dx)
            sc8 = float(np.float32(8.0 ** -0.25))
            dq = proj_T(QT, wv("l2q"), XT, xT, scale=sc8, wdep=d_wc)
            dk = proj_T(KT, wv("l2k"), XT, xT, scale=sc8, wdep=d_wc)
            dv = proj_tok(V2, wv("l2v"), XT, xT, wdep=d_wc)
            ka = heads_attn(QT, KT, lambda t, h: V2[:, t, 8 * h:8 * h + 8], 16, 8, wv("hm8"), dq, dk, dv)
            oT = to_T(lambda t: O[:, t, :], XT, [[a_, dq, dk, dv] for a_ in ka])
            y = proj_tok(O, wv("l2o"), XT, [[oT, o_] for o_ in oT], wdep=d_wc)
            return post(X, O, y)

        def fin_b2(ps, g, k):
            return tt(O[:, 4 * g:4 * g + 4, :], v4(ps), wv("l2b2").unsqueeze(1).to_broadcast([128, 4, 128]),
                      ALU.add, k, d_ve)

        def l2_ffn(X, dx):
            n, xT = pre(X, dx)
            y = mlp(XT, xT, wv("l2w1"), wv("l2b1"), 4, ACT.Gelu, wv("l2w2").rearrange("p (j c) -> p j c", c=128),
                    fin_b2, d_wc)
            return post(X, O, y)

        for hf in range(2):
            dxh[hf] = l2_attn(halves[hf], dxh[hf])
            P.fence()
            dxh[hf] = l2_ffn(halves[hf], dxh[hf])
            P.fence()

        EPS = float(np.finfo(np.float32).eps)
        DTv, Av = MISC[:, 200:216], MISC[:, 216:232]
        DOUT, DREV = MISC[:, 232:248], MISC[:, 248:264]
        W2_, W3_, W4_, W5_ = (MISC[:, 264 + 16 * i:280 + 16 * i] for i in range(4))
        W1_ = wv("dt")
        a = ts(W2_, W1_, -1.0, None, ALU.mult, None, d_ve)
        a = tt(W2_, W2_, W1_, ALU.min, a)
        u = P.act(lambda e: e.activation(W2_, W2_, ACT.Exp), a)
        w1p = ts(W3_, W2_, 1.0, None, ALU.add, None, u)
        ln = P.act(lambda e: e.activation(W4_, W3_, ACT.Ln), w1p)
        d1 = ts(W3_, W3_, -1.0, None, ALU.add, None, ln)
        eq = ts(W5_, W3_, 0.0, None, ALU.is_equal, None, d1)
        a = tt(W3_, W3_, W5_, ALU.add, eq)
        a = P.dve(lambda e: e.reciprocal(W3_, W3_), a)
        a = tt(W3_, W3_, W2_, ALU.mult, a)
        a = tt(W4_, W4_, W3_, ALU.mult, a)
        a2 = tt(W5_, W5_, W2_, ALU.mult, a)
        a = tt(W4_, W4_, W5_, ALU.add, a, a2)
        a = P.dve(lambda e: e.scalar_tensor_tensor(DTv, W1_, 0.0, W4_, ALU.max, ALU.add), a)
        ea = P.act(lambda e: e.activation(Av, wv("al"), ACT.Exp), d_ve)
        da = P.dve(lambda e: e.scalar_tensor_tensor(Av, Av, -1.0, DTv, ALU.mult, ALU.mult), ea, a)
        HORD = list(range(0, 16, 2)) + list(range(1, 16, 2))
        LM = wAB[:, 6144:8192].rearrange("p (h q) -> p h q", h=16)
        kl = []
        for n, h in enumerate(HORD):
            k = P.act(lambda e, n=n, h=h: e.activation(LM[:, n, :], wv("dif"), ACT.Exp, scale=Av[:, h:h + 1]),
                      da, d_co)
            kl.append(tt(LM[:, n, :], LM[:, n, :], wv("tri"), ALU.mult, k))
        a = ts(W2_, Av, wv("qp1"), None, ALU.mult, None, da)
        k1 = P.act(lambda e: e.activation(DOUT, W2_, ACT.Exp), a)
        a = ts(W3_, Av, wv("rev"), None, ALU.mult, None, da)
        k2 = P.act(lambda e: e.activation(DREV, W3_, ACT.Exp), a)
        k2 = tt(DREV, DREV, DTv, ALU.mult, k2)
        kpar = [k1, k2] + kl
        P.fence()

        def mix(dst, a_, ra, b_, rb, g, *deps):
            s = slice(4 * g, 4 * g + 4)
            tmp, w = S2.take()
            k1 = tt(v4(tmp), b_[:, s, :], rb.unsqueeze(1).to_broadcast([128, 4, 128]), ALU.mult, w, d_ve, *deps)
            k2 = tt(dst[:, s, :], a_[:, s, :], ra.unsqueeze(1).to_broadcast([128, 4, 128]), ALU.mult, d_ve, *deps)
            k3 = tt(dst[:, s, :], dst[:, s, :], v4(tmp), ALU.add, k1, k2)
            S2.give(tmp, k3)
            return [k3] * 4

        def bc16(x):
            return x.unsqueeze(2).to_broadcast([128, 16, 16])

        def mamba(X, dx):
            dn = norm(lambda t: X[:, t, :], lambda t: XN[:, t, :], dx)
            dz = []
            for g in range(4):
                dz += mix(Z, XN, wv("rm0"), XN, wv("rm1"), g, dn[4 * g:4 * g + 4])
            dxm = to_T(lambda t: Z[:, t, :], XT, dz)
            NT = AR[:, 2048:4096]
            VT = R0[:, 0:4096].rearrange("p (c n) -> p c n", c=2)
            GT = R0[:, 4096:8192].rearrange("p (c n) -> p c n", c=2)
            BT = R0[:, 8192:12288].rearrange("p (h n) -> p h n", h=8)
            CT = R0[:, 12288:16384].rearrange("p (h n) -> p h n", h=8)
            TMPN = R0[:, 8192:10240].rearrange("p (t c) -> p t c", c=128)
            RAW = R0[:, 12288:16384].rearrange("p (c n) -> p c n", c=2)
            nn = norm(lambda t: Z[:, t, :], lambda t: TMPN[:, t, :], dz, rms=True, eps=EPS)
            dnT = to_T(lambda t: TMPN[:, t, :], NT, nn)
            dval, dgat = [], []
            for c in range(2):
                dr = proj_T(RAW[:, c, :], wv("inp")[:, c * 128:(c + 1) * 128], NT, dnT, wdep=d_wc)
                cw = wv("convw")[:, 4 * c:4 * c + 4]
                cb = wv("convb")[:, c:c + 1]
                r0 = RAW[:, c, :].rearrange("p (b n) -> p b n", n=256)
                o0 = VT[:, c, :].rearrange("p (b n) -> p b n", n=256)
                k = ts(VT[:, c, :], RAW[:, c, :], cw[:, 3:4], cb, ALU.mult, ALU.add, dr, d_ve)
                for s in (1, 2, 3):
                    k = P.dve(lambda e, r0=r0, o0=o0, cw=cw, s=s: e.scalar_tensor_tensor(
                        o0[:, :, s:256], r0[:, :, 0:256 - s], cw[:, 3 - s:4 - s], o0[:, :, s:256],
                        ALU.mult, ALU.add), k)
                dval.append(P.act(lambda e, c=c: e.activation(VT[:, c, :], VT[:, c, :], ACT.Silu), k))
            for c in range(2):
                for g in range(4):
                    ps, w = PS.take()
                    k = mm(ps[:, :], wv("inp")[:, 256 + c * 128:256 + (c + 1) * 128], NT[:, g * 512:(g + 1) * 512],
                           True, True, w, dnT[4 * g:4 * g + 4], d_wc)
                    v = P.act(lambda e, ps=ps, c=c, g=g: e.activation(GT[:, c, g * 512:(g + 1) * 512], ps[:, :],
                                                                      ACT.Silu), k)
                    PS.give(ps, v)
                    dgat.append(v)
            P.fence()
            H2, hw2 = S2.take()
            HS = H2[:, 0:256].rearrange("p (j c) -> p j c", j=8)
            dy = [None] * 16
            hk = hw2
            ko = None
            prevb = None
            for g in range(4):
                kb = []
                for h in range(8):
                    for dst, nme in ((BT, "bp"), (CT, "cp")):
                        ps, w = PS.take()
                        k = mm(ps[:, :], wv(nme)[:, h * 128:(h + 1) * 128], XT[:, g * 512:(g + 1) * 512], True, True,
                               w, dxm, d_wc)
                        v = evac(dst[:, h, :], ps[:, :], k, prevb)
                        PS.give(ps, v)
                        kb.append(v)

                def tile(j, g=g, kb=kb):
                    nonlocal hk, ko, kyy, kst, kpj
                    t = 4 * g + j
                    odd = j % 2
                    sl = slice(j * 128, (j + 1) * 128)
                    gl = slice(t * 128, (t + 1) * 128)
                    ps, w = PS.take()
                    for c in range(2):
                        k = tr(ps[:, c * 128:(c + 1) * 128], VT[:, c, gl], w, dval)
                    xv, xw = S2.take()
                    vt3 = ps[:, 0:256].rearrange("p (h d) -> p h d", d=16)
                    kx1 = tt(xv[:, 0:256].rearrange("p (h d) -> p h d", d=16), vt3, bc16(DTv), ALU.mult, k, xw, kpar)
                    kx2 = kx1
                    if not odd:
                        kx2 = tt(xv[:, 256:512].rearrange("p (h d) -> p h d", d=16), vt3, bc16(DREV), ALU.mult,
                                 k, xw, kpar)
                    PS.give(ps, kx1, kx2)
                    py, yw = PS.take()
                    for c in range(4):
                        pc, w = PS.take()
                        for i in range(4):
                            h = HORD[4 * c + i]
                            r = 64 * (h % 2)
                            k = mm(pc[:, i * 128:(i + 1) * 128], BT[r:r + 64, h // 2, sl], CT[r:r + 64, h // 2, sl],
                                   True, True, w, kb)
                        cb, cw_ = S2.take()
                        v = tt(cb, pc[:, :], LM[:, 4 * c:4 * c + 4, :].rearrange("p h q -> p (h q)"), ALU.mult,
                               k, cw_, kpar)
                        PS.give(pc, v)
                        for i in range(4):
                            h = HORD[4 * c + i]
                            kyy = mm(py[:, h * 16:(h + 1) * 16], cb[:, i * 128:(i + 1) * 128],
                                     xv[:, h * 16:(h + 1) * 16], True, True, yw, v, kx1)
                        S2.give(cb, kyy)
                    ys, ysw = S2.take()
                    if odd:
                        po, pw = PS.take()
                        for jj in range(8):
                            ko = mm(po[:, jj * 32:(jj + 1) * 32], CT[:, jj, sl], HS[:, jj, :], True, True, pw, kb, hk)
                        a = tt(ys[:, 0:256].rearrange("p (h d) -> p h d", d=16),
                               po[:, 0:256].rearrange("p (h d) -> p h d", d=16), bc16(DOUT), ALU.mult, ko, ysw, kpar)
                        PS.give(po, a)
                        a = tt(ys[:, 0:256], ys[:, 0:256], py[:, 0:256], ALU.add, a, kyy)
                    else:
                        a = evac(ys[:, 0:256], py[:, 0:256], kyy, ysw)
                        bt = []
                        for c in range(2):
                            ps, w = PS.take()
                            for i in range(4):
                                k = tr(ps[:, i * 128:(i + 1) * 128], BT[:, 4 * c + i, sl], w, kb)
                            bb, bw = S2.take()
                            v = evac(bb, ps[:, :], k, bw)
                            PS.give(ps, v)
                            bt.append((bb, v))
                        ps, w = PS.take()
                        for jj in range(8):
                            bb, v = bt[jj // 4]
                            kst = mm(ps[:, jj * 32:(jj + 1) * 32], bb[:, (jj % 4) * 128:(jj % 4 + 1) * 128],
                                     xv[:, 256 + jj * 32:256 + (jj + 1) * 32], True, True, w, v, kx2)
                        for bb, v in bt:
                            S2.give(bb, kst)
                        hk = tt(HS, ps[:, 0:256].rearrange("p (j c) -> p j c", j=8),
                                wv("bm64").unsqueeze(1).to_broadcast([128, 8, 32]), ALU.mult, kst, hk, ko, d_co)
                        PS.give(ps, hk)
                    PS.give(py, a)
                    S2.give(xv, kyy, kst)
                    ps, w = PS.take()
                    for c in range(2):
                        k = tr(ps[:, c * 128:(c + 1) * 128], ys[:, c * 128:(c + 1) * 128], w, a)
                    S2.give(ys, k)
                    yt, ytw = S2.take()
                    ks = []
                    for c in range(2):
                        v = P.dve(lambda e, c=c, ps=ps, yt=yt, gl=gl: e.scalar_tensor_tensor(
                            yt[:, c * 128:(c + 1) * 128], VT[:, c, gl], wv("dpar")[:, c:c + 1],
                            ps[:, c * 128:(c + 1) * 128], ALU.mult, ALU.add), k, ytw)
                        ks.append(tt(yt[:, c * 128:(c + 1) * 128], yt[:, c * 128:(c + 1) * 128], GT[:, c, gl],
                                     ALU.mult, v, dgat))
                    PS.give(ps, ks)
                    ps, w = PS.take()
                    for c in range(2):
                        kpj = mm(ps[:, 0:128], yt[:, c * 128:(c + 1) * 128], wv("outp")[:, c * 128:(c + 1) * 128],
                                 c == 0, c == 1, w, ks)
                    S2.give(yt, kpj)
                    tmp, tw = S2.take()
                    a = tt(tmp[:, 0:128], ps[:, 0:128], wv("msc"), ALU.mult, kpj, tw)
                    PS.give(ps, a)
                    dy[t] = tt(Z[:, t, :], Z[:, t, :], tmp[:, 0:128], ALU.add, a)
                    S2.give(tmp, dy[t])

                kyy = kst = kpj = None
                for j in range(4):
                    tile(j)
                prevb = [kyy, ko, kst]
            S2.give(H2, hk)
            return dy

        YN = R0[:, 6144:8192].rearrange("p (t c) -> p t c", c=128)
        QK = R0[:, 8192:8192 + 16 * 192].rearrange("p (t c) -> p t c", c=192)
        QR = R0[:, 11392:11392 + 2048].rearrange("p (t c) -> p t c", c=128)
        KR = R0[:, 13440:13440 + 2048].rearrange("p (t c) -> p t c", c=128)

        def relu_mlp(dz, fc, pj, sc):
            nn = norm(lambda t: Z[:, t, :], lambda t: YN[:, t, :], dz, rms=True, eps=EPS)
            nT = to_T(lambda t: YN[:, t, :], XT, nn)
            return mlp(XT, nT, wv(fc), None, 4, "relu2", wv(pj).rearrange("p (j c) -> p j c", c=128),
                       add_scaled(Z, wv(sc)), d_wm)

        def gqa(dza):
            nn = norm(lambda t: Z[:, t, :], lambda t: YN[:, t, :], dza, rms=True, eps=EPS)
            nT = to_T(lambda t: YN[:, t, :], XT, nn)
            dqk = [None] * 16
            for g in range(8):
                ps, w = PS.take()
                for j in range(2):
                    t = 2 * g + j
                    k = mm(ps[:, j * 192:(j + 1) * 192], XT[:, t * 128:(t + 1) * 128], wv("qkv"), True, True,
                           w, nT[t], d_wc)
                v = evac(QK[:, 2 * g:2 * g + 2, :], ps[:, 0:384].rearrange("p (t c) -> p t c", c=192), k)
                PS.give(ps, v)
                dqk[2 * g] = dqk[2 * g + 1] = v
            dqr = [None] * 16

            def rope(t):
                j = t % 2
                s2, sw = S2.take()
                ss, ssw = SS.take()
                qk = QK[:, t, 0:160]
                q3 = qk.rearrange("p (h d) -> p h d", d=8)
                sq = s2[:, 0:160]
                a = tt(sq, qk, qk, ALU.mult, dqk[t], sw)
                a = P.dve(lambda e: e.tensor_reduce(ss[:, 0:20], sq.rearrange("p (h d) -> p h d", d=8),
                                                    X_AX, ALU.add), a, ssw)
                a = ts(ss[:, 0:20], ss[:, 0:20], 0.125, EPS, ALU.mult, ALU.add, a)
                a = P.pool(lambda e: e.tensor_tensor(ss[:, 20:40], ss[:, 0:20],
                                                     mhalf[:, 0:1].to_broadcast([128, 20]), ALU.pow), a)
                yield
                b1_ = tt(ss[:, 20:36], ss[:, 20:36], wv("qg"), ALU.mult, a, d_ve)
                b1_ = ts(ss[:, 20:36], ss[:, 20:36], float(np.float32(8.0 ** -0.5)), None, ALU.mult, None, b1_)
                a = tt(q3, q3, ss[:, 20:40].unsqueeze(2).to_broadcast([128, 20, 8]), ALU.mult, b1_)
                SS.give(ss, a)
                cos = wv("cos")[:, 4 * j:4 * j + 4].unsqueeze(1).to_broadcast([128, 20, 4])
                sin = wv("sin")[:, 4 * j:4 * j + 4].unsqueeze(1).to_broadcast([128, 20, 4])
                xa, xb = q3[:, :, 0:4], q3[:, :, 4:8]
                r3 = s2[:, 0:160].rearrange("p (h d) -> p h d", d=8)
                u3 = s2[:, 160:320].rearrange("p (h d) -> p h d", d=8)
                e1 = tt(r3[:, :, 0:4], xa, cos, ALU.mult, a, d_co)
                e2 = tt(u3[:, :, 0:4], xb, sin, ALU.mult, a)
                e3 = tt(r3[:, :, 4:8], xb, cos, ALU.mult, a)
                e4 = tt(u3[:, :, 4:8], xa, sin, ALU.mult, a)
                o1 = tt(q3[:, :, 0:4], r3[:, :, 0:4], u3[:, :, 0:4], ALU.add, e1, e2, e4)
                o2 = tt(q3[:, :, 4:8], r3[:, :, 4:8], u3[:, :, 4:8], ALU.subtract, e3, e4, e2)
                S2.give(s2, o1, o2)
                k5 = P.pool(lambda e: e.tensor_copy(QR[:, t, :], QK[:, t, 0:128]), o1, o2)
                kr4 = KR[:, t, :].rearrange("p (g r d) -> p g r d", g=4, d=8)
                k3_ = QK[:, t, 128:160].rearrange("p (g d) -> p g d", d=8)
                kk = [P.pool(lambda e, r=r: e.tensor_copy(kr4[:, :, r, :], k3_), o1, o2) for r in range(4)]
                dqr[t] = [k5, kk]

            pipe(rope(t) for t in range(16))
            P.fence()
            dq = to_T(lambda t: QR[:, t, :], QT, dqr)
            dk = to_T(lambda t: KR[:, t, :], KT, dqr)
            ka = heads_attn(QT, KT, lambda t, h: QK[:, t, 160 + 8 * (h // 4):168 + 8 * (h // 4)], 16, 8, wv("hm8"),
                            dq, dk, dqk)
            oT = to_T(lambda t: O[:, t, :], XT, ka)
            return proj_tok(None, wv("ow"), XT, oT, wdep=d_wc, fin=add_scaled(Z, wv("asc")))

        for hf in range(2):
            X = halves[hf]
            dy = mamba(X, dxh[hf])
            P.fence()
            dz = relu_mlp(dy, "mfc", "mpj", "mmsc")
            P.fence()
            dza = []
            for g in range(4):
                dza += mix(Z, Z, wv("ra0"), XN, wv("ra1"), g, dz[4 * g:4 * g + 4])
            dz = gqa(dza)
            P.fence()
            dz = relu_mlp(dz, "afc", "apj", "amsc")
            dxh[hf] = post(X, Z, dz)
            last = P.fence()

        OA = AR[:, 4096:8192].rearrange("p (t c) -> p t c", c=128)
        d_we = [dma(AR[:, 8192 + 1024 * e:9216 + 1024 * e], wd[:, 1024 * e:1024 * (e + 1)], last) for e in range(8)]
        xTh = []
        for hf in range(2):
            n = norm(lambda t: halves[hf][:, t, :], lambda t: ZX[:, 16 * hf + t, :], dxh[hf])
            xTh += to_T(lambda t: ZX[:, 16 * hf + t, :], XTA[:, 2048 * hf:2048 * hf + 2048], n)
        GM = AR[:, 16384:16640].rearrange("p (m c) -> p m c", m=2)
        ps, w = PS.take()
        for t in range(32):
            k = mm(ps[:, t * 8:(t + 1) * 8], XTA[:, t * 128:(t + 1) * 128], wv("gate"), True, True, w, xTh[t], d_ve)
        PRB = AR[:, 16640:16896]
        PR2 = AR[:, 16896:17152]
        st = AR[:, 17152:17216]
        p3 = ps[:, 0:256].rearrange("p (t e) -> p t e", e=8)
        s3 = PRB.rearrange("p (t e) -> p t e", e=8)
        a = P.dve(lambda e: e.tensor_reduce(st[:, 0:32], p3, X_AX, ALU.max), k)
        a = tt(s3, p3, st[:, 0:32].unsqueeze(2).to_broadcast([128, 32, 8]), ALU.subtract, a)
        PS.give(ps, a)
        a = P.act(lambda e: e.activation(PRB, PRB, ACT.Exp), a)
        a = P.dve(lambda e: e.tensor_reduce(st[:, 32:64], s3, X_AX, ALU.add), a)
        a = P.dve(lambda e: e.reciprocal(st[:, 32:64], st[:, 32:64]), a)
        kp = tt(PR2.rearrange("p (m b e) -> p b m e", m=2, b=16), PRB.rearrange("p (b m e) -> p b m e", m=2, b=16),
                st[:, 32:64].rearrange("p (b m) -> p b m", m=2).unsqueeze(3).to_broadcast([128, 16, 2, 8]),
                ALU.mult, a)
        ps, w = PS.take()
        for m_ in range(2):
            k = tr(ps[:, m_ * 128:(m_ + 1) * 128], PR2[:, m_ * 128:(m_ + 1) * 128], w, kp)
        pp, wk = AR[:, 17216:17472], AR[:, 17472:17728]
        m8 = AR[:, 17728:17736]
        v1 = P.dve(lambda e, s_=ps[:, 0:256]: e.tensor_copy(pp, s_), k)
        a = v2 = P.dve(lambda e, s_=ps[:, 0:256]: e.tensor_copy(wk, s_), k)
        PS.give(ps, v1, v2)
        for r in range(8):
            a = P.dve(lambda e: e.max(m8, wk), a)
            a = P.dve(lambda e: e.match_replace(wk, m8, wk, -1.0), a)
        a = ts(wk, wk, 0.0, None, ALU.is_lt, None, a)
        a = tt(wk, wk, pp, ALU.mult, a, v1)
        ps, w = PS.take()
        for m_ in range(2):
            k = tr(ps[:, m_ * 128:(m_ + 1) * 128], wk[:, m_ * 128:(m_ + 1) * 128], w, a)
        kg = P.dve(lambda e: e.tensor_copy(GM, ps[:, 0:256].rearrange("p (m c) -> p m c", m=2)), k)
        PS.give(ps, kg)
        dyp = [None] * 32
        for ex in range(8):
            we = AR[:, 8192 + 1024 * ex:9216 + 1024 * ex]
            for hf in range(2):
                def fin_e(ps, g, k, ex=ex, hf=hf):
                    vs = []
                    for j in range(4):
                        t = 16 * hf + 4 * g + j
                        c = 8 * (t // 2) + ex
                        gm = GM[:, t % 2, c:c + 1]
                        pj = ps[:, j * 128:(j + 1) * 128]
                        if ex == 0:
                            v = ts(OA[:, t, :], pj, gm, None, ALU.mult, None, k, kg)
                        else:
                            v = P.dve(lambda e, t=t, pj=pj, gm=gm: e.scalar_tensor_tensor(
                                OA[:, t, :], pj, gm, OA[:, t, :], ALU.mult, ALU.add), k, dyp[t])
                        dyp[t] = v
                        vs.append(v)
                    return vs
                mlp(XTA[:, 2048 * hf:2048 * hf + 2048], xTh[16 * hf:16 * hf + 16], we[:, 0:512], None, 4,
                    ACT.Gelu_apprx_tanh, we[:, 512:1024].rearrange("p (j c) -> p j c", c=128), fin_e, d_we[ex])
        YB = AR[:, 0:2048].bitcast(BF16).rearrange("p (t c) -> p t c", c=128)
        SB = AR[:, 17792:17856].bitcast(BF16)
        SF = AR[:, 17920:18304]
        P.fence()
        kf = [P.dve(lambda e, g=g: e.tensor_copy(YB[:, 4 * g:4 * g + 4, :], OA[:, 4 * g:4 * g + 4, :]), dyp)
              for g in range(8)]
        ag = []
        for t in range(32):
            a = P.dve(lambda e, t=t: e.bn_stats(SF[:, 6 * t:6 * t + 6], YB[:, t, :]), kf[t // 4])
            ag.append(P.dve(lambda e, t=t: e.bn_aggr(SF[:, 192 + 2 * t:194 + 2 * t], SF[:, 6 * t:6 * t + 6]), a))
        mv = SF[:, 192:256].rearrange("p (t c) -> p t c", c=2)
        mb_, vb_, eb_, sb_ = SB[:, 0:32], SB[:, 32:64], SB[:, 64:96], SB[:, 96:128]
        a1 = P.dve(lambda e: e.tensor_copy(mb_, mv[:, :, 0]), ag)
        a2 = P.dve(lambda e: e.tensor_copy(vb_, mv[:, :, 1]), ag)
        a3_ = ts(eb_, vb_, EPSB, None, ALU.add, None, a2)
        s_ = P.act(lambda e: e.activation(sb_, eb_, ACT.Sqrt), a3_)
        rr = P.dve(lambda e: e.reciprocal(SF[:, 256:288], sb_), s_)
        mf = P.dve(lambda e: e.tensor_copy(SF[:, 288:320], mb_), a1)
        orows = out.rearrange("b (t p) d -> p (b t) d", p=128)
        outs = []
        for t in range(32):
            a = ts(YB[:, t, :], YB[:, t, :], SF[:, 288 + t:289 + t], None, ALU.subtract, None, mf)
            a = ts(YB[:, t, :], YB[:, t, :], SF[:, 256 + t:257 + t], None, ALU.mult, None, a, rr)
            outs.append(tt(XA[:, t, :], XA[:, t, :], YB[:, t, :], ALU.add, a))
            if t % 8 == 7:
                d_out = dma(orows[:, t - 7:t + 1, :], XA[:, t - 7:t + 1, :], outs[t - 7:t + 1])
                d_outs.append(d_out)
        for d_out in d_outs:
            P.op("sp", lambda e: None, d_out)

        used = {e: set() for e in P.q}
        for e in P.q:
            for deps, _ in P.q[e]:
                for d in deps:
                    if isinstance(d, Tok):
                        used[d.eng].add(d.idx)
        STEP = 4000
        where = {}
        for e in P.q:
            n = 0
            for idx in sorted(used[e]):
                where[(e, idx)] = (n // STEP, n % STEP + 1)
                n += 1
        esem = {}
        for e in P.q:
            if used[e]:
                for c in range((len(used[e]) + STEP - 1) // STEP):
                    esem[(e, c)] = ctx.enter_context(nc.semaphore(f"s_{e}{c}"))

        def stream(name, eng):
            seen = {}
            seen_dma = set()
            for idx, (deps, fn) in enumerate(P.q[name]):
                need = {}
                for d in deps:
                    if isinstance(d, DmaTok):
                        if id(d) not in seen_dma:
                            seen_dma.add(id(d))
                            eng.wait_ge(d.sem, d.val)
                    else:
                        if d.eng == name == "pe":
                            continue
                        need[d.eng] = max(need.get(d.eng, (-1, 0)), where[(d.eng, d.idx)])
                for p, at in need.items():
                    if seen.get(p, (-1, 0)) < at:
                        seen[p] = at
                        eng.wait_ge(esem[(p, at[0])], at[1])
                ins = fn(eng)
                if idx in used[name] and ins is not None:
                    ins.then_inc(esem[(name, where[(name, idx)][0])], 1)

        block = ctx.enter_context(nc.Block())

        @block.sync
        def _(eng):
            stream("sp", eng)

        @block.gpsimd
        def _(eng):
            stream("pool", eng)

        @block.scalar
        def _(eng):
            stream("act", eng)

        @block.tensor
        def _(eng):
            stream("pe", eng)

        @block.vector
        def _(eng):
            stream("dve", eng)


def shape_constants():
    c = np.zeros((128, NCO), np.float32)
    i = np.arange(128)

    def put(name, v):
        o, n = CO[name]
        c[:v.shape[0], o:o + n] = v

    put("ident", np.eye(128, dtype=np.float32))
    put("cmask", np.where(i[None, :] > i[:, None], np.float32(NEG), np.float32(0)))
    put("dif", np.maximum(i[None, :] - i[:, None], 0).astype(np.float32))
    put("tri", (i[None, :] >= i[:, None]).astype(np.float32))
    put("qp1", (i[:, None] + 1).astype(np.float32))
    put("rev", (127 - i[:, None]).astype(np.float32))
    inv = (np.float32(1.0) / np.power(np.float32(10000.0), np.arange(0, 8, 2, dtype=np.float32) / np.float32(8)))
    f = np.outer(np.arange(256, dtype=np.float32), inv.astype(np.float32)).astype(np.float32)
    put("cos", np.cos(f).astype(np.float32).reshape(2, 128, 4).transpose(1, 0, 2).reshape(128, 8))
    put("sin", np.sin(f).astype(np.float32).reshape(2, 128, 4).transpose(1, 0, 2).reshape(128, 8))
    put("hm8", (i[:, None] // 8 == np.arange(16)[None, :]).astype(np.float32))
    put("hm16", (i[:, None] // 16 == np.arange(4)[None, :]).astype(np.float32))
    put("bm64", (i[:, None] // 64 == np.arange(32)[None, :] // 16).astype(np.float32))
    put("bm16", (np.arange(64)[:, None] // 16 == np.arange(64)[None, :] // 16).astype(np.float32))
    return c


def step_constant():
    s, i = np.arange(384), np.arange(128)
    return (s[None, :] - 128 <= i[:, None]).astype(np.float32)


def kernel(**inputs):
    import numpy as _np
    import concourse.bacc as _bacc
    from concourse import mybir as _mybir
    from concourse.bass_utils import run_bass_kernel_spmd as _run

    I = {k: _np.asarray(v) for k, v in inputs.items()}

    def pack(tab, n, parts, dt=_np.float32):
        a = _np.zeros((128, n), dt)
        for name, v in parts.items():
            o, w = tab[name]
            assert v.shape[1] == w, (name, v.shape, w)
            a[:v.shape[0], o:o + w] = v
        return a

    def ktiles(w):
        k = w.shape[0] // 128
        return w.reshape(k, 128, -1).transpose(1, 0, 2).reshape(128, -1)

    def rep(v):
        v = v.reshape(1, -1)
        return _np.broadcast_to(v, (128, v.shape[1]))

    pa = {"wq0": I["L0_attn_Wq"], "wk0": I["L0_attn_Wk"], "wvd": I["L0_attn_Wvdown"].T, "wvu": I["L0_attn_Wvup"]}
    for i in range(4):
        q, k, v = I["L1_attn_Wq"][i], I["L1_attn_Wk"][i], I["L1_attn_Wv"][i]
        pa[f"l1q{i}"], pa[f"l1k{i}"] = q, k
        pa[f"l1vqk{i}"] = _np.concatenate([v, q[:, 64:], k[:, 64:]], axis=1)
        pa[f"l1o{i}"] = I["L1_attn_Wo"][i]
        pa[f"l1w1{i}"] = I["L1_attn_W1"][i]
        pa[f"l1w2{i}"] = ktiles(I["L1_attn_W2"][i])
    pb = {"phi": I["L1_ffn_phi"].reshape(128, 2048), "W": I["L1_ffn_W"].transpose(1, 0, 2).reshape(128, 8192)}
    pa["bo"], pa["b2"] = rep(I["L1_attn_bo"]), rep(I["L1_attn_b2"])
    pc = {"l2q": I["L2_attn_Wq"], "l2k": I["L2_attn_Wk"], "l2v": I["L2_attn_Wv"], "l2o": I["L2_attn_Wo"],
          "l2w1": I["L2_ffn_w1"], "l2w2": ktiles(I["L2_ffn_w2"]), "inp": I["L3_attn_in_proj_w"],
          "bp": I["L3_attn_B_proj_w"], "cp": I["L3_attn_C_proj_w"], "outp": ktiles(I["L3_attn_out_proj_w"]),
          "qkv": _np.concatenate([I["L3_attn_q_w"], I["L3_attn_k_w"], I["L3_attn_v_w"]], axis=1),
          "ow": I["L3_attn_o_w"]}
    pd = {}
    for e in range(8):
        pd[f"w1{e}"], pd[f"w2{e}"] = I["L3_ffn_w1"][e], ktiles(I["L3_ffn_w2"][e])
    pm = {"mfc": I["L3_attn_m_fc_w"], "mpj": ktiles(I["L3_attn_m_proj_w"]),
          "afc": I["L3_attn_a_fc_w"], "apj": ktiles(I["L3_attn_a_proj_w"])}
    pi = {"wg": I["L0_ffn_w_gate"].T, "wu": I["L0_ffn_w_up"].T, "wd": ktiles(I["L0_ffn_w_down"].T)}

    pv = {"ln1g": I["L1_attn_ln1_g"].T, "ln1b": I["L1_attn_ln1_b"].T, "ln2g": I["L1_attn_ln2_g"].T,
          "ln2b": I["L1_attn_ln2_b"].T,
          "b1": I["L1_attn_b1"].reshape(4, 4, 128).transpose(2, 0, 1).reshape(128, 16),
          "l2b1": I["L2_ffn_b1"].reshape(4, 128).T,
          "convw": I["L3_attn_conv_w"].reshape(2, 128, 4).transpose(1, 0, 2).reshape(128, 8),
          "convb": I["L3_attn_conv_b"].reshape(2, 128).T,
          "dpar": _np.repeat(I["L3_attn_D_param"], 16).reshape(2, 128).T,
          "mb": I["L1_ffn_b"].T, "dt": rep(I["L3_attn_dt_bias"]), "al": rep(I["L3_attn_A_log"]),
          "qg": rep(I["L3_attn_q_gain"]), "gate": I["L3_ffn_gate_w"], "l2b2": rep(I["L2_ffn_b2"]), "rm0": rep(I["L3_attn_resid_mix_m"][0]),
          "rm1": rep(I["L3_attn_resid_mix_m"][1]), "msc": rep(I["L3_attn_mamba_scale"]),
          "mmsc": rep(I["L3_attn_m_mlp_scale"]), "ra0": rep(I["L3_attn_resid_mix_a"][0]),
          "ra1": rep(I["L3_attn_resid_mix_a"][1]), "asc": rep(I["L3_attn_attn_scale"]),
          "amsc": rep(I["L3_attn_a_mlp_scale"])}
    arrays = {
        "wa": pack(WA, NA, pa), "wb": pack(WB, NB, pb), "wc": pack(WC, NC, pc), "wd": pack(WD, ND, pd), "wm": pack(WM, NM, pm),
        "wi": pack(WI, NI, pi, _np.int32), "ve": pack(VE, NV, pv), "co": shape_constants(), "step": step_constant(),
        "xin": _np.ascontiguousarray(I["L0_attn_inputs"]),
    }
    nc = _bacc.Bacc("TRN2", target_bir_lowering=False, num_devices=1)
    args = [nc.dram_tensor(k, a.shape, _mybir.dt.from_np(a.dtype), kind="ExternalInput").ap()
            for k, a in arrays.items()]
    o = nc.dram_tensor("y", (16, 256, 128), _mybir.dt.float32, kind="ExternalOutput").ap()
    build(nc, *args, o)
    r = _run(nc, [arrays], core_ids=[0])
    return r.results[0]["y"]
```

```python
from contextlib import ExitStack

import numpy as np

import concourse.bass as bass
from concourse import mybir

F32 = mybir.dt.float32
BF16 = mybir.dt.bfloat16
I32 = mybir.dt.int32
ALU = mybir.AluOpType
ACT = mybir.ActivationFunctionType
X_AX = mybir.AxisListType.X
NEG = -3.0e38
FMIN = float(np.finfo(np.float32).min)
NS2 = 8
STAG0, STAG1 = 30, 60
EPSB = 1.0013580322265625e-05


def layout(pieces):
    at, off = {}, 0
    for name, n in pieces:
        at[name] = (off, n)
        off += n
    return at, off


WA, NA = layout([("wq0", 32), ("wk0", 32), ("wvd", 128), ("wvu", 128)]
                + [(f"{n}{i}", w) for i in range(4)
                   for n, w in (("l1q", 128), ("l1k", 128), ("l1vqk", 256), ("l1o", 128), ("l1w1", 512), ("l1w2", 512))]
                + [("bo", 512), ("b2", 512)])
WB, NB = layout([("phi", 2048), ("W", 8192)])
WM, NM = layout([("mfc", 512), ("mpj", 512), ("afc", 512), ("apj", 512)])
WC, NC = layout([("l2q", 128), ("l2k", 128), ("l2v", 128), ("l2o", 128), ("l2w1", 512), ("l2w2", 512),
                 ("inp", 512), ("bp", 1024), ("cp", 1024), ("outp", 256),
                 ("qkv", 192), ("ow", 128)])
WD, ND = layout([(f"{n}{e}", 512) for e in range(8) for n in ("w1", "w2")])
WI, NI = layout([("wg", 384), ("wu", 384), ("wd", 384)])
VE, NV = layout([("ln1g", 4), ("ln1b", 4), ("ln2g", 4), ("ln2b", 4), ("b1", 16), ("l2b1", 4), ("convw", 8),
                 ("convb", 2), ("dpar", 2), ("mb", 64), ("dt", 16), ("al", 16),
                 ("qg", 16), ("gate", 8), ("l2b2", 128), ("rm0", 128), ("rm1", 128),
                 ("msc", 128), ("mmsc", 128), ("ra0", 128), ("ra1", 128), ("asc", 128), ("amsc", 128)])
CO, NCO = layout([("ident", 128), ("cmask", 128), ("dif", 128), ("tri", 128), ("qp1", 1),
                  ("rev", 1), ("cos", 8), ("sin", 8), ("hm8", 16), ("hm16", 4), ("bm64", 32), ("bm16", 64)])


class Tok:
    __slots__ = ("eng", "idx")

    def __init__(self, eng, idx):
        self.eng, self.idx = eng, idx


class DmaTok:
    __slots__ = ("sem", "val")

    def __init__(self, sem, val):
        self.sem, self.val = sem, val


def flat(deps):
    for d in deps:
        if d is None:
            continue
        if isinstance(d, (list, tuple)):
            yield from flat(d)
        else:
            yield d


class Queues:

    def __init__(self):
        self.q = {e: [] for e in ("pe", "act", "dve", "pool", "sp")}
        self.pending = {e: [] for e in self.q}

    def op(self, eng, fn, *deps):
        d = list(flat(deps)) + self.pending[eng]
        self.pending[eng] = []
        self.q[eng].append((d, fn))
        return Tok(eng, len(self.q[eng]) - 1)

    def pe(self, fn, *deps):
        return self.op("pe", fn, *deps)

    def act(self, fn, *deps):
        return self.op("act", fn, *deps)

    def dve(self, fn, *deps):
        return self.op("dve", fn, *deps)

    def pool(self, fn, *deps):
        return self.op("pool", fn, *deps)

    def fence(self):
        last = [Tok(e, len(self.q[e]) - 1) for e in ("pe", "act", "dve", "pool") if self.q[e]]
        for e in ("pe", "act", "dve", "pool"):
            self.pending[e] = [t for t in last]
        return last


class Ring:

    def __init__(self, bufs):
        self.free = [(b, []) for b in bufs]

    def take(self):
        assert self.free, "no buffer has been given back"
        return self.free.pop(0)

    def give(self, buf, *toks):
        self.free.append((buf, list(flat(toks))))

    def lend(self, bufs):
        self.free += [(b, list(flat([d]))) for b, d in bufs]

    def back(self, bufs):
        assert all(any(b is f for f, _ in self.free) for b, _ in bufs)
        self.free = [(f, d) for f, d in self.free if not any(f is b for b, _ in bufs)]


def gpipe(gens, lag=1):
    live, gens, n = [], list(gens), 0
    while gens or live:
        for g in list(live):
            try:
                next(g)
            except StopIteration:
                live.remove(g)
        if gens and (n % lag == 0 or not live):
            g = gens.pop(0)
            try:
                next(g)
                live.append(g)
            except StopIteration:
                pass
        n += 1
        yield


def par(*gens):
    out, live = [None] * len(gens), list(enumerate(gens))
    while live:
        for n, g in list(live):
            try:
                next(g)
            except StopIteration as e:
                out[n] = e.value
                live.remove((n, g))
        if live:
            yield
    return out


def flow(make, items, slots, stagger):
    items, free, live, since = list(items), list(slots), [], stagger
    while items or live:
        for g, s in list(live):
            try:
                next(g)
            except StopIteration:
                live.remove((g, s))
                free.append(s)
        since += 1
        if items and free and (since >= stagger or not live):
            s = free.pop(0)
            live.append((make(items.pop(0), s), s))
            since = 0


def get(ring):
    n = 0
    while not ring.free:
        n += 1
        assert n < 1000, "the ring is held for good"
        yield
    return ring.take()


def build(nc, wa, wb, wc, wd, wm, wi, ve, co, step, xin, out):
    ctx = ExitStack()
    with ctx:
        def sb(name, shape, dt=F32):
            return ctx.enter_context(nc.sbuf_tensor(name, shape, dt))

        XA = sb("XA", [128, 32, 128])
        AR = sb("AR", [128, 24576])
        wAB = sb("wAB", [128, 8192])
        wCs = sb("wCs", [128, NC])
        vecs = sb("vecs", [128, NV])
        cons = sb("cons", [128, NCO])
        identb = sb("identb", [128, 128], BF16)
        cmaskb = sb("cmaskb", [128, 128], BF16)
        MISC = sb("MISC", [128, 512])
        R8 = sb("R8", [128, 2, 2048])
        R2 = sb("R2", [128, NS2, 512])
        RS = sb("RS", [128, 12, 64])
        psum = [ctx.enter_context(nc.psum_tensor(f"ps{i}", [128, 512], F32)) for i in range(8)]

        P = Queues()
        PS = Ring(psum)
        S8 = Ring([R8[:, i, :] for i in range(2)])
        S2 = Ring([R2[:, i, :] for i in range(NS2)])
        SS = Ring([RS[:, i, :] for i in range(12)])
        sems = []

        def dma(dst, src, *deps):
            s = ctx.enter_context(nc.semaphore(f"s_dma{len(sems)}"))
            sems.append(s)
            P.op("sp", lambda e: (e.dma_start(dst, src).then_inc(s, 16), None)[1], *deps)
            return DmaTok(s, 16)

        def wv(name):
            for tab, t, base in ((WA, wAB, 0), (WM, wAB, 4096), (WC, wCs, 0), (VE, vecs, 0), (CO, cons, 0)):
                if name in tab:
                    o, n = tab[name]
                    return t[:, base + o:base + o + n]
            raise KeyError(name)

        ident = wv("ident")
        SLOT = 8192
        XG = [XA[:, 4 * g:4 * g + 4, :] for g in range(8)]

        d_co = dma(cons[:, :], co)
        xrows = xin.rearrange("b (t p) d -> p (b t) d", p=128)
        d_x = [dma(XA[:, 4 * i:4 * i + 4, :], xrows[:, 4 * i:4 * i + 4, :]) for i in range(2)]
        d_wa0 = dma(wAB[:, 0:320], wa[:, 0:320])
        STEPM = AR[:, 6400:6784]
        d_st = dma(STEPM, step)
        d_ve = dma(vecs[:, :], ve)
        wi_s = AR[:, SLOT + 6400:SLOT + 6400 + NI].bitcast(I32)
        d_wi = dma(wi_s, wi)
        d_x += [dma(XA[:, 4 * i:4 * i + 4, :], xrows[:, 4 * i:4 * i + 4, :]) for i in range(2, 8)]
        d_wa = dma(wAB[:, 320:NA], wa[:, 320:NA])
        d_wc = dma(wCs[:, :], wc)
        t_cb = P.act(lambda e: e.copy(identb[:, :], ident), d_co)
        t_cb = [t_cb, P.act(lambda e: e.copy(cmaskb[:, :], wv("cmask")), d_co)]
        mhalf = MISC[:, 0:4]
        t_mh = P.dve(lambda e: e.memset(mhalf, -0.5))

        load = {"act": 0.0, "dve": 0.0}

        def size(ap):
            n = 1
            for d in ap.shape[1:]:
                n *= d
            return n

        def mm(out, lhsT, rhs, start, stop, *deps):
            return P.pe(lambda e: e.matmul(out, lhsT, rhs, start=start, stop=stop), *deps)

        def tr(out, in_, *deps):
            k = in_.shape[0]
            return P.pe(lambda e: e.transpose(out, in_, ident[0:k, 0:k]), d_co, *deps)

        def cp(eng, out, in_, *deps):
            load[eng] += (0.19 + size(out) / 1200) if eng == "act" else (0.12 + size(out) / 960)
            if eng == "act":
                return P.act(lambda e: e.copy(out, in_), *deps)
            return P.dve(lambda e: e.tensor_copy(out, in_), *deps)

        def evac(out, in_, *deps):
            return cp("act" if load["act"] < load["dve"] else "dve", out, in_, *deps)

        def act(out, in_, f, *deps, bias=None, scale=None, acc=None):
            load["act"] += 0.2 + size(out) / 1200 + (0.09 if acc is not None else 0)
            kw = {}
            if bias is not None:
                kw["bias"] = bias
            if scale is not None:
                kw["scale"] = scale
            if acc is not None:
                kw["accum_out"] = acc
            return P.act(lambda e: e.activation(out, in_, f, **kw), *deps)

        def tt(out, a, b, op, *deps):
            load["dve"] += 0.08 + size(out) / 960
            return P.dve(lambda e: e.tensor_tensor(out, a, b, op), *deps)

        def ts(out, a, s1, s2, op0, op1, *deps):
            load["dve"] += 0.08 + size(out) / 1500
            if op1 is None:
                return P.dve(lambda e: e.tensor_scalar(out, a, s1, None, op0), *deps)
            return P.dve(lambda e: e.tensor_scalar(out, a, s1, s2, op0, op1), *deps)

        def stt(out, a, s, b, op0, op1, *deps):
            load["dve"] += 0.08 + size(out) / 960
            return P.dve(lambda e: e.scalar_tensor_tensor(out, a, s, b, op0, op1), *deps)

        def red(out, a, op, *deps, negate=False):
            load["dve"] += 0.08 + size(a) / 960
            return P.dve(lambda e: e.tensor_reduce(out, a, X_AX, op, negate=negate), *deps)

        def rcp(out, a, *deps):
            load["dve"] += 0.08 + size(out) / 960
            return P.dve(lambda e: e.reciprocal(out, a), *deps)

        def v4(ps):
            return ps[:, :].rearrange("p (t c) -> p t c", c=128)

        def rep4(v):
            return v.unsqueeze(1).to_broadcast([128, 4, 128])

        def norm(src, dst, deps, rms=False, eps=1e-5):
            buf, w = yield from get(SS)
            st = [P.dve(lambda e, i=i: e.bn_stats(buf[:, 6 * i:6 * i + 6], src[:, i, :]), w, deps) for i in range(4)]
            ag = [P.dve(lambda e, i=i: e.bn_aggr(buf[:, 24 + 2 * i:26 + 2 * i], buf[:, 6 * i:6 * i + 6]), st[i])
                  for i in range(4)]
            load["dve"] += 1.2
            mv = buf[:, 24:32].rearrange("p (i c) -> p i c", c=2)
            if rms:
                a = tt(buf[:, 32:36], mv[:, :, 0], mv[:, :, 0], ALU.mult, ag)
                b = stt(buf[:, 36:40], buf[:, 32:36], eps, mv[:, :, 1], ALU.add, ALU.add, a, ag)
            else:
                b = ts(buf[:, 36:40], mv[:, :, 1], eps, None, ALU.add, None, ag)
            r = P.pool(lambda e: e.tensor_tensor(buf[:, 40:44], buf[:, 36:40], mhalf, ALU.pow), b, t_mh)
            yield
            last = []
            for i in range(4):
                rs = buf[:, 40 + i:41 + i]
                if rms:
                    last.append(ts(dst[:, i, :], src[:, i, :], rs, None, ALU.mult, None, r, st))
                else:
                    last.append(ts(dst[:, i, :], src[:, i, :], buf[:, 24 + 2 * i:25 + 2 * i], rs, ALU.subtract,
                                   ALU.mult, r, ag[i], st))
            SS.give(buf, last)
            return last

        def to_T(src, dstT, deps, g_=None, b_=None):
            ps, w = yield from get(PS)
            for i in range(4):
                k = tr(ps[:, i * 128:(i + 1) * 128], src[:, i, :], w, deps)
            if g_ is None:
                v = evac(dstT, ps[:, :], k)
            else:
                v = ts(dstT, ps[:, :], g_, b_, ALU.mult, ALU.add, k, d_ve)
            PS.give(ps, v)
            return v

        def proj_T(dst, w_, srcT, deps, scale=None):
            m = w_.shape[1]
            ps, w = yield from get(PS)
            k = mm(ps[0:m, :], w_, srcT, True, True, w, deps)
            v = evac(dst, ps[0:m, :], k) if scale is None else ts(dst, ps[0:m, :], scale, None, ALU.mult, None, k)
            PS.give(ps, v)
            return v

        def proj_tok(w_, srcT, deps, fin):
            ps, w = yield from get(PS)
            for i in range(4):
                k = mm(ps[:, i * 128:(i + 1) * 128], srcT[:, i * 128:(i + 1) * 128], w_, True, True, w, deps)
            v = fin(ps, k)
            PS.give(ps, v)
            return v

        def to(dst):
            return lambda ps, k: evac(dst, v4(ps), k)

        def add_rep(dst, rep):
            def fin(ps, k):
                a = tt(dst, dst, v4(ps), ALU.add, k)
                return tt(dst, dst, rep4(rep), ALU.add, a, d_ve, d_wa)
            return fin

        def add_scaled(dst, rep):
            def fin(ps, k):
                tmp, w = S2.take()
                a = tt(v4(tmp), v4(ps), rep4(rep), ALU.mult, k, w, d_ve)
                b = tt(dst, dst, v4(tmp), ALU.add, a)
                S2.give(tmp, b)
                return [a, b]
            return fin

        def pre(X, XN, XT, deps):
            n = yield from norm(X, XN, deps)
            return (yield from to_T(XN, XT, n))

        def post(X, Y, deps):
            n = yield from norm(Y, Y, deps)
            return tt(X, X, Y, ALU.add, n)

        def mlp(xT, deps, w1, b1, nh, kind, w2, fin, wdep, w1b=None):
            h, hw = yield from get(S8)
            h3 = h.rearrange("p (j n) -> p j n", n=512)
            hk = []
            for j in range(nh):
                ps, w = yield from get(PS)
                k = mm(ps[:, :], w1[:, j * 128:(j + 1) * 128], xT, True, True, w, wdep, deps)
                if kind == "silu":
                    a = act(h3[:, j, :], ps[:, :], ACT.Silu, hw, k)
                    PS.give(ps, a)
                    p2, w_2 = yield from get(PS)
                    k2 = mm(p2[:, :], w1b[:, j * 128:(j + 1) * 128], xT, True, True, w_2, wdep)
                    v = tt(h3[:, j, :], h3[:, j, :], p2[:, :], ALU.mult, a, k2)
                    PS.give(p2, v)
                elif kind == "relu2":
                    a = act(h3[:, j, :], ps[:, :], ACT.Relu, hw, k)
                    PS.give(ps, a)
                    v = P.pool(lambda e, x=h3[:, j, :]: e.tensor_tensor(x, x, x, ALU.mult), a)
                else:
                    v = act(h3[:, j, :], ps[:, :], kind, hw, k, d_ve, bias=None if b1 is None else b1[:, j:j + 1])
                    PS.give(ps, v)
                hk.append(v)
                yield
            ps, w = yield from get(PS)
            for i in range(4):
                for j in range(nh):
                    k = mm(ps[:, i * 128:(i + 1) * 128], h3[:, j, i * 128:(i + 1) * 128], w2[:, j, :],
                           j == 0, j == nh - 1, w, hk)
            S8.give(h, k)
            v = fin(ps, k)
            PS.give(ps, v)
            yield
            return v

        def attn_item(q, kT, v0, v1, po0, po1, deps, kdeps, done):
            ps, w = yield from get(PS)
            p_, pw = yield from get(S2)
            st, sw = yield from get(SS)
            mm(ps[:, 0:128], q[:, 0:128], kT[:, 0:128], True, False, w, deps, kdeps)
            mm(ps[:, 0:128], identb[:, :], cmaskb[:, :], False, True, t_cb)
            mm(ps[:, 128:384], q[:, 128:256], kT[:, 0:256], True, False)
            k = mm(ps[:, 256:384], identb[:, :], cmaskb[:, :], False, True)
            m0 = red(st[:, 0:1], ps[:, 0:128], ALU.max, k, sw, negate=True)
            m1 = red(st[:, 1:2], ps[:, 128:384], ALU.max, k, sw, negate=True)
            x0 = act(p_[:, 0:128], ps[:, 0:128], ACT.Exp, m0, m1, pw, bias=st[:, 0:1])
            x1 = act(p_[:, 128:384], ps[:, 128:384], ACT.Exp, m1, bias=st[:, 1:2])
            PS.give(ps, x1)
            SS.give(st, x1)
            yield k
            pt, w = yield from get(PS)
            pT, pw = yield from get(S2)
            for j in range(3):
                k = tr(pt[:, j * 128:(j + 1) * 128], p_[:, j * 128:(j + 1) * 128], w, x0, x1)
            S2.give(p_, k)
            v = evac(pT[:, 0:384], pt[:, 0:384], k, pw)
            PS.give(pt, v)
            yield
            mm(po0, pT[:, 0:128], v0, True, True, v, deps, kdeps)
            mm(po1, pT[:, 128:256], v0, True, False)
            k = mm(po1, pT[:, 256:384], v1, False, True)
            S2.give(pT, k)
            done.append(k)

        def attn(QT, KT, V, nh, hd, hm, O4, deps):
            out = []
            c = hd + 1
            for b in range(2):
                po, pow_ = yield from get(PS)
                done, qm = [], {}

                def mask(h, b=b, qm=qm):
                    q, qw = yield from get(S2)
                    a = P.pool(lambda e: e.tensor_scalar(q[:, 0:256], QT[:, b * 256:(b + 1) * 256], hm[:, h:h + 1],
                                                         None, ALU.mult), deps, qw, d_co)
                    qm[h] = (q, a)

                def item(h, b=b, po=po, pow_=pow_, done=done, qm=qm, mask=mask):
                    if h not in qm:
                        yield from mask(h)
                    if h + 1 < nh and S2.free:
                        yield from mask(h + 1)
                    q, a = qm[h]
                    t0 = 2 * b
                    it = attn_item(q[:, 0:256], KT[:, t0 * 128:(t0 + 2) * 128], V(t0, h), V(t0 + 1, h),
                                   po[:, h * c:(h + 1) * c], po[:, (nh + h) * c:(nh + h + 1) * c],
                                   [a, pow_], deps, done)
                    while True:
                        k = next(it)
                        yield
                        if k is not None:
                            S2.give(q, k)
                            break
                    yield from it

                yield from gpipe(item(h) for h in range(nh))
                r, rw = yield from get(SS)
                p4 = po[:, 0:2 * nh * c].rearrange("p (t h d) -> p t h d", t=2, d=c)
                r3 = r[:, 0:2 * nh].rearrange("p (t h) -> p t h", t=2)
                k = rcp(r3, p4[:, :, :, hd], done, rw)
                for t in range(2):
                    a = tt(O4[:, 2 * b + t, 0:nh * hd].rearrange("p (h d) -> p h d", d=hd), p4[:, t, :, 0:hd],
                           r3[:, t, :].unsqueeze(2).to_broadcast([128, nh, hd]), ALU.mult, k, done)
                    out.append(a)
                PS.give(po, a)
                SS.give(r, a)
            return out

        WV = AR[:, 6784:6912]
        ps, w = PS.take()
        k = mm(ps[:, 0:128], wv("wvd")[0:32, :], wv("wvu")[0:32, :], True, True, w, d_wa0)
        dwv = evac(WV, ps[:, 0:128], k)
        PS.give(ps, dwv)
        wgu = AR[:, 2 * SLOT + 6400:2 * SLOT + 6400 + NI]
        t_wi = ts(wgu, wi_s, float(np.float32(1.0 / 127.0)), None, ALU.mult, None, d_wi)

        def l0_item(b, qt, QT0, KT0, V0, O4, dq, dk, dv, out):
            t = 2 * b + qt
            ps, w = yield from get(PS)
            s_, sw = yield from get(S2)
            st, stw = yield from get(SS)
            k = mm(ps[:, 0:256], QT0[:, t * 128:(t + 1) * 128], KT0[:, b * 256:(b + 1) * 256], True, True, w, dq, dk)
            sc, zz = s_[:, 0:256], s_[:, 256:512]
            o = 128 - 128 * qt
            a = tt(sc, ps[:, 0:256], STEPM[:, o:o + 256], ALU.mult, k, sw, d_st)
            PS.give(ps, a)
            c = ts(zz, sc, 0.0, FMIN, ALU.is_equal, ALU.mult, a)
            d = tt(sc, sc, zz, ALU.add, c)
            m = red(st[:, 0:1], sc, ALU.max, d, stw, negate=True)
            x = act(sc, sc, ACT.Exp, m, bias=st[:, 0:1], acc=st[:, 1:2])
            r = rcp(st[:, 2:3], st[:, 1:2], x)
            yield
            pt, w = yield from get(PS)
            pT, pw = yield from get(S2)
            for j in range(2):
                k = tr(pt[:, j * 128:(j + 1) * 128], sc[:, j * 128:(j + 1) * 128], w, x)
            S2.give(s_, k)
            v = evac(pT[:, 0:256], pt[:, 0:256], k, pw)
            PS.give(pt, v)
            yield
            po, w = yield from get(PS)
            for j in range(2):
                k = mm(po[:, 0:128], pT[:, j * 128:(j + 1) * 128], V0[:, 2 * b + j, :], j == 0, j == 1, w, v, dv)
            S2.give(pT, k)
            y = ts(O4[:, t, :], po[:, 0:128], st[:, 2:3], None, ALU.mult, None, k, r)
            PS.give(po, y)
            SS.give(st, y)
            out.append(y)

        def linear_attn(VQ, QG, CTX, CN, CR, GS, EK, O4, dv):
            q4 = VQ[:, :, 136:200].rearrange("p t (h d) -> p t h d", d=16)
            kk = VQ[:, :, 200:264]
            gs = GS.rearrange("p (t h) -> p t h", t=4)
            gb = gs.unsqueeze(3).to_broadcast([128, 4, 4, 16])
            a = red(gs, q4, ALU.max, dv)
            a = tt(q4, q4, gb, ALU.subtract, a)
            a = act(VQ[:, :, 136:200], VQ[:, :, 136:200], ACT.Exp, a)
            c = ts(EK, kk, 0.0, None, ALU.min, None, dv)
            c = act(EK, EK, ACT.Exp, c)
            yield
            a = red(gs, q4, ALU.add, a)
            a = rcp(gs, gs, a)
            a = tt(q4, q4, gb, ALU.mult, a)
            c = stt(kk, kk, 0.0, EK, ALU.max, ALU.add, c)
            yield
            ps, w = yield from get(PS)
            for j in range(4):
                k = tr(ps[0:64, j * 128:(j + 1) * 128], VQ[:, j, 136:200], w, a)
            dqg = evac(QG, ps[0:64, :], k)
            PS.give(ps, dqg)
            dctx = []
            for us in ((0, 2), (1,)):
                ps, w = yield from get(PS)
                nu = len(us)
                for bb in range(2):
                    for n, u in enumerate(us):
                        t, r, c_ = 2 * bb + u // 2, 64 * (u % 2), (nu * bb + n) * 65
                        k = mm(ps[0:64, c_:c_ + 65], VQ[r:r + 64, t, 200:264], VQ[r:r + 64, t, 68:133],
                               True, True, w, c)
                v = evac(CTX[:, :, us[0]:3:2, :],
                         ps[0:64, 0:130 * nu].rearrange("p (b u c) -> p b u c", b=2, c=65), k)
                PS.give(ps, v)
                dctx.append(v)
            yield
            c = dctx
            for u in (1, 2):
                c = tt(CTX[:, :, u, :], CTX[:, :, u, :], CTX[:, :, u - 1, :], ALU.add, c)
            c = ts(CR, CTX[:, :, :, 64], 1e-6, None, ALU.add, None, c)
            c = rcp(CR, CR, c)
            a = tt(CN, CTX[:, :, :, 0:64], CR.unsqueeze(3).to_broadcast([64, 2, 3, 64]), ALU.mult, c)
            CNf = CN.rearrange("p b u c -> p (b u) c")
            a = tt(CNf, CNf, wv("bm16")[0:64, :].unsqueeze(1).to_broadcast([64, 6, 64]), ALU.mult, a, d_co)
            yield
            ps, w = yield from get(PS)
            for bb in range(2):
                for u in range(1, 4):
                    j, r = 2 * bb + u // 2, 64 * (u % 2)
                    k = mm(ps[r:r + 64, j * 64:(j + 1) * 64],
                           QG[:, bb * 256 + u * 64:bb * 256 + (u + 1) * 64], CN[:, bb, u - 1, :], True, True,
                           w, a, dqg)
            p3 = ps[:, 0:256].rearrange("p (t c) -> p t c", c=64)
            o3 = O4[:, :, 64:128]
            pz = P.dve(lambda e: e.memset(o3[0:64, 0:4:2, :], 0.0))
            v1 = cp("act", o3[64:128, 0:4:2, :], p3[64:128, 0:4:2, :], k)
            v2 = cp("act", o3[:, 1:4:2, :], p3[:, 1:4:2, :], k)
            PS.give(ps, v2)
            return [pz, v1, v2]

        def group01(g, base):
            S = AR[:, base * SLOT:(base + 1) * SLOT]
            X = XG[g]

            def t3(o):
                return S[:, o:o + 512].rearrange("p (t c) -> p t c", c=128)

            XN, O4, Z, V0 = t3(0), t3(512), t3(1024), t3(1536)
            XT, QT, KT = S[:, 2048:2560], S[:, 2560:3072], S[:, 3072:3584]
            VQ = S[:, 3584:3584 + 4 * 264].rearrange("p (t c) -> p t c", c=264)
            QG = S[0:64, 4640:5152]
            CTX = S[0:64, 5152:5152 + 390].rearrange("p (b u c) -> p b u c", b=2, c=65)
            CN = S[0:64, 5542:5542 + 384].rearrange("p (b u c) -> p b u c", b=2, c=64)
            CR = S[0:64, 5926:5932].rearrange("p (b u) -> p b u", b=2)
            GS = S[:, 5936:5952]
            EK = S[:, 5952:6208].rearrange("p (t c) -> p t c", c=64)
            xT = yield from pre(X, XN, XT, d_x[g])
            yield
            dq = yield from proj_T(QT[0:32, :], wv("wq0"), XT, [xT, d_wa0], scale=float(32.0 ** -0.5))
            dk = yield from proj_T(KT[0:32, :], wv("wk0"), XT, [xT, d_wa0])
            dv = yield from proj_tok(WV, XT, [xT, dwv], to(V0))
            yield
            y = []
            yield from gpipe(l0_item(b, qt, QT[0:32, :], KT[0:32, :], V0, O4, dq, dk, dv, y)
                             for b in range(2) for qt in range(2))
            dx = yield from post(X, O4, y)
            yield
            xT = yield from pre(X, XN, XT, dx)
            yield
            y = yield from mlp(XT, xT, wgu[:, 0:384], None, 3, "silu",
                               wgu[:, 768:1152].rearrange("p (j c) -> p j c", c=128), to(O4), t_wi,
                               w1b=wgu[:, 384:768])
            dx = yield from post(X, O4, y)
            yield
            t1 = P.dve(lambda e: e.memset(VQ[:, :, 0:68].rearrange("p t (h d) -> p t h d", d=17)[:, :, :, 16:17], 1.0))
            t1 = [t1, P.dve(lambda e: e.memset(VQ[:, :, 132:133], 1.0))]
            dz = yield from norm(X, Z, dx)
            for i in range(4):
                def col(n):
                    return wv(n)[:, i:i + 1]
                n = yield from norm(Z, XN, dz)
                hT = yield from to_T(XN, XT, n, col("ln1g"), col("ln1b"))
                yield
                dq = yield from proj_T(QT, wv(f"l1q{i}"), XT, [hT, d_wa], scale=0.25)
                dk = yield from proj_T(KT, wv(f"l1k{i}"), XT, [hT, d_wa])
                dv = [t1]
                for g2 in range(2):
                    ps, w = yield from get(PS)
                    for j in range(2):
                        t = 2 * g2 + j
                        k = mm(ps[:, j * 256:(j + 1) * 256], XT[:, t * 128:(t + 1) * 128], wv(f"l1vqk{i}"),
                               True, True, w, hT, d_wa)
                    p2 = ps[:, :].rearrange("p (t c) -> p t c", c=256)
                    vq = VQ[:, 2 * g2:2 * g2 + 2, :]
                    a = cp("act", vq[:, :, 0:68].rearrange("p t (h d) -> p t h d", d=17)[:, :, :, 0:16],
                           p2[:, :, 0:64].rearrange("p t (h d) -> p t h d", d=16), k)
                    b_ = cp("act", vq[:, :, 68:132], p2[:, :, 64:128], k)
                    c = cp("act", vq[:, :, 136:264], p2[:, :, 128:256], k)
                    PS.give(ps, c)
                    dv += [a, b_, c]
                yield
                ka, kl = yield from par(
                    attn(QT, KT, lambda t, h: VQ[:, t, 17 * h:17 * h + 17], 4, 16, wv("hm16"), O4, [dq, dk, dv]),
                    linear_attn(VQ, QG, CTX, CN, CR, GS, EK, O4, dv))
                yield
                oT = yield from to_T(O4, XT, [ka, kl])
                dz = yield from proj_tok(wv(f"l1o{i}"), XT, [oT, d_wa],
                                         add_rep(Z, wv("bo")[:, i * 128:(i + 1) * 128]))
                yield
                n = yield from norm(Z, XN, dz)
                hT = yield from to_T(XN, XT, n, col("ln2g"), col("ln2b"))
                yield
                dz = yield from mlp(XT, hT, wv(f"l1w1{i}"), wv("b1")[:, 4 * i:4 * i + 4], 4, ACT.Gelu,
                                    wv(f"l1w2{i}").rearrange("p (j c) -> p j c", c=128),
                                    add_rep(Z, wv("b2")[:, i * 128:(i + 1) * 128]), d_wa)
            dxg[g] = yield from post(X, Z, dz)

        dxg = [None] * 8
        lent = [(AR[:, 6912:7424], []), (AR[:, 7424:7936], []), (AR[:, 15744:16256], []),
                (AR[:, 14592:15104], t_wi), (AR[:, 15104:15616], t_wi), (AR[:, 23936:24448], [])]
        S2.lend(lent)
        flow(group01, range(8), range(3), STAG0)
        S2.back(lent)
        last = P.fence()

        phi = wAB[:, 0:2048]
        d_phi = dma(phi, wb[:, 0:2048], last)
        d_wm = dma(wAB[:, 4096:4096 + NM], wm, last)
        XTA = AR[:, 0:4096]
        ZX = AR[:, 20480:24576].rearrange("p (t c) -> p t c", c=128)
        LR = Ring([AR[:, 4096 + 2048 * i:6144 + 2048 * i] for i in range(3)])
        DR = Ring([AR[:, 10240 + 2048 * i:12288 + 2048 * i] for i in range(2)])
        YA = AR[:, 14336:18432].rearrange("p (b m e) -> p b m e", b=16, m=2)
        SL = AR[:, 18432:20480].rearrange("p (b s) -> p b s", b=16)
        WR = Ring([wAB[:, 2048 + 512 * i:2560 + 512 * i] for i in range(4)])
        XN4 = ZX[:, :, :].rearrange("p (b m) d -> p b m d", m=2)
        xTh = [None] * 8

        def smoe_in(g, _):
            xTh[g] = yield from pre(XG[g], ZX[:, 4 * g:4 * g + 4, :], XTA[:, 512 * g:512 * g + 512], dxg[g])

        flow(smoe_in, range(8), range(4), 1)
        MR = MISC[:, 64:96].rearrange("p (m b) -> p m b", m=2)
        LS = MISC[:, 96:128].rearrange("p (m b) -> p m b", m=2)
        smoe = {"acc": None, "stat": [None, None]}

        def wload(q):
            b_, w = WR.take()
            return b_, dma(b_, wb[:, 2048 + 512 * q:2560 + 512 * q], w, last)

        wch = {q: wload(q) for q in range(3)}

        def unit(q, mt):
            L, lw = LR.take()
            L3 = L.rearrange("p (b s) -> p b s", b=16)
            ev = []
            for g in range(4):
                ps, w = PS.take()
                for i in range(4):
                    t = 2 * (4 * g + i) + mt
                    k = mm(ps[:, i * 128:(i + 1) * 128], XTA[:, t * 128:(t + 1) * 128],
                           phi[:, q * 128:(q + 1) * 128], True, True, w, xTh[t // 4], d_phi)
                v = evac(L3[:, 4 * g:4 * g + 4, :], v4(ps), k, lw)
                PS.give(ps, v)
                ev.append(v)
            D, dw = DR.take()
            D3 = D.rearrange("p (b s) -> p b s", b=16)
            Ds = D.rearrange("p (b s) -> p s b", b=16)
            tmp, tw = S2.take()
            m1 = tmp[:, 0:128]
            mb = m1.unsqueeze(1).to_broadcast([128, 16, 128])
            a = red(m1, L.rearrange("p (b s) -> p s b", b=16), ALU.max, ev, tw)
            a0 = tt(D3, L3, mb, ALU.subtract, a, dw)
            x = P.act(lambda e: e.activation(D, D, ACT.Exp), a0)
            st, sw = SS.take()
            tm, al, rs, nm = st[:, 0:16], st[:, 16:32], st[:, 32:48], st[:, 48:64]
            mr, ls = MR[:, mt, :], LS[:, mt, :]
            pst = smoe["stat"][mt]
            b1 = P.dve(lambda e: e.tensor_reduce(tm, L3, X_AX, ALU.max), ev, sw)
            if q == 0:
                b2 = P.dve(lambda e: e.tensor_copy(mr, tm), b1)
                ax = None
            else:
                b2 = tt(tm, tm, mr, ALU.max, b1, pst)
                b3 = tt(al, mr, tm, ALU.subtract, b2)
                ax = P.act(lambda e: e.activation(al, al, ACT.Exp), b3)
                b2 = P.dve(lambda e: e.tensor_copy(mr, tm), b3)
            b4 = ts(nm, mr, -1.0, None, ALU.mult, None, b2)
            ex = None
            for b in range(16):
                ex = P.act(lambda e, b=b: e.activation(L3[:, b, :], L3[:, b, :], ACT.Exp, bias=nm[:, b:b + 1],
                                                       accum_out=rs[:, b:b + 1]), b4, a0)
            if q == 0:
                c = P.dve(lambda e: e.tensor_copy(ls, rs), ex)
            else:
                c = tt(ls, ls, al, ALU.mult, ax, pst)
                c = tt(ls, ls, rs, ALU.add, c, ex)
            smoe["stat"][mt] = [c, b2]
            a = P.dve(lambda e: e.tensor_reduce(m1, Ds, X_AX, ALU.add), x)
            a = P.dve(lambda e: e.reciprocal(m1, m1), a)
            a = tt(D3, D3, mb, ALU.mult, a)
            S2.give(tmp, a)
            yield
            if mt == 0:
                smoe["acc"] = [PS.take() for _ in range(4)]
            acc = smoe["acc"]
            for b in range(16):
                k = P.pe(lambda e, b=b: e.matmul(acc[b // 4][0][:, (b % 4) * 128:(b % 4 + 1) * 128],
                                                 XN4[:, b, mt, :], D3[:, b, :], start=(mt == 0 and b % 4 == 0),
                                                 stop=(mt == 1), skip_group_check=True), acc[b // 4][1], a)
            DR.give(D, k)
            smoe[("E", q, mt)] = (L, L3, st, al, [ex, ax], c)
            if mt == 0:
                return
            sl = []
            for g in range(4):
                v = evac(SL[:, 4 * g:4 * g + 4, :], v4(acc[g][0]), k, smoe.get("slread"))
                PS.give(acc[g][0], v)
                sl.append(v)
            yield
            yt, yw = S8.take()
            yt3 = yt.rearrange("p (b s) -> p b s", b=16)
            W, dW = wch[q]
            kk = []
            for i in range(4):
                ps, w = PS.take()
                k = mm(ps[:, :].rearrange("p (b s) -> p b s", b=16), W[:, i * 128:(i + 1) * 128],
                       SL[:, :, i * 32:(i + 1) * 32], True, True, w, sl, dW)
                bb = wv("mb")[:, 4 * q + i:4 * q + i + 1]
                v = ts(yt3[:, :, i * 32:(i + 1) * 32], ps[:, :].rearrange("p (b s) -> p b s", b=16), bb, None,
                       ALU.add, None, k, yw, d_ve)
                PS.give(ps, v)
                kk.append(v)
            smoe["slread"] = k
            WR.give(W, k)
            if q + 3 < 16:
                wch[q + 3] = wload(q + 3)
            ym, mw = S8.take()
            ym3 = ym.rearrange("p (b e) -> p b e", b=16)
            ky = []
            for g in range(4):
                pt, w = PS.take()
                for i in range(4):
                    b = 4 * g + i
                    k = tr(pt[:, i * 128:(i + 1) * 128], yt3[:, b, :], w, kk)
                v = evac(ym3[:, 4 * g:4 * g + 4, :], v4(pt), k, mw)
                PS.give(pt, v)
                ky.append(v)
            S8.give(yt, k)
            for m_ in range(2):
                L_, E3, st_, al_, kx, kc = smoe.pop(("E", q, m_))
                for g in range(4):
                    pt, w = PS.take()
                    for i in range(4):
                        k = tr(pt[:, i * 128:(i + 1) * 128], E3[:, 4 * g + i, :], w, kx)
                    eT, ew = S2.take()
                    v = evac(eT, pt[:, :], k, ew)
                    PS.give(pt, v)
                    if g == 3:
                        LR.give(L_, k)
                    po, w = PS.take()
                    for i in range(4):
                        b = 4 * g + i
                        k = mm(po[:, i * 128:(i + 1) * 128], eT[:, i * 128:(i + 1) * 128], ym3[:, b, :], True, True,
                               w, v, ky[g])
                    S2.give(eT, k)
                    for i in range(4):
                        b = 4 * g + i
                        pi = po[:, i * 128:(i + 1) * 128]
                        if q == 0:
                            v = P.dve(lambda e, b=b, pi=pi, m_=m_: e.tensor_copy(YA[:, b, m_, :], pi), k)
                        else:
                            v = P.dve(lambda e, b=b, pi=pi, m_=m_, al_=al_: e.scalar_tensor_tensor(
                                YA[:, b, m_, :], YA[:, b, m_, :], al_[:, b:b + 1], pi, ALU.mult, ALU.add),
                                k, kx, smoe.get(("ya", b, m_)))
                        smoe[("ya", b, m_)] = v
                    PS.give(po, [smoe[("ya", 4 * g + i, m_)] for i in range(4)])
                SS.give(st_, v, kc)
            S8.give(ym, k)

        for _ in gpipe(unit(q, mt) for q in range(16) for mt in range(2)):
            pass
        rl = rcp(LS, LS, smoe["stat"])
        P.fence()

        def smoe_out(g, _):
            k = [ts(YA[:, t // 2, t % 2, :], YA[:, t // 2, t % 2, :], LS[:, t % 2, t // 2:t // 2 + 1], None,
                    ALU.mult, None, rl) for t in range(4 * g, 4 * g + 4)]
            yield
            dxg[g] = yield from post(XG[g], YA.rearrange("p b m e -> p (b m) e")[:, 4 * g:4 * g + 4, :], k)

        flow(smoe_out, range(8), range(4), 1)
        P.fence()

        EPS = float(np.finfo(np.float32).eps)
        DTv, Av = MISC[:, 200:216], MISC[:, 216:232]
        DOUT, DREV = MISC[:, 232:248], MISC[:, 248:264]
        W2_, W3_, W4_, W5_ = (MISC[:, 264 + 16 * i:280 + 16 * i] for i in range(4))
        W1_ = wv("dt")
        a = ts(W2_, W1_, -1.0, None, ALU.mult, None, d_ve)
        a = tt(W2_, W2_, W1_, ALU.min, a)
        u = P.act(lambda e: e.activation(W2_, W2_, ACT.Exp), a)
        w1p = ts(W3_, W2_, 1.0, None, ALU.add, None, u)
        ln = P.act(lambda e: e.activation(W4_, W3_, ACT.Ln), w1p)
        d1 = ts(W3_, W3_, -1.0, None, ALU.add, None, ln)
        eq = ts(W5_, W3_, 0.0, None, ALU.is_equal, None, d1)
        a = tt(W3_, W3_, W5_, ALU.add, eq)
        a = P.dve(lambda e: e.reciprocal(W3_, W3_), a)
        a = tt(W3_, W3_, W2_, ALU.mult, a)
        a = tt(W4_, W4_, W3_, ALU.mult, a)
        a2 = tt(W5_, W5_, W2_, ALU.mult, a)
        a = tt(W4_, W4_, W5_, ALU.add, a, a2)
        a = P.dve(lambda e: e.scalar_tensor_tensor(DTv, W1_, 0.0, W4_, ALU.max, ALU.add), a)
        ea = P.act(lambda e: e.activation(Av, wv("al"), ACT.Exp), d_ve)
        da = P.dve(lambda e: e.scalar_tensor_tensor(Av, Av, -1.0, DTv, ALU.mult, ALU.mult), ea, a)
        HORD = list(range(0, 16, 2)) + list(range(1, 16, 2))
        LM = wAB[:, 6144:8192].rearrange("p (h q) -> p h q", h=16)
        kl = []
        for n, h in enumerate(HORD):
            k = P.act(lambda e, n=n, h=h: e.activation(LM[:, n, :], wv("dif"), ACT.Exp, scale=Av[:, h:h + 1]),
                      da, d_co)
            kl.append(tt(LM[:, n, :], LM[:, n, :], wv("tri"), ALU.mult, k))
        a = ts(W2_, Av, wv("qp1"), None, ALU.mult, None, da)
        k1 = P.act(lambda e: e.activation(DOUT, W2_, ACT.Exp), a)
        a = ts(W3_, Av, wv("rev"), None, ALU.mult, None, da)
        k2 = P.act(lambda e: e.activation(DREV, W3_, ACT.Exp), a)
        k2 = tt(DREV, DREV, DTv, ALU.mult, k2)
        kpar = [k1, k2] + kl

        def mix(dst, a_, ra, b_, rb, *deps):
            tmp, w = yield from get(S2)
            k1 = tt(v4(tmp), b_, rep4(rb), ALU.mult, w, d_ve, *deps)
            k2 = tt(dst, a_, rep4(ra), ALU.mult, d_ve, *deps)
            k3 = tt(dst, dst, v4(tmp), ALU.add, k1, k2)
            S2.give(tmp, k3)
            return k3

        def bc16(x):
            return x.unsqueeze(2).to_broadcast([128, 16, 16])

        def scan_tile(t, odd, VT, GT, BT, CT, HS, kb, dval, dgat, st_, Z, out):
            sl = slice(odd * 128, odd * 128 + 128)
            gl = slice(t * 128, (t + 1) * 128)
            ps, w = yield from get(PS)
            xv, xw = yield from get(S2)
            for c in range(2):
                k = tr(ps[:, c * 128:(c + 1) * 128], VT[:, c, gl], w, dval)
            vt3 = ps[:, 0:256].rearrange("p (h d) -> p h d", d=16)
            kx1 = tt(xv[:, 0:256].rearrange("p (h d) -> p h d", d=16), vt3, bc16(DTv), ALU.mult, k, xw, kpar)
            kx2 = kx1
            if not odd:
                kx2 = tt(xv[:, 256:512].rearrange("p (h d) -> p h d", d=16), vt3, bc16(DREV), ALU.mult, k, xw, kpar)
            PS.give(ps, kx1, kx2)
            yield
            py, yw = yield from get(PS)
            ys, ysw = yield from get(S2)
            kst = None
            for c in range(4):
                pc, w = yield from get(PS)
                cb, cw_ = yield from get(S2)
                for i in range(4):
                    h = HORD[4 * c + i]
                    r = 64 * (h % 2)
                    k = mm(pc[:, i * 128:(i + 1) * 128], BT[r:r + 64, h // 2, sl], CT[r:r + 64, h // 2, sl],
                           True, True, w, kb)
                v = tt(cb, pc[:, :], LM[:, 4 * c:4 * c + 4, :].rearrange("p h q -> p (h q)"), ALU.mult, k, cw_, kpar)
                PS.give(pc, v)
                yield
                for i in range(4):
                    h = HORD[4 * c + i]
                    kyy = mm(py[:, h * 16:(h + 1) * 16], cb[:, i * 128:(i + 1) * 128],
                             xv[:, h * 16:(h + 1) * 16], True, True, yw, v, kx1)
                S2.give(cb, kyy)
            if odd:
                po, pw = yield from get(PS)
                for jj in range(8):
                    ko = mm(po[:, jj * 32:(jj + 1) * 32], CT[:, jj, sl], HS[:, jj, :], True, True, pw, kb,
                            st_["hk"])
                a = tt(ys[:, 0:256].rearrange("p (h d) -> p h d", d=16),
                       po[:, 0:256].rearrange("p (h d) -> p h d", d=16), bc16(DOUT), ALU.mult, ko, ysw, kpar)
                PS.give(po, a)
                a = tt(ys[:, 0:256], ys[:, 0:256], py[:, 0:256], ALU.add, a, kyy)
                st_["end"] = [ko, kyy]
            else:
                a = evac(ys[:, 0:256], py[:, 0:256], kyy, ysw)
                bt = []
                for c in range(2):
                    ps, w = yield from get(PS)
                    bb, bw = yield from get(S2)
                    for i in range(4):
                        k = tr(ps[:, i * 128:(i + 1) * 128], BT[:, 4 * c + i, sl], w, kb)
                    v = evac(bb, ps[:, :], k, bw)
                    PS.give(ps, v)
                    bt.append((bb, v))
                yield
                ps, w = yield from get(PS)
                for jj in range(8):
                    bb, v = bt[jj // 4]
                    kst = mm(ps[:, jj * 32:(jj + 1) * 32], bb[:, (jj % 4) * 128:(jj % 4 + 1) * 128],
                             xv[:, 256 + jj * 32:256 + (jj + 1) * 32], True, True, w, v, kx2)
                for bb, v in bt:
                    S2.give(bb, kst)
                st_["hk"] = tt(HS, ps[:, 0:256].rearrange("p (j c) -> p j c", j=8),
                               wv("bm64").unsqueeze(1).to_broadcast([128, 8, 32]), ALU.mult, kst, st_["hw"], d_co)
                PS.give(ps, st_["hk"])
            PS.give(py, a)
            S2.give(xv, kyy, kst)
            yield
            ps, w = yield from get(PS)
            yt, ytw = yield from get(S2)
            for c in range(2):
                k = tr(ps[:, c * 128:(c + 1) * 128], ys[:, c * 128:(c + 1) * 128], w, a)
            S2.give(ys, k)
            ks = []
            for c in range(2):
                v = stt(yt[:, c * 128:(c + 1) * 128], VT[:, c, gl], wv("dpar")[:, c:c + 1],
                        ps[:, c * 128:(c + 1) * 128], ALU.mult, ALU.add, k, ytw)
                ks.append(tt(yt[:, c * 128:(c + 1) * 128], yt[:, c * 128:(c + 1) * 128], GT[:, c, gl],
                             ALU.mult, v, dgat))
            PS.give(ps, ks)
            yield
            ps, w = yield from get(PS)
            for c in range(2):
                k = mm(ps[:, 0:128], yt[:, c * 128:(c + 1) * 128], wv("outp")[:, c * 128:(c + 1) * 128],
                       c == 0, c == 1, w, ks)
            S2.give(yt, k)
            tmp, tw = yield from get(S2)
            a = tt(tmp[:, 0:128], ps[:, 0:128], wv("msc"), ALU.mult, k, tw)
            PS.give(ps, a)
            a = tt(Z[:, t, :], Z[:, t, :], tmp[:, 0:128], ALU.add, a)
            S2.give(tmp, a)
            out.append(a)

        def group23(g, base):
            S = AR[:, base * SLOT:(base + 1) * SLOT]
            X = XG[g]

            def t3(o):
                return S[:, o:o + 512].rearrange("p (t c) -> p t c", c=128)

            XN, O4, Z = t3(0), t3(512), t3(1024)
            XT = S[:, 1536:2048]
            NTm = S[:, 512:1024]
            VT = S[:, 2048:3072].rearrange("p (c n) -> p c n", c=2)
            GT = S[:, 3072:4096].rearrange("p (c n) -> p c n", c=2)
            BT = S[:, 4096:6144].rearrange("p (h n) -> p h n", h=8)
            CT = S[:, 6144:8192].rearrange("p (h n) -> p h n", h=8)
            RAW = S[:, 4096:5120].rearrange("p (c n) -> p c n", c=2)
            YN = t3(7680)
            QT, KT = S[:, 4096:4608], S[:, 4608:5120]
            V9 = S[:, 5120:5696].rearrange("p (t h d) -> p t h d", t=4, d=9)
            QK = S[:, 5696:5696 + 640].rearrange("p (t c) -> p t c", c=160)
            QR = S[:, 6336:6848].rearrange("p (t c) -> p t c", c=128)
            KR = S[:, 6848:7360].rearrange("p (t c) -> p t c", c=128)
            xT = yield from pre(X, XN, XT, dxg[g])
            yield
            sc8 = float(np.float32(8.0 ** -0.25))
            t1 = P.dve(lambda e: e.memset(V9[:, :, :, 8:9], 1.0))
            dq = yield from proj_T(QT, wv("l2q"), XT, [xT, d_wc], scale=sc8)
            dk = yield from proj_T(KT, wv("l2k"), XT, [xT, d_wc], scale=sc8)

            def fin_v(ps, k):
                p4 = v4(ps).rearrange("p t (h d) -> p t h d", d=8)
                return [cp("act", V9[:, t, :, 0:8], p4[:, t, :, :], k) for t in range(4)]

            dv = yield from proj_tok(wv("l2v"), XT, [xT, d_wc], fin_v)
            yield
            ka = yield from attn(QT, KT, lambda t, h: V9[:, t, h, :], 16, 8, wv("hm8"), O4, [dq, dk, dv, t1])
            yield
            oT = yield from to_T(O4, XT, ka)
            yield
            y = yield from proj_tok(wv("l2o"), XT, [oT, d_wc], to(O4))
            yield
            dx = yield from post(X, O4, y)
            xT = yield from pre(X, XN, XT, dx)
            yield
            y = yield from mlp(XT, xT, wv("l2w1"), wv("l2b1"), 4, ACT.Gelu,
                               wv("l2w2").rearrange("p (j c) -> p j c", c=128),
                               lambda ps, k: tt(O4, v4(ps), rep4(wv("l2b2")), ALU.add, k, d_ve), d_wc)
            dx = yield from post(X, O4, y)
            yield
            dn = yield from norm(X, XN, dx)
            dz = yield from mix(Z, XN, wv("rm0"), XN, wv("rm1"), dn)
            yield
            dxm = yield from to_T(Z, XT, dz)
            nn = yield from norm(Z, YN, dz, rms=True, eps=EPS)
            dnT = yield from to_T(YN, NTm, nn)
            yield
            dval, dgat = [], []
            for c in range(2):
                dr = yield from proj_T(RAW[:, c, :], wv("inp")[:, c * 128:(c + 1) * 128], NTm, [dnT, d_wc])
                cw = wv("convw")[:, 4 * c:4 * c + 4]
                cb = wv("convb")[:, c:c + 1]
                r0 = RAW[:, c, :].rearrange("p (b n) -> p b n", n=256)
                o0 = VT[:, c, :].rearrange("p (b n) -> p b n", n=256)
                k = ts(VT[:, c, :], RAW[:, c, :], cw[:, 3:4], cb, ALU.mult, ALU.add, dr, d_ve)
                for s in (1, 2, 3):
                    k = stt(o0[:, :, s:256], r0[:, :, 0:256 - s], cw[:, 3 - s:4 - s], o0[:, :, s:256],
                            ALU.mult, ALU.add, k)
                dval.append([k, act(VT[:, c, :], VT[:, c, :], ACT.Silu, k)])
                yield
            for c in range(2):
                ps, w = yield from get(PS)
                k = mm(ps[:, :], wv("inp")[:, 256 + c * 128:256 + (c + 1) * 128], NTm, True, True, w, dnT, d_wc)
                v = act(GT[:, c, :], ps[:, :], ACT.Silu, k)
                PS.give(ps, v)
                dgat.append(v)
            yield
            H2, hw2 = yield from get(S2)
            HS = H2[:, 0:256].rearrange("p (j c) -> p j c", j=8)
            st_ = {"hw": [hw2], "end": None}
            dy = []
            for b in range(2):
                kb = []
                for h in range(0, 8, 2):
                    for dst, nme in ((BT, "bp"), (CT, "cp")):
                        ps, w = yield from get(PS)
                        for i in range(2):
                            k = mm(ps[:, i * 256:(i + 1) * 256], wv(nme)[:, (h + i) * 128:(h + i + 1) * 128],
                                   XT[:, b * 256:(b + 1) * 256], True, True, w, dxm, d_wc)
                        v = evac(dst[:, h:h + 2, :], ps[:, :].rearrange("p (h n) -> p h n", h=2), k,
                                 st_["end"], dval, dnT)
                        PS.give(ps, v)
                        kb.append(v)
                    yield
                yield from gpipe((scan_tile(2 * b + j, j, VT, GT, BT, CT, HS, kb, dval, dgat, st_, Z, dy)
                                  for j in range(2)), lag=7)
                st_["hw"] = [st_["end"]]
            S2.give(H2, st_["end"])
            def relu_mlp(dz, fc, pj, sc):
                nn = yield from norm(Z, YN, dz, rms=True, eps=EPS)
                nT = yield from to_T(YN, XT, nn)
                yield
                return (yield from mlp(XT, nT, wv(fc), None, 4, "relu2", wv(pj).rearrange("p (j c) -> p j c", c=128),
                                       add_scaled(Z, wv(sc)), d_wm))

            dz = yield from relu_mlp([dy, st_["end"]], "mfc", "mpj", "mmsc")
            dza = yield from mix(Z, Z, wv("ra0"), XN, wv("ra1"), dz)
            yield
            nn = yield from norm(Z, YN, dza, rms=True, eps=EPS)
            nT = yield from to_T(YN, XT, nn)
            yield
            dqk = []
            t2 = P.dve(lambda e: e.memset(V9[:, :, 0:4, 8:9], 1.0), nT)
            for g2 in range(2):
                ps, w = yield from get(PS)
                for j in range(2):
                    t = 2 * g2 + j
                    k = mm(ps[:, j * 192:(j + 1) * 192], XT[:, t * 128:(t + 1) * 128], wv("qkv"), True, True,
                           w, nT, d_wc)
                p3 = ps[:, 0:384].rearrange("p (t c) -> p t c", c=192)
                v = cp("act", QK[:, 2 * g2:2 * g2 + 2, :], p3[:, :, 0:160], k)
                v2 = cp("act", V9[:, 2 * g2:2 * g2 + 2, 0:4, 0:8],
                        p3[:, :, 160:192].rearrange("p t (h d) -> p t h d", d=8), k)
                PS.give(ps, v2)
                dqk += [v, v2]
            yield
            dqr = []

            def rope(t):
                j = t % 2
                s2, sw = yield from get(S2)
                ss, ssw = yield from get(SS)
                qk = QK[:, t, :]
                q3 = qk.rearrange("p (h d) -> p h d", d=8)
                sq = s2[:, 0:160]
                a = tt(sq, qk, qk, ALU.mult, dqk, sw)
                a = red(ss[:, 0:20], sq.rearrange("p (h d) -> p h d", d=8), ALU.add, a, ssw)
                a = ts(ss[:, 0:20], ss[:, 0:20], 0.125, EPS, ALU.mult, ALU.add, a)
                a = P.pool(lambda e: e.tensor_tensor(ss[:, 20:40], ss[:, 0:20],
                                                     mhalf[:, 0:1].to_broadcast([128, 20]), ALU.pow), a)
                yield
                b1_ = stt(ss[:, 20:36], ss[:, 20:36], float(np.float32(8.0 ** -0.5)), wv("qg"), ALU.mult, ALU.mult,
                          a, d_ve)
                a = tt(q3, q3, ss[:, 20:40].unsqueeze(2).to_broadcast([128, 20, 8]), ALU.mult, b1_)
                SS.give(ss, a)
                cos = wv("cos")[:, 4 * j:4 * j + 4].unsqueeze(1).to_broadcast([128, 20, 4])
                sin = wv("sin")[:, 4 * j:4 * j + 4].unsqueeze(1).to_broadcast([128, 20, 4])
                xa, xb = q3[:, :, 0:4], q3[:, :, 4:8]
                r3 = s2[:, 0:160].rearrange("p (h d) -> p h d", d=8)
                u3 = s2[:, 160:320].rearrange("p (h d) -> p h d", d=8)
                e1 = tt(r3[:, :, 0:4], xa, cos, ALU.mult, a, d_co)
                e2 = tt(u3[:, :, 0:4], xb, sin, ALU.mult, a)
                e3 = tt(r3[:, :, 4:8], xb, cos, ALU.mult, a)
                e4 = tt(u3[:, :, 4:8], xa, sin, ALU.mult, a)
                yield
                kr4 = KR[:, t, :].rearrange("p (g r d) -> p g r d", g=4, d=8)
                o1 = tt(q3[:, :, 0:4], r3[:, :, 0:4], u3[:, :, 0:4], ALU.add, e1, e2, e4)
                o2 = tt(q3[:, :, 4:8], r3[:, :, 4:8], u3[:, :, 4:8], ALU.subtract, e3, e4, e2)
                S2.give(s2, o1, o2)
                dqr.append(P.pool(lambda e: e.tensor_copy(QR[:, t, :], QK[:, t, 0:128]), o1, o2))
                k3_ = QK[:, t, 128:160].rearrange("p (g d) -> p g d", d=8)
                dqr.append(P.dve(lambda e: e.tensor_copy(kr4, k3_.unsqueeze(2).to_broadcast([128, 4, 4, 8])), o1, o2))

            yield from gpipe(rope(t) for t in range(4))
            dq = yield from to_T(QR, QT, dqr)
            dk = yield from to_T(KR, KT, dqr)
            yield
            ka = yield from attn(QT, KT, lambda t, h: V9[:, t, h // 4, :], 16, 8, wv("hm8"), O4, [dq, dk, dqk, t2])
            yield
            oT = yield from to_T(O4, XT, ka)
            yield
            dz = yield from proj_tok(wv("ow"), XT, [oT, d_wc], add_scaled(Z, wv("asc")))
            yield
            dz = yield from relu_mlp(dz, "afc", "apj", "amsc")
            dxg[g] = yield from post(X, Z, dz)

        lent = [(wAB[:, 512 * i:512 * i + 512], []) for i in range(8)]
        S2.lend(lent)
        flow(group23, range(8), range(3), STAG1)
        S2.back(lent)
        last = P.fence()

        OA = AR[:, 4096:8192].rearrange("p (t c) -> p t c", c=128)
        d_we = [dma(AR[:, 8192 + 1024 * e:9216 + 1024 * e], wd[:, 1024 * e:1024 * (e + 1)], last) for e in range(8)]
        flow(smoe_in, range(8), range(4), 1)
        GM = AR[:, 16384:16640].rearrange("p (m c) -> p m c", m=2)
        ps, w = PS.take()
        for t in range(32):
            k = mm(ps[:, t * 8:(t + 1) * 8], XTA[:, t * 128:(t + 1) * 128], wv("gate"), True, True, w, xTh[t // 4], d_ve)
        PRB = AR[:, 16640:16896]
        PR2 = AR[:, 16896:17152]
        st = AR[:, 17152:17216]
        p3 = ps[:, 0:256].rearrange("p (t e) -> p t e", e=8)
        s3 = PRB.rearrange("p (t e) -> p t e", e=8)
        a = P.dve(lambda e: e.tensor_reduce(st[:, 0:32], p3, X_AX, ALU.max), k)
        a = tt(s3, p3, st[:, 0:32].unsqueeze(2).to_broadcast([128, 32, 8]), ALU.subtract, a)
        PS.give(ps, a)
        a = P.act(lambda e: e.activation(PRB, PRB, ACT.Exp), a)
        a = P.dve(lambda e: e.tensor_reduce(st[:, 32:64], s3, X_AX, ALU.add), a)
        a = P.dve(lambda e: e.reciprocal(st[:, 32:64], st[:, 32:64]), a)
        kp = tt(PR2.rearrange("p (m b e) -> p b m e", m=2, b=16), PRB.rearrange("p (b m e) -> p b m e", m=2, b=16),
                st[:, 32:64].rearrange("p (b m) -> p b m", m=2).unsqueeze(3).to_broadcast([128, 16, 2, 8]),
                ALU.mult, a)
        ps, w = PS.take()
        for m_ in range(2):
            k = tr(ps[:, m_ * 128:(m_ + 1) * 128], PR2[:, m_ * 128:(m_ + 1) * 128], w, kp)
        pp, wk = AR[:, 17216:17472], AR[:, 17472:17728]
        m8 = AR[:, 17728:17736]
        v1 = P.dve(lambda e, s_=ps[:, 0:256]: e.tensor_copy(pp, s_), k)
        a = v2 = P.dve(lambda e, s_=ps[:, 0:256]: e.tensor_copy(wk, s_), k)
        PS.give(ps, v1, v2)
        for r in range(8):
            a = P.dve(lambda e: e.max(m8, wk), a)
            a = P.dve(lambda e: e.match_replace(wk, m8, wk, -1.0), a)
        a = ts(wk, wk, 0.0, None, ALU.is_lt, None, a)
        a = tt(wk, wk, pp, ALU.mult, a, v1)
        ps, w = PS.take()
        for m_ in range(2):
            k = tr(ps[:, m_ * 128:(m_ + 1) * 128], wk[:, m_ * 128:(m_ + 1) * 128], w, a)
        kg = P.dve(lambda e: e.tensor_copy(GM, ps[:, 0:256].rearrange("p (m c) -> p m c", m=2)), k)
        PS.give(ps, kg)
        dyp = [None] * 32

        def expert(it, _):
            ex, g = it
            we = AR[:, 8192 + 1024 * ex:9216 + 1024 * ex]

            def fin(ps, k):
                vs = []
                for j in range(4):
                    t = 4 * g + j
                    c = 8 * (t // 2) + ex
                    gm = GM[:, t % 2, c:c + 1]
                    pj = ps[:, j * 128:(j + 1) * 128]
                    if ex == 0:
                        v = ts(OA[:, t, :], pj, gm, None, ALU.mult, None, k, kg)
                    else:
                        v = stt(OA[:, t, :], pj, gm, OA[:, t, :], ALU.mult, ALU.add, k, dyp[t])
                    dyp[t] = v
                    vs.append(v)
                return vs

            yield from mlp(XTA[:, 512 * g:512 * g + 512], xTh[g], we[:, 0:512], None, 4, ACT.Gelu_apprx_tanh,
                           we[:, 512:1024].rearrange("p (j c) -> p j c", c=128), fin, d_we[ex])

        flow(expert, [(ex, g) for ex in range(8) for g in range(8)], range(2), 2)
        d_outs = []
        YB = AR[:, 0:2048].bitcast(BF16).rearrange("p (t c) -> p t c", c=128)
        SB = AR[:, 17792:17856].bitcast(BF16)
        SF = AR[:, 17920:18304]
        P.fence()
        kf = [P.dve(lambda e, g=g: e.tensor_copy(YB[:, 4 * g:4 * g + 4, :], OA[:, 4 * g:4 * g + 4, :]), dyp)
              for g in range(8)]
        ag = []
        for t in range(32):
            a = P.dve(lambda e, t=t: e.bn_stats(SF[:, 6 * t:6 * t + 6], YB[:, t, :]), kf[t // 4])
            ag.append(P.dve(lambda e, t=t: e.bn_aggr(SF[:, 192 + 2 * t:194 + 2 * t], SF[:, 6 * t:6 * t + 6]), a))
        mv = SF[:, 192:256].rearrange("p (t c) -> p t c", c=2)
        mb_, vb_, eb_, sb_ = SB[:, 0:32], SB[:, 32:64], SB[:, 64:96], SB[:, 96:128]
        a1 = P.dve(lambda e: e.tensor_copy(mb_, mv[:, :, 0]), ag)
        a2 = P.dve(lambda e: e.tensor_copy(vb_, mv[:, :, 1]), ag)
        a3_ = ts(eb_, vb_, EPSB, None, ALU.add, None, a2)
        s_ = P.act(lambda e: e.activation(sb_, eb_, ACT.Sqrt), a3_)
        rr = P.dve(lambda e: e.reciprocal(SF[:, 256:288], sb_), s_)
        mf = P.dve(lambda e: e.tensor_copy(SF[:, 288:320], mb_), a1)
        orows = out.rearrange("b (t p) d -> p (b t) d", p=128)
        outs = []
        for t in range(32):
            a = ts(YB[:, t, :], YB[:, t, :], SF[:, 288 + t:289 + t], None, ALU.subtract, None, mf)
            a = ts(YB[:, t, :], YB[:, t, :], SF[:, 256 + t:257 + t], None, ALU.mult, None, a, rr)
            outs.append(tt(XA[:, t, :], XA[:, t, :], YB[:, t, :], ALU.add, a))
            if t % 8 == 7:
                d_out = dma(orows[:, t - 7:t + 1, :], XA[:, t - 7:t + 1, :], outs[t - 7:t + 1])
                d_outs.append(d_out)
        for d_out in d_outs:
            P.op("sp", lambda e: None, d_out)

        used = {e: set() for e in P.q}
        for e in P.q:
            for deps, _ in P.q[e]:
                for d in deps:
                    if isinstance(d, Tok):
                        used[d.eng].add(d.idx)
        STEP = 4000
        where = {}
        for e in P.q:
            n = 0
            for idx in sorted(used[e]):
                where[(e, idx)] = (n // STEP, n % STEP + 1)
                n += 1
        esem = {}
        for e in P.q:
            if used[e]:
                for c in range((len(used[e]) + STEP - 1) // STEP):
                    esem[(e, c)] = ctx.enter_context(nc.semaphore(f"s_{e}{c}"))

        def stream(name, eng):
            seen = {}
            seen_dma = set()
            for idx, (deps, fn) in enumerate(P.q[name]):
                need = {}
                for d in deps:
                    if isinstance(d, DmaTok):
                        if id(d) not in seen_dma:
                            seen_dma.add(id(d))
                            eng.wait_ge(d.sem, d.val)
                    else:
                        if d.eng == name == "pe":
                            continue
                        need[d.eng] = max(need.get(d.eng, (-1, 0)), where[(d.eng, d.idx)])
                for p, at in need.items():
                    if seen.get(p, (-1, 0)) < at:
                        seen[p] = at
                        eng.wait_ge(esem[(p, at[0])], at[1])
                ins = fn(eng)
                if idx in used[name] and ins is not None:
                    ins.then_inc(esem[(name, where[(name, idx)][0])], 1)

        block = ctx.enter_context(nc.Block())

        @block.sync
        def _(eng):
            stream("sp", eng)

        @block.gpsimd
        def _(eng):
            stream("pool", eng)

        @block.scalar
        def _(eng):
            stream("act", eng)

        @block.tensor
        def _(eng):
            stream("pe", eng)

        @block.vector
        def _(eng):
            stream("dve", eng)


def shape_constants():
    c = np.zeros((128, NCO), np.float32)
    i = np.arange(128)

    def put(name, v):
        o, n = CO[name]
        c[:v.shape[0], o:o + n] = v

    put("ident", np.eye(128, dtype=np.float32))
    put("cmask", np.where(i[None, :] > i[:, None], np.float32(NEG), np.float32(0)))
    put("dif", np.maximum(i[None, :] - i[:, None], 0).astype(np.float32))
    put("tri", (i[None, :] >= i[:, None]).astype(np.float32))
    put("qp1", (i[:, None] + 1).astype(np.float32))
    put("rev", (127 - i[:, None]).astype(np.float32))
    inv = (np.float32(1.0) / np.power(np.float32(10000.0), np.arange(0, 8, 2, dtype=np.float32) / np.float32(8)))
    f = np.outer(np.arange(256, dtype=np.float32), inv.astype(np.float32)).astype(np.float32)
    put("cos", np.cos(f).astype(np.float32).reshape(2, 128, 4).transpose(1, 0, 2).reshape(128, 8))
    put("sin", np.sin(f).astype(np.float32).reshape(2, 128, 4).transpose(1, 0, 2).reshape(128, 8))
    put("hm8", (i[:, None] // 8 == np.arange(16)[None, :]).astype(np.float32))
    put("hm16", (i[:, None] // 16 == np.arange(4)[None, :]).astype(np.float32))
    put("bm64", (i[:, None] // 64 == np.arange(32)[None, :] // 16).astype(np.float32))
    put("bm16", (np.arange(64)[:, None] // 16 == np.arange(64)[None, :] // 16).astype(np.float32))
    return c


def step_constant():
    s, i = np.arange(384), np.arange(128)
    return (s[None, :] - 128 <= i[:, None]).astype(np.float32)


def kernel(**inputs):
    import numpy as _np
    import concourse.bacc as _bacc
    from concourse import mybir as _mybir
    from concourse.bass_utils import run_bass_kernel_spmd as _run

    I = {k: _np.asarray(v) for k, v in inputs.items()}

    def pack(tab, n, parts, dt=_np.float32):
        a = _np.zeros((128, n), dt)
        for name, v in parts.items():
            o, w = tab[name]
            assert v.shape[1] == w, (name, v.shape, w)
            a[:v.shape[0], o:o + w] = v
        return a

    def ktiles(w):
        k = w.shape[0] // 128
        return w.reshape(k, 128, -1).transpose(1, 0, 2).reshape(128, -1)

    def rep(v):
        v = v.reshape(1, -1)
        return _np.broadcast_to(v, (128, v.shape[1]))

    pa = {"wq0": I["L0_attn_Wq"], "wk0": I["L0_attn_Wk"], "wvd": I["L0_attn_Wvdown"].T, "wvu": I["L0_attn_Wvup"]}
    for i in range(4):
        q, k, v = I["L1_attn_Wq"][i], I["L1_attn_Wk"][i], I["L1_attn_Wv"][i]
        pa[f"l1q{i}"], pa[f"l1k{i}"] = q, k
        pa[f"l1vqk{i}"] = _np.concatenate([v, q[:, 64:], k[:, 64:]], axis=1)
        pa[f"l1o{i}"] = I["L1_attn_Wo"][i]
        pa[f"l1w1{i}"] = I["L1_attn_W1"][i]
        pa[f"l1w2{i}"] = ktiles(I["L1_attn_W2"][i])
    pb = {"phi": I["L1_ffn_phi"].reshape(128, 2048), "W": I["L1_ffn_W"].transpose(1, 0, 2).reshape(128, 8192)}
    pa["bo"], pa["b2"] = rep(I["L1_attn_bo"]), rep(I["L1_attn_b2"])
    pc = {"l2q": I["L2_attn_Wq"], "l2k": I["L2_attn_Wk"], "l2v": I["L2_attn_Wv"], "l2o": I["L2_attn_Wo"],
          "l2w1": I["L2_ffn_w1"], "l2w2": ktiles(I["L2_ffn_w2"]), "inp": I["L3_attn_in_proj_w"],
          "bp": I["L3_attn_B_proj_w"], "cp": I["L3_attn_C_proj_w"], "outp": ktiles(I["L3_attn_out_proj_w"]),
          "qkv": _np.concatenate([I["L3_attn_q_w"], I["L3_attn_k_w"], I["L3_attn_v_w"]], axis=1),
          "ow": I["L3_attn_o_w"]}
    pd = {}
    for e in range(8):
        pd[f"w1{e}"], pd[f"w2{e}"] = I["L3_ffn_w1"][e], ktiles(I["L3_ffn_w2"][e])
    pm = {"mfc": I["L3_attn_m_fc_w"], "mpj": ktiles(I["L3_attn_m_proj_w"]),
          "afc": I["L3_attn_a_fc_w"], "apj": ktiles(I["L3_attn_a_proj_w"])}
    pi = {"wg": I["L0_ffn_w_gate"].T, "wu": I["L0_ffn_w_up"].T, "wd": ktiles(I["L0_ffn_w_down"].T)}

    pv = {"ln1g": I["L1_attn_ln1_g"].T, "ln1b": I["L1_attn_ln1_b"].T, "ln2g": I["L1_attn_ln2_g"].T,
          "ln2b": I["L1_attn_ln2_b"].T,
          "b1": I["L1_attn_b1"].reshape(4, 4, 128).transpose(2, 0, 1).reshape(128, 16),
          "l2b1": I["L2_ffn_b1"].reshape(4, 128).T,
          "convw": I["L3_attn_conv_w"].reshape(2, 128, 4).transpose(1, 0, 2).reshape(128, 8),
          "convb": I["L3_attn_conv_b"].reshape(2, 128).T,
          "dpar": _np.repeat(I["L3_attn_D_param"], 16).reshape(2, 128).T,
          "mb": I["L1_ffn_b"].T, "dt": rep(I["L3_attn_dt_bias"]), "al": rep(I["L3_attn_A_log"]),
          "qg": rep(I["L3_attn_q_gain"]), "gate": I["L3_ffn_gate_w"], "l2b2": rep(I["L2_ffn_b2"]), "rm0": rep(I["L3_attn_resid_mix_m"][0]),
          "rm1": rep(I["L3_attn_resid_mix_m"][1]), "msc": rep(I["L3_attn_mamba_scale"]),
          "mmsc": rep(I["L3_attn_m_mlp_scale"]), "ra0": rep(I["L3_attn_resid_mix_a"][0]),
          "ra1": rep(I["L3_attn_resid_mix_a"][1]), "asc": rep(I["L3_attn_attn_scale"]),
          "amsc": rep(I["L3_attn_a_mlp_scale"])}
    arrays = {
        "wa": pack(WA, NA, pa), "wb": pack(WB, NB, pb), "wc": pack(WC, NC, pc), "wd": pack(WD, ND, pd), "wm": pack(WM, NM, pm),
        "wi": pack(WI, NI, pi, _np.int32), "ve": pack(VE, NV, pv), "co": shape_constants(), "step": step_constant(),
        "xin": _np.ascontiguousarray(I["L0_attn_inputs"]),
    }
    nc = _bacc.Bacc("TRN2", target_bir_lowering=False, num_devices=1)
    args = [nc.dram_tensor(k, a.shape, _mybir.dt.from_np(a.dtype), kind="ExternalInput").ap()
            for k, a in arrays.items()]
    o = nc.dram_tensor("y", (16, 256, 128), _mybir.dt.float32, kind="ExternalOutput").ap()
    build(nc, *args, o)
    r = _run(nc, [arrays], core_ids=[0])
    return r.results[0]["y"]
```

```python
from contextlib import ExitStack

import numpy as np

import concourse.bass as bass
from concourse import mybir

F32 = mybir.dt.float32
BF16 = mybir.dt.bfloat16
I32 = mybir.dt.int32
ALU = mybir.AluOpType
ACT = mybir.ActivationFunctionType
X_AX = mybir.AxisListType.X
NEG = -3.0e38
FMIN = float(np.finfo(np.float32).min)
NS2 = 8
STAG0, STAG1 = 2, 2
PARB = False
SCLAG = 3
SLAG = 12
EPSB = 1.0013580322265625e-05


def layout(pieces):
    at, off = {}, 0
    for name, n in pieces:
        at[name] = (off, n)
        off += n
    return at, off


WA, NA = layout([("wq0", 32), ("wk0", 32), ("wvd", 128), ("wvu", 128)]
                + [(f"{n}{i}", w) for i in range(4)
                   for n, w in (("l1q", 128), ("l1k", 128), ("l1vqk", 256), ("l1o", 128), ("l1w1", 512), ("l1w2", 512))]
                + [("bo", 512), ("b2", 512)])
WB, NB = layout([("phi", 2048), ("W", 8192)])
WM, NM = layout([("mfc", 512), ("mpj", 512), ("afc", 512), ("apj", 512)])
WC, NC = layout([("l2q", 128), ("l2k", 128), ("l2v", 128), ("l2o", 128), ("l2w1", 512), ("l2w2", 512),
                 ("inp", 512), ("bp", 1024), ("cp", 1024), ("outp", 256),
                 ("qkv", 192), ("ow", 128)])
WD, ND = layout([(f"{n}{e}", 512) for e in range(8) for n in ("w1", "w2")])
WI, NI = layout([("wg", 384), ("wu", 384), ("wd", 384)])
VE, NV = layout([("ln1g", 4), ("ln1b", 4), ("ln2g", 4), ("ln2b", 4), ("b1", 16), ("l2b1", 4), ("convw", 8),
                 ("convb", 2), ("dpar", 2), ("mb", 64), ("dt", 16), ("al", 16),
                 ("qg", 16), ("gate", 8), ("l2b2", 128), ("rm0", 128), ("rm1", 128),
                 ("msc", 128), ("mmsc", 128), ("ra0", 128), ("ra1", 128), ("asc", 128), ("amsc", 128)])
CO, NCO = layout([("ident", 128), ("cmask", 128), ("dif", 128), ("tri", 128), ("qp1", 1),
                  ("rev", 1), ("cos", 8), ("sin", 8), ("hm8", 16), ("hm16", 4), ("bm64", 32), ("bm16", 64), ("iota", 64)])


class Tok:
    __slots__ = ("eng", "idx")

    def __init__(self, eng, idx):
        self.eng, self.idx = eng, idx


class DmaTok:
    __slots__ = ("sem", "val")

    def __init__(self, sem, val):
        self.sem, self.val = sem, val


def flat(deps):
    for d in deps:
        if d is None:
            continue
        if isinstance(d, (list, tuple)):
            yield from flat(d)
        else:
            yield d


class Queues:

    def __init__(self):
        self.q = {e: [] for e in ("pe", "act", "dve", "pool", "sp")}
        self.pending = {e: [] for e in self.q}

    def op(self, eng, fn, *deps):
        d = list(flat(deps)) + self.pending[eng]
        self.pending[eng] = []
        self.q[eng].append((d, fn))
        return Tok(eng, len(self.q[eng]) - 1)

    def pe(self, fn, *deps):
        return self.op("pe", fn, *deps)

    def act(self, fn, *deps):
        return self.op("act", fn, *deps)

    def dve(self, fn, *deps):
        return self.op("dve", fn, *deps)

    def pool(self, fn, *deps):
        return self.op("pool", fn, *deps)

    def fence(self):
        last = [Tok(e, len(self.q[e]) - 1) for e in ("pe", "act", "dve", "pool") if self.q[e]]
        for e in ("pe", "act", "dve", "pool"):
            self.pending[e] = [t for t in last]
        return last


class Ring:

    def __init__(self, bufs):
        self.free = [(b, []) for b in bufs]

    def take(self):
        assert self.free, "no buffer has been given back"
        return self.free.pop(0)

    def give(self, buf, *toks):
        self.free.append((buf, list(flat(toks))))

    def lend(self, bufs):
        self.free += [(b, list(flat([d]))) for b, d in bufs]

    def back(self, bufs):
        assert all(any(b is f for f, _ in self.free) for b, _ in bufs)
        self.free = [(f, d) for f, d in self.free if not any(f is b for b, _ in bufs)]


def gpipe(gens, lag=1):
    live, gens, n = [], list(gens), 0
    while gens or live:
        for g in list(live):
            try:
                next(g)
            except StopIteration:
                live.remove(g)
        if gens and (n % lag == 0 or not live):
            g = gens.pop(0)
            try:
                next(g)
                live.append(g)
            except StopIteration:
                pass
        n += 1
        yield


def par(*gens):
    out, live = [None] * len(gens), list(enumerate(gens))
    while live:
        for n, g in list(live):
            try:
                next(g)
            except StopIteration as e:
                out[n] = e.value
                live.remove((n, g))
        if live:
            yield
    return out


def flow(make, items, slots, stagger):
    items, free, live, since = list(items), list(slots), [], stagger
    while items or live:
        for g, s in list(live):
            try:
                next(g)
            except StopIteration:
                live.remove((g, s))
                free.append(s)
        since += 1
        if items and free and (since >= stagger or not live):
            s = free.pop(0)
            live.append((make(items.pop(0), s), s))
            since = 0


def get(ring):
    n = 0
    while not ring.free:
        n += 1
        assert n < 1000, "the ring is held for good"
        yield
    return ring.take()


def build(nc, wa, wb, wc, wd, wm, wi, ve, co, step, xin, out):
    ctx = ExitStack()
    with ctx:
        def sb(name, shape, dt=F32):
            return ctx.enter_context(nc.sbuf_tensor(name, shape, dt))

        XA = sb("XA", [128, 32, 128])
        AR = sb("AR", [128, 24576])
        wAB = sb("wAB", [128, 8192])
        wCs = sb("wCs", [128, NC])
        vecs = sb("vecs", [128, NV])
        cons = sb("cons", [128, NCO])
        identb = sb("identb", [128, 128], BF16)
        cmaskb = sb("cmaskb", [128, 128], BF16)
        MISC = sb("MISC", [128, 512])
        R8 = sb("R8", [128, 2, 2048])
        R2 = sb("R2", [128, NS2, 512])
        RS = sb("RS", [128, 12, 64])
        psum = [ctx.enter_context(nc.psum_tensor(f"ps{i}", [128, 512], F32)) for i in range(8)]

        P = Queues()
        PS = Ring(psum)
        S8 = Ring([R8[:, i, :] for i in range(2)])
        S2 = Ring([R2[:, i, :] for i in range(NS2)])
        SS = Ring([RS[:, i, :] for i in range(12)])
        sems = []

        def dma(dst, src, *deps):
            s = ctx.enter_context(nc.semaphore(f"s_dma{len(sems)}"))
            sems.append(s)
            P.op("sp", lambda e: (e.dma_start(dst, src).then_inc(s, 16), None)[1], *deps)
            return DmaTok(s, 16)

        def wv(name):
            for tab, t, base in ((WA, wAB, 0), (WM, wAB, 4096), (WC, wCs, 0), (VE, vecs, 0), (CO, cons, 0)):
                if name in tab:
                    o, n = tab[name]
                    return t[:, base + o:base + o + n]
            raise KeyError(name)

        ident = wv("ident")
        SLOT = 8192
        XG = [XA[:, 4 * g:4 * g + 4, :] for g in range(8)]

        d_co = dma(cons[:, :], co)
        xrows = xin.rearrange("b (t p) d -> p (b t) d", p=128)
        d_x = [dma(XA[:, 4 * i:4 * i + 4, :], xrows[:, 4 * i:4 * i + 4, :]) for i in range(2)]
        d_wa0 = dma(wAB[:, 0:320], wa[:, 0:320])
        STEPM = AR[:, 6400:6784]
        d_st = dma(STEPM, step)
        d_ve = dma(vecs[:, :], ve)
        wi_s = AR[:, SLOT + 6400:SLOT + 6400 + NI].bitcast(I32)
        d_wi = dma(wi_s, wi)
        d_x += [dma(XA[:, 4 * i:4 * i + 4, :], xrows[:, 4 * i:4 * i + 4, :]) for i in range(2, 8)]
        d_wa = dma(wAB[:, 320:NA], wa[:, 320:NA])
        t_cb = P.act(lambda e: e.copy(identb[:, :], ident), d_co)
        t_cb = [t_cb, P.act(lambda e: e.copy(cmaskb[:, :], wv("cmask")), d_co)]
        mhalf = MISC[:, 0:4]
        t_mh = P.dve(lambda e: e.memset(mhalf, -0.5))

        load = {"act": 0.0, "dve": 0.0}

        def size(ap):
            n = 1
            for d in ap.shape[1:]:
                n *= d
            return n

        def mm(out, lhsT, rhs, start, stop, *deps):
            return P.pe(lambda e: e.matmul(out, lhsT, rhs, start=start, stop=stop), *deps)

        def tr(out, in_, *deps):
            k = in_.shape[0]
            return P.pe(lambda e: e.transpose(out, in_, ident[0:k, 0:k]), d_co, *deps)

        def cp(eng, out, in_, *deps):
            load[eng] += (0.19 + size(out) / 1200) if eng == "act" else (0.12 + size(out) / 960)
            if eng == "act":
                return P.act(lambda e: e.copy(out, in_), *deps)
            return P.dve(lambda e: e.tensor_copy(out, in_), *deps)

        def evac(out, in_, *deps):
            return cp("act" if load["act"] < load["dve"] else "dve", out, in_, *deps)

        def act(out, in_, f, *deps, bias=None, scale=None, acc=None):
            load["act"] += 0.2 + size(out) / 1200 + (0.09 if acc is not None else 0)
            kw = {}
            if bias is not None:
                kw["bias"] = bias
            if scale is not None:
                kw["scale"] = scale
            if acc is not None:
                kw["accum_out"] = acc
            return P.act(lambda e: e.activation(out, in_, f, **kw), *deps)

        def tt(out, a, b, op, *deps):
            load["dve"] += 0.08 + size(out) / 960
            return P.dve(lambda e: e.tensor_tensor(out, a, b, op), *deps)

        def ts(out, a, s1, s2, op0, op1, *deps):
            load["dve"] += 0.08 + size(out) / 1500
            if op1 is None:
                return P.dve(lambda e: e.tensor_scalar(out, a, s1, None, op0), *deps)
            return P.dve(lambda e: e.tensor_scalar(out, a, s1, s2, op0, op1), *deps)

        def stt(out, a, s, b, op0, op1, *deps):
            load["dve"] += 0.08 + size(out) / 960
            return P.dve(lambda e: e.scalar_tensor_tensor(out, a, s, b, op0, op1), *deps)

        def red(out, a, op, *deps, negate=False):
            load["dve"] += 0.08 + size(a) / 960
            return P.dve(lambda e: e.tensor_reduce(out, a, X_AX, op, negate=negate), *deps)

        def rcp(out, a, *deps):
            load["dve"] += 0.08 + size(out) / 960
            return P.dve(lambda e: e.reciprocal(out, a), *deps)

        def v4(ps):
            return ps[:, :].rearrange("p (t c) -> p t c", c=128)

        def rep4(v):
            return v.unsqueeze(1).to_broadcast([128, 4, 128])

        def norm(src, dst, deps, rms=False, eps=1e-5):
            buf, w = yield from get(SS)
            st = [P.dve(lambda e, i=i: e.bn_stats(buf[:, 6 * i:6 * i + 6], src[:, i, :]), w, deps) for i in range(4)]
            ag = [P.dve(lambda e, i=i: e.bn_aggr(buf[:, 24 + 2 * i:26 + 2 * i], buf[:, 6 * i:6 * i + 6]), st[i])
                  for i in range(4)]
            load["dve"] += 1.2
            mv = buf[:, 24:32].rearrange("p (i c) -> p i c", c=2)
            if rms:
                a = tt(buf[:, 32:36], mv[:, :, 0], mv[:, :, 0], ALU.mult, ag)
                b = stt(buf[:, 36:40], buf[:, 32:36], eps, mv[:, :, 1], ALU.add, ALU.add, a, ag)
            else:
                b = ts(buf[:, 36:40], mv[:, :, 1], eps, None, ALU.add, None, ag)
            r = P.pool(lambda e: e.tensor_tensor(buf[:, 40:44], buf[:, 36:40], mhalf, ALU.pow), b, t_mh)
            yield
            last = []
            for i in range(4):
                rs = buf[:, 40 + i:41 + i]
                if rms:
                    last.append(ts(dst[:, i, :], src[:, i, :], rs, None, ALU.mult, None, r, st))
                else:
                    last.append(ts(dst[:, i, :], src[:, i, :], buf[:, 24 + 2 * i:25 + 2 * i], rs, ALU.subtract,
                                   ALU.mult, r, ag[i], st))
            SS.give(buf, last)
            return last

        def to_T(src, dstT, deps, g_=None, b_=None):
            yield
            ps, w = yield from get(PS)
            for i in range(4):
                k = tr(ps[:, i * 128:(i + 1) * 128], src[:, i, :], w, deps)
            if g_ is None:
                v = evac(dstT, ps[:, :], k)
            else:
                v = ts(dstT, ps[:, :], g_, b_, ALU.mult, ALU.add, k, d_ve)
            PS.give(ps, v)
            return v

        def proj_T(dst, w_, srcT, deps, scale=None):
            m = w_.shape[1]
            ps, w = yield from get(PS)
            k = mm(ps[0:m, :], w_, srcT, True, True, w, deps)
            v = evac(dst, ps[0:m, :], k) if scale is None else ts(dst, ps[0:m, :], scale, None, ALU.mult, None, k)
            PS.give(ps, v)
            return v

        def proj_tok(w_, srcT, deps, fin):
            ps, w = yield from get(PS)
            for i in range(4):
                k = mm(ps[:, i * 128:(i + 1) * 128], srcT[:, i * 128:(i + 1) * 128], w_, True, True, w, deps)
            v = fin(ps, k)
            PS.give(ps, v)
            return v

        def to(dst):
            return lambda ps, k: evac(dst, v4(ps), k)

        def add_rep(dst, rep):
            def fin(ps, k):
                a = tt(dst, dst, v4(ps), ALU.add, k)
                return tt(dst, dst, rep4(rep), ALU.add, a, d_ve, d_wa)
            return fin

        def add_scaled(dst, rep):
            def fin(ps, k):
                tmp, w = S2.take()
                a = tt(v4(tmp), v4(ps), rep4(rep), ALU.mult, k, w, d_ve)
                b = tt(dst, dst, v4(tmp), ALU.add, a)
                S2.give(tmp, b)
                return [a, b]
            return fin

        def pre(X, XN, XT, deps):
            n = yield from norm(X, XN, deps)
            return (yield from to_T(XN, XT, n))

        def post(X, Y, deps):
            n = yield from norm(Y, Y, deps)
            return tt(X, X, Y, ALU.add, n)

        def mlp(xT, deps, w1, b1, nh, kind, w2, fin, wdep, w1b=None):
            h, hw = yield from get(S8)
            h3 = h.rearrange("p (j n) -> p j n", n=512)
            hk = []
            for j in range(nh):
                ps, w = yield from get(PS)
                k = mm(ps[:, :], w1[:, j * 128:(j + 1) * 128], xT, True, True, w, wdep, deps)
                if kind == "silu":
                    a = act(h3[:, j, :], ps[:, :], ACT.Silu, hw, k)
                    PS.give(ps, a)
                    p2, w_2 = yield from get(PS)
                    k2 = mm(p2[:, :], w1b[:, j * 128:(j + 1) * 128], xT, True, True, w_2, wdep)
                    v = tt(h3[:, j, :], h3[:, j, :], p2[:, :], ALU.mult, a, k2)
                    PS.give(p2, v)
                elif kind == "relu2":
                    a = act(h3[:, j, :], ps[:, :], ACT.Relu, hw, k)
                    v = stt(h3[:, j, :], ps[:, :], 0.0, h3[:, j, :], ALU.max, ALU.mult, a)
                    PS.give(ps, v)
                else:
                    v = act(h3[:, j, :], ps[:, :], kind, hw, k, d_ve, bias=None if b1 is None else b1[:, j:j + 1])
                    PS.give(ps, v)
                hk.append(v)
                yield
            yield
            ps, w = yield from get(PS)
            for i in range(4):
                for j in range(nh):
                    k = mm(ps[:, i * 128:(i + 1) * 128], h3[:, j, i * 128:(i + 1) * 128], w2[:, j, :],
                           j == 0, j == nh - 1, w, hk)
            S8.give(h, k)
            v = fin(ps, k)
            PS.give(ps, v)
            yield
            return v

        def attn_item(q, kT, v0, v1, po0, po1, deps, kdeps, done):
            ps, w = yield from get(PS)
            p_, pw = yield from get(S2)
            st, sw = yield from get(SS)
            mm(ps[:, 0:128], q[:, 0:128], kT[:, 0:128], True, False, w, deps, kdeps)
            mm(ps[:, 0:128], identb[:, :], cmaskb[:, :], False, True, t_cb)
            mm(ps[:, 128:384], q[:, 128:256], kT[:, 0:256], True, False)
            k = mm(ps[:, 256:384], identb[:, :], cmaskb[:, :], False, True)
            m0 = red(st[:, 0:1], ps[:, 0:128], ALU.max, k, sw, negate=True)
            m1 = red(st[:, 1:2], ps[:, 128:384], ALU.max, k, sw, negate=True)
            x0 = act(p_[:, 0:128], ps[:, 0:128], ACT.Exp, m0, m1, pw, bias=st[:, 0:1])
            x1 = act(p_[:, 128:384], ps[:, 128:384], ACT.Exp, m1, bias=st[:, 1:2])
            PS.give(ps, x1)
            SS.give(st, x1)
            yield k
            pt, w = yield from get(PS)
            pT, pw = yield from get(S2)
            for j in range(3):
                k = tr(pt[:, j * 128:(j + 1) * 128], p_[:, j * 128:(j + 1) * 128], w, x0, x1)
            S2.give(p_, k)
            v = evac(pT[:, 0:384], pt[:, 0:384], k, pw)
            PS.give(pt, v)
            yield
            mm(po0, pT[:, 0:128], v0, True, True, v, deps, kdeps)
            mm(po1, pT[:, 128:256], v0, True, False)
            k = mm(po1, pT[:, 256:384], v1, False, True)
            S2.give(pT, k)
            done.append(k)

        def attn(QT, KT, V, nh, hd, hm, O4, deps):
            out = []
            c = hd + 1

            def batch(b):
                po, pow_ = yield from get(PS)
                done, qm = [], {}

                def mask(h, b=b, qm=qm):
                    q, qw = yield from get(S2)
                    a = P.pool(lambda e: e.tensor_scalar(q[:, 0:256], QT[:, b * 256:(b + 1) * 256], hm[:, h:h + 1],
                                                         None, ALU.mult), deps, qw, d_co)
                    qm[h] = (q, a)

                def item(h, b=b, po=po, pow_=pow_, done=done, qm=qm, mask=mask):
                    if h not in qm:
                        yield from mask(h)
                    if h + 1 < nh and len(S2.free) > 3:
                        yield from mask(h + 1)
                    q, a = qm[h]
                    t0 = 2 * b
                    it = attn_item(q[:, 0:256], KT[:, t0 * 128:(t0 + 2) * 128], V(t0, h), V(t0 + 1, h),
                                   po[:, h * c:(h + 1) * c], po[:, (nh + h) * c:(nh + h + 1) * c],
                                   [a, pow_], deps, done)
                    while True:
                        k = next(it)
                        yield
                        if k is not None:
                            S2.give(q, k)
                            break
                    yield from it

                yield from gpipe(item(h) for h in range(nh))
                r, rw = yield from get(SS)
                p4 = po[:, 0:2 * nh * c].rearrange("p (t h d) -> p t h d", t=2, d=c)
                r3 = r[:, 0:2 * nh].rearrange("p (t h) -> p t h", t=2)
                k = rcp(r3, p4[:, :, :, hd], done, rw)
                for t in range(2):
                    a = tt(O4[:, 2 * b + t, 0:nh * hd].rearrange("p (h d) -> p h d", d=hd), p4[:, t, :, 0:hd],
                           r3[:, t, :].unsqueeze(2).to_broadcast([128, nh, hd]), ALU.mult, k, done)
                    out.append(a)
                PS.give(po, a)
                SS.give(r, a)

            if PARB:
                yield from par(batch(0), batch(1))
            else:
                for b in range(2):
                    yield from batch(b)
            return out

        WV = AR[:, 6784:6912]
        ps, w = PS.take()
        k = mm(ps[:, 0:128], wv("wvd")[0:32, :], wv("wvu")[0:32, :], True, True, w, d_wa0)
        dwv = evac(WV, ps[:, 0:128], k)
        PS.give(ps, dwv)
        wgu = AR[:, 2 * SLOT + 6400:2 * SLOT + 6400 + NI]
        t_wi = ts(wgu, wi_s, float(np.float32(1.0 / 127.0)), None, ALU.mult, None, d_wi)

        def l0_item(b, qt, QT0, KT0, V0, O4, dq, dk, dv, out):
            t = 2 * b + qt
            ps, w = yield from get(PS)
            s_, sw = yield from get(S2)
            st, stw = yield from get(SS)
            k = mm(ps[:, 0:256], QT0[:, t * 128:(t + 1) * 128], KT0[:, b * 256:(b + 1) * 256], True, True, w, dq, dk)
            sc, zz = s_[:, 0:256], s_[:, 256:512]
            o = 128 - 128 * qt
            a = tt(sc, ps[:, 0:256], STEPM[:, o:o + 256], ALU.mult, k, sw, d_st)
            PS.give(ps, a)
            c = ts(zz, sc, 0.0, FMIN, ALU.is_equal, ALU.mult, a)
            d = tt(sc, sc, zz, ALU.add, c)
            m = red(st[:, 0:1], sc, ALU.max, d, stw, negate=True)
            x = act(sc, sc, ACT.Exp, m, bias=st[:, 0:1], acc=st[:, 1:2])
            r = rcp(st[:, 2:3], st[:, 1:2], x)
            yield
            pt, w = yield from get(PS)
            pT, pw = yield from get(S2)
            for j in range(2):
                k = tr(pt[:, j * 128:(j + 1) * 128], sc[:, j * 128:(j + 1) * 128], w, x)
            S2.give(s_, k)
            v = evac(pT[:, 0:256], pt[:, 0:256], k, pw)
            PS.give(pt, v)
            yield
            po, w = yield from get(PS)
            for j in range(2):
                k = mm(po[:, 0:128], pT[:, j * 128:(j + 1) * 128], V0[:, 2 * b + j, :], j == 0, j == 1, w, v, dv)
            S2.give(pT, k)
            y = ts(O4[:, t, :], po[:, 0:128], st[:, 2:3], None, ALU.mult, None, k, r)
            PS.give(po, y)
            SS.give(st, y)
            out.append(y)

        def linear_attn(VQ, QG, CTX, CN, CR, GS, EK, O4, dv):
            q4 = VQ[:, :, 136:200].rearrange("p t (h d) -> p t h d", d=16)
            kk = VQ[:, :, 200:264]
            gs = GS.rearrange("p (t h) -> p t h", t=4)
            gb = gs.unsqueeze(3).to_broadcast([128, 4, 4, 16])
            a = red(gs, q4, ALU.max, dv)
            a = tt(q4, q4, gb, ALU.subtract, a)
            a = act(VQ[:, :, 136:200], VQ[:, :, 136:200], ACT.Exp, a)
            c = ts(EK, kk, 0.0, None, ALU.min, None, dv)
            c = act(EK, EK, ACT.Exp, c)
            yield
            a = red(gs, q4, ALU.add, a)
            a = rcp(gs, gs, a)
            a = tt(q4, q4, gb, ALU.mult, a)
            c = stt(kk, kk, 0.0, EK, ALU.max, ALU.add, c)
            yield
            ps, w = yield from get(PS)
            for j in range(4):
                k = tr(ps[0:64, j * 128:(j + 1) * 128], VQ[:, j, 136:200], w, a)
            dqg = evac(QG, ps[0:64, :], k)
            PS.give(ps, dqg)
            dctx = []
            for us in ((0, 2), (1,)):
                ps, w = yield from get(PS)
                nu = len(us)
                for bb in range(2):
                    for n, u in enumerate(us):
                        t, r, c_ = 2 * bb + u // 2, 64 * (u % 2), (nu * bb + n) * 65
                        k = mm(ps[0:64, c_:c_ + 65], VQ[r:r + 64, t, 200:264], VQ[r:r + 64, t, 68:133],
                               True, True, w, c)
                v = evac(CTX[:, :, us[0]:3:2, :],
                         ps[0:64, 0:130 * nu].rearrange("p (b u c) -> p b u c", b=2, c=65), k)
                PS.give(ps, v)
                dctx.append(v)
            yield
            c = dctx
            for u in (1, 2):
                c = tt(CTX[:, :, u, :], CTX[:, :, u, :], CTX[:, :, u - 1, :], ALU.add, c)
            c = ts(CR, CTX[:, :, :, 64], 1e-6, None, ALU.add, None, c)
            c = rcp(CR, CR, c)
            a = tt(CN, CTX[:, :, :, 0:64], CR.unsqueeze(3).to_broadcast([64, 2, 3, 64]), ALU.mult, c)
            CNf = CN.rearrange("p b u c -> p (b u) c")
            a = tt(CNf, CNf, wv("bm16")[0:64, :].unsqueeze(1).to_broadcast([64, 6, 64]), ALU.mult, a, d_co)
            yield
            ps, w = yield from get(PS)
            for bb in range(2):
                for u in range(1, 4):
                    j, r = 2 * bb + u // 2, 64 * (u % 2)
                    k = mm(ps[r:r + 64, j * 64:(j + 1) * 64],
                           QG[:, bb * 256 + u * 64:bb * 256 + (u + 1) * 64], CN[:, bb, u - 1, :], True, True,
                           w, a, dqg)
            p3 = ps[:, 0:256].rearrange("p (t c) -> p t c", c=64)
            o3 = O4[:, :, 64:128]
            pz = P.dve(lambda e: e.memset(o3[0:64, 0:4:2, :], 0.0))
            v1 = cp("act", o3[64:128, 0:4:2, :], p3[64:128, 0:4:2, :], k)
            v2 = cp("act", o3[:, 1:4:2, :], p3[:, 1:4:2, :], k)
            PS.give(ps, v2)
            return [pz, v1, v2]

        def group01(g, base):
            S = AR[:, base * SLOT:(base + 1) * SLOT]
            X = XG[g]

            def t3(o):
                return S[:, o:o + 512].rearrange("p (t c) -> p t c", c=128)

            XN, O4, Z, V0 = t3(0), t3(512), t3(1024), t3(1536)
            XT, QT, KT = S[:, 2048:2560], S[:, 2560:3072], S[:, 3072:3584]
            VQ = S[:, 3584:3584 + 4 * 264].rearrange("p (t c) -> p t c", c=264)
            QG = S[0:64, 4640:5152]
            CTX = S[0:64, 5152:5152 + 390].rearrange("p (b u c) -> p b u c", b=2, c=65)
            CN = S[0:64, 5542:5542 + 384].rearrange("p (b u c) -> p b u c", b=2, c=64)
            CR = S[0:64, 5926:5932].rearrange("p (b u) -> p b u", b=2)
            GS = S[:, 5936:5952]
            EK = S[:, 5952:6208].rearrange("p (t c) -> p t c", c=64)
            xT = yield from pre(X, XN, XT, d_x[g])
            yield
            dq = yield from proj_T(QT[0:32, :], wv("wq0"), XT, [xT, d_wa0], scale=float(32.0 ** -0.5))
            dk = yield from proj_T(KT[0:32, :], wv("wk0"), XT, [xT, d_wa0])
            dv = yield from proj_tok(WV, XT, [xT, dwv], to(V0))
            yield
            y = []
            yield from gpipe(l0_item(b, qt, QT[0:32, :], KT[0:32, :], V0, O4, dq, dk, dv, y)
                             for b in range(2) for qt in range(2))
            dx = yield from post(X, O4, y)
            yield
            xT = yield from pre(X, XN, XT, dx)
            yield
            y = yield from mlp(XT, xT, wgu[:, 0:384], None, 3, "silu",
                               wgu[:, 768:1152].rearrange("p (j c) -> p j c", c=128), to(O4), t_wi,
                               w1b=wgu[:, 384:768])
            dx = yield from post(X, O4, y)
            yield
            t1 = P.dve(lambda e: e.memset(VQ[:, :, 0:68].rearrange("p t (h d) -> p t h d", d=17)[:, :, :, 16:17], 1.0))
            t1 = [t1, P.dve(lambda e: e.memset(VQ[:, :, 132:133], 1.0))]
            dz = yield from norm(X, Z, dx)
            for i in range(4):
                def col(n):
                    return wv(n)[:, i:i + 1]
                n = yield from norm(Z, XN, dz)
                hT = yield from to_T(XN, XT, n, col("ln1g"), col("ln1b"))
                yield
                dq = yield from proj_T(QT, wv(f"l1q{i}"), XT, [hT, d_wa], scale=0.25)
                dk = yield from proj_T(KT, wv(f"l1k{i}"), XT, [hT, d_wa])
                dv = [t1]
                for g2 in range(2):
                    ps, w = yield from get(PS)
                    for j in range(2):
                        t = 2 * g2 + j
                        k = mm(ps[:, j * 256:(j + 1) * 256], XT[:, t * 128:(t + 1) * 128], wv(f"l1vqk{i}"),
                               True, True, w, hT, d_wa)
                    p2 = ps[:, :].rearrange("p (t c) -> p t c", c=256)
                    vq = VQ[:, 2 * g2:2 * g2 + 2, :]
                    a = cp("act", vq[:, :, 0:68].rearrange("p t (h d) -> p t h d", d=17)[:, :, :, 0:16],
                           p2[:, :, 0:64].rearrange("p t (h d) -> p t h d", d=16), k)
                    b_ = cp("act", vq[:, :, 68:132], p2[:, :, 64:128], k)
                    c = cp("act", vq[:, :, 136:264], p2[:, :, 128:256], k)
                    PS.give(ps, c)
                    dv += [a, b_, c]
                yield
                ka, kl = yield from par(
                    attn(QT, KT, lambda t, h: VQ[:, t, 17 * h:17 * h + 17], 4, 16, wv("hm16"), O4, [dq, dk, dv]),
                    linear_attn(VQ, QG, CTX, CN, CR, GS, EK, O4, dv))
                yield
                oT = yield from to_T(O4, XT, [ka, kl])
                dz = yield from proj_tok(wv(f"l1o{i}"), XT, [oT, d_wa],
                                         add_rep(Z, wv("bo")[:, i * 128:(i + 1) * 128]))
                yield
                n = yield from norm(Z, XN, dz)
                hT = yield from to_T(XN, XT, n, col("ln2g"), col("ln2b"))
                yield
                dz = yield from mlp(XT, hT, wv(f"l1w1{i}"), wv("b1")[:, 4 * i:4 * i + 4], 4, ACT.Gelu,
                                    wv(f"l1w2{i}").rearrange("p (j c) -> p j c", c=128),
                                    add_rep(Z, wv("b2")[:, i * 128:(i + 1) * 128]), d_wa)
            dxg[g] = yield from post(X, Z, dz)

        dxg = [None] * 8
        lent = [(AR[:, 6912:7424], []), (AR[:, 7424:7936], []), (AR[:, 15744:16256], []),
                (AR[:, 14592:15104], t_wi), (AR[:, 15104:15616], t_wi), (AR[:, 23936:24448], [])]
        lent += [(wCs[:, 512 * i:512 * i + 512], []) for i in range(9)]
        S2.lend(lent)
        flow(group01, range(8), range(3), STAG0)
        S2.back(lent)
        last = P.fence()

        phi = wAB[:, 0:2048]
        d_phi = dma(phi, wb[:, 0:2048], last)
        d_wc = dma(wCs[:, :], wc, last)
        XTA = AR[:, 0:4096]
        ZX = AR[:, 20480:24576].rearrange("p (t c) -> p t c", c=128)
        LR = Ring([AR[:, 4096 + 2048 * i:6144 + 2048 * i] for i in range(3)] + [wAB[:, 4096:6144]])
        DR = Ring([AR[:, 10240 + 2048 * i:12288 + 2048 * i] for i in range(2)] + [wAB[:, 6144:8192]])
        YA = AR[:, 14336:18432].rearrange("p (b m e) -> p b m e", b=16, m=2)
        SL = AR[:, 18432:20480].rearrange("p (b s) -> p b s", b=16)
        WR = Ring([wAB[:, 2048 + 512 * i:2560 + 512 * i] for i in range(4)])
        XN4 = ZX[:, :, :].rearrange("p (b m) d -> p b m d", m=2)
        xTh = [None] * 8

        def smoe_in(g, _):
            xTh[g] = yield from pre(XG[g], ZX[:, 4 * g:4 * g + 4, :], XTA[:, 512 * g:512 * g + 512], dxg[g])

        flow(smoe_in, range(8), range(4), 1)
        MR = MISC[:, 64:96].rearrange("p (m b) -> p m b", m=2)
        LS = MISC[:, 96:128].rearrange("p (m b) -> p m b", m=2)
        smoe = {"acc": None, "stat": [None, None]}

        def wload(q):
            b_, w = WR.take()
            return b_, dma(b_, wb[:, 2048 + 512 * q:2560 + 512 * q], w, last)

        wch = {q: wload(q) for q in range(3)}

        def half(q, mt):
            L, lw = yield from get(LR)
            L3 = L.rearrange("p (b s) -> p b s", b=16)
            ev = []
            for g in range(4):
                ps, w = yield from get(PS)
                for i in range(4):
                    t = 2 * (4 * g + i) + mt
                    k = mm(ps[:, i * 128:(i + 1) * 128], XTA[:, t * 128:(t + 1) * 128],
                           phi[:, q * 128:(q + 1) * 128], True, True, w, xTh[t // 4], d_phi)
                v = evac(L3[:, 4 * g:4 * g + 4, :], v4(ps), k, lw)
                PS.give(ps, v)
                ev.append(v)
                yield
            D, dw = yield from get(DR)
            D3 = D.rearrange("p (b s) -> p b s", b=16)
            Ds = D.rearrange("p (b s) -> p s b", b=16)
            tmp, tw = yield from get(S2)
            m1 = tmp[:, 0:128]
            mb = m1.unsqueeze(1).to_broadcast([128, 16, 128])
            a = red(m1, L.rearrange("p (b s) -> p s b", b=16), ALU.max, ev, tw)
            a0 = tt(D3, L3, mb, ALU.subtract, a, dw)
            x = act(D, D, ACT.Exp, a0)
            yield
            st, sw = yield from get(SS)
            tm, al, rs, nm = st[:, 0:16], st[:, 16:32], st[:, 32:48], st[:, 48:64]
            mr, ls = MR[:, mt, :], LS[:, mt, :]
            pst = smoe["stat"][mt]
            b1 = red(tm, L3, ALU.max, ev, sw)
            if q == 0:
                b2 = P.dve(lambda e: e.tensor_copy(mr, tm), b1)
                ax = None
            else:
                b2 = tt(tm, tm, mr, ALU.max, b1, pst)
                b3 = tt(al, mr, tm, ALU.subtract, b2)
                ax = P.act(lambda e: e.activation(al, al, ACT.Exp), b3)
                b2 = P.dve(lambda e: e.tensor_copy(mr, tm), b3)
            b4 = ts(nm, mr, -1.0, None, ALU.mult, None, b2)
            yield
            a = red(m1, Ds, ALU.add, x)
            a = P.dve(lambda e: e.reciprocal(m1, m1), a)
            a = P.pool(lambda e: e.tensor_tensor(D3, D3, mb, ALU.mult), a)
            S2.give(tmp, a)
            ex = None
            for b in range(16):
                ex = act(L3[:, b, :], L3[:, b, :], ACT.Exp, b4, a0, bias=nm[:, b:b + 1], acc=rs[:, b:b + 1])
                if b % 4 == 3:
                    yield
            if q == 0:
                c = P.dve(lambda e: e.tensor_copy(ls, rs), ex)
            else:
                c = tt(ls, ls, al, ALU.mult, ax, pst)
                c = tt(ls, ls, rs, ALU.add, c, ex)
            smoe["stat"][mt] = [c, b2]
            yield
            return (L, L3, st, al, [ex, ax], c), (D, D3, a)

        def unit(q):
            h0 = yield from half(q, 0)
            h1 = yield from half(q, 1)
            D3s = [h0[1][1], h1[1][1]]
            ad = [h0[1][2], h1[1][2]]
            sl = []
            for g in range(4):
                ps, w = yield from get(PS)
                for i in range(4):
                    b = 4 * g + i
                    for mt in range(2):
                        k = mm(ps[:, i * 128:(i + 1) * 128], XN4[:, b, mt, :], D3s[mt][:, b, :], mt == 0, mt == 1,
                               w, ad)
                v = evac(SL[:, 4 * g:4 * g + 4, :], v4(ps), k, smoe.get("slread"))
                PS.give(ps, v)
                sl.append(v)
                yield
            DR.give(h0[1][0], k)
            DR.give(h1[1][0], k)
            yt, yw = yield from get(S8)
            yt3 = yt.rearrange("p (b s) -> p b s", b=16)
            W, dW = wch[q]
            kk = []
            for i in range(4):
                ps, w = yield from get(PS)
                k = mm(ps[:, :].rearrange("p (b s) -> p b s", b=16), W[:, i * 128:(i + 1) * 128],
                       SL[:, :, i * 32:(i + 1) * 32], True, True, w, sl, dW)
                bb = wv("mb")[:, 4 * q + i:4 * q + i + 1]
                v = act(yt3[:, :, i * 32:(i + 1) * 32], ps[:, :].rearrange("p (b s) -> p b s", b=16),
                        ACT.Identity, k, yw, d_ve, bias=bb)
                PS.give(ps, v)
                kk.append(v)
                yield
            smoe["slread"] = k
            WR.give(W, k)
            if q + 3 < 16:
                wch[q + 3] = wload(q + 3)
            ym, mw = yield from get(S8)
            ym3 = ym.rearrange("p (b e) -> p b e", b=16)
            ky = []
            for g in range(4):
                pt, w = yield from get(PS)
                for i in range(4):
                    b = 4 * g + i
                    k = tr(pt[:, i * 128:(i + 1) * 128], yt3[:, b, :], w, kk)
                v = evac(ym3[:, 4 * g:4 * g + 4, :], v4(pt), k, mw)
                PS.give(pt, v)
                ky.append(v)
                yield
            S8.give(yt, k)

            def back(m_, g):
                L_, E3, st_, al_, kx, kc = (h0, h1)[m_][0]
                pt, w = yield from get(PS)
                for i in range(4):
                    k = tr(pt[:, i * 128:(i + 1) * 128], E3[:, 4 * g + i, :], w, kx)
                eT, ew = yield from get(S2)
                v = evac(eT, pt[:, :], k, ew)
                PS.give(pt, v)
                if g == 3:
                    LR.give(L_, k)
                yield
                yield
                po, w = yield from get(PS)
                for i in range(4):
                    b = 4 * g + i
                    k = mm(po[:, i * 128:(i + 1) * 128], eT[:, i * 128:(i + 1) * 128], ym3[:, b, :], True, True,
                           w, v, ky[g])
                S2.give(eT, k)
                smoe["yk"] = k
                for i in range(4):
                    b = 4 * g + i
                    pi = po[:, i * 128:(i + 1) * 128]
                    if q == 0:
                        v = P.dve(lambda e, b=b, pi=pi: e.tensor_copy(YA[:, b, m_, :], pi), k)
                    else:
                        v = stt(YA[:, b, m_, :], YA[:, b, m_, :], al_[:, b:b + 1], pi, ALU.mult, ALU.add,
                                k, kx, smoe.get(("ya", b, m_)))
                    smoe[("ya", b, m_)] = v
                PS.give(po, [smoe[("ya", 4 * g + i, m_)] for i in range(4)])
                if g == 3:
                    SS.give(st_, v, kc)

            yield from gpipe(back(m_, g) for m_ in range(2) for g in range(4))
            S8.give(ym, smoe["yk"])

        for _ in gpipe((unit(q) for q in range(16)), SLAG):
            pass
        rl = rcp(LS, LS, smoe["stat"])
        P.fence()

        def smoe_out(g, _):
            k = [ts(YA[:, t // 2, t % 2, :], YA[:, t // 2, t % 2, :], LS[:, t % 2, t // 2:t // 2 + 1], None,
                    ALU.mult, None, rl) for t in range(4 * g, 4 * g + 4)]
            yield
            dxg[g] = yield from post(XG[g], YA.rearrange("p b m e -> p (b m) e")[:, 4 * g:4 * g + 4, :], k)

        flow(smoe_out, range(8), range(4), 1)
        last = P.fence()

        EPS = float(np.finfo(np.float32).eps)
        d_wm = dma(wAB[:, 4096:4096 + NM], wm, last)
        kpar = []
        DTv, Av = MISC[:, 200:216], MISC[:, 216:232]
        DOUT, DREV = MISC[:, 232:248], MISC[:, 248:264]
        W2_, W3_, W4_, W5_ = (MISC[:, 264 + 16 * i:280 + 16 * i] for i in range(4))
        HORD = list(range(0, 16, 2)) + list(range(1, 16, 2))
        LM = wAB[:, 6144:8192].rearrange("p (h q) -> p h q", h=16)

        def decay():
            W1_ = wv("dt")
            a = ts(W2_, W1_, -1.0, None, ALU.mult, None, d_ve)
            a = tt(W2_, W2_, W1_, ALU.min, a)
            u = P.act(lambda e: e.activation(W2_, W2_, ACT.Exp), a)
            yield
            w1p = ts(W3_, W2_, 1.0, None, ALU.add, None, u)
            ln = P.act(lambda e: e.activation(W4_, W3_, ACT.Ln), w1p)
            yield
            d1 = ts(W3_, W3_, -1.0, None, ALU.add, None, ln)
            eq = ts(W5_, W3_, 0.0, None, ALU.is_equal, None, d1)
            a = tt(W3_, W3_, W5_, ALU.add, eq)
            a = P.dve(lambda e: e.reciprocal(W3_, W3_), a)
            yield
            a = tt(W3_, W3_, W2_, ALU.mult, a)
            a = tt(W4_, W4_, W3_, ALU.mult, a)
            a2 = tt(W5_, W5_, W2_, ALU.mult, a)
            a = tt(W4_, W4_, W5_, ALU.add, a, a2)
            a = P.dve(lambda e: e.scalar_tensor_tensor(DTv, W1_, 0.0, W4_, ALU.max, ALU.add), a)
            yield
            ea = P.act(lambda e: e.activation(Av, wv("al"), ACT.Exp), d_ve)
            da = P.dve(lambda e: e.scalar_tensor_tensor(Av, Av, -1.0, DTv, ALU.mult, ALU.mult), ea, a)
            kl = []
            for n, h in enumerate(HORD):
                k = P.act(lambda e, n=n, h=h: e.activation(LM[:, n, :], wv("dif"), ACT.Exp, scale=Av[:, h:h + 1]),
                          da, d_co)
                kl.append(tt(LM[:, n, :], LM[:, n, :], wv("tri"), ALU.mult, k))
                yield
            a = ts(W2_, Av, wv("qp1"), None, ALU.mult, None, da)
            k1 = P.act(lambda e: e.activation(DOUT, W2_, ACT.Exp), a)
            a = ts(W3_, Av, wv("rev"), None, ALU.mult, None, da)
            k2 = P.act(lambda e: e.activation(DREV, W3_, ACT.Exp), a)
            k2 = tt(DREV, DREV, DTv, ALU.mult, k2)
            kpar.extend([k1, k2, *kl])


        def mix(dst, a_, ra, b_, rb, *deps):
            tmp, w = yield from get(S2)
            k1 = tt(v4(tmp), b_, rep4(rb), ALU.mult, w, d_ve, *deps)
            k2 = tt(dst, a_, rep4(ra), ALU.mult, d_ve, *deps)
            k3 = tt(dst, dst, v4(tmp), ALU.add, k1, k2)
            S2.give(tmp, k3)
            return k3

        def bc16(x):
            return x.unsqueeze(2).to_broadcast([128, 16, 16])

        def scan_tile(t, odd, VT, GT, BT, CT, HS, kb, dval, dgat, st_, Z, out):
            sl = slice(odd * 128, odd * 128 + 128)
            gl = slice(t * 128, (t + 1) * 128)
            ps, w = yield from get(PS)
            xv, xw = yield from get(S2)
            for c in range(2):
                k = tr(ps[:, c * 128:(c + 1) * 128], VT[:, c, gl], w, dval)
            vt3 = ps[:, 0:256].rearrange("p (h d) -> p h d", d=16)
            kx1 = tt(xv[:, 0:256].rearrange("p (h d) -> p h d", d=16), vt3, bc16(DTv), ALU.mult, k, xw, kpar)
            kx2 = kx1
            if not odd:
                kx2 = tt(xv[:, 256:512].rearrange("p (h d) -> p h d", d=16), vt3, bc16(DREV), ALU.mult, k, xw, kpar)
            PS.give(ps, kx1, kx2)
            yield
            py, yw = yield from get(PS)
            ys, ysw = yield from get(S2)
            kst = None
            for c in range(4):
                pc, w = yield from get(PS)
                cb, cw_ = yield from get(S2)
                for i in range(4):
                    h = HORD[4 * c + i]
                    r = 64 * (h % 2)
                    k = mm(pc[:, i * 128:(i + 1) * 128], BT[r:r + 64, h // 2, sl], CT[r:r + 64, h // 2, sl],
                           True, True, w, kb)
                v = tt(cb, pc[:, :], LM[:, 4 * c:4 * c + 4, :].rearrange("p h q -> p (h q)"), ALU.mult, k, cw_, kpar)
                PS.give(pc, v)
                yield
                for i in range(4):
                    h = HORD[4 * c + i]
                    kyy = mm(py[:, h * 16:(h + 1) * 16], cb[:, i * 128:(i + 1) * 128],
                             xv[:, h * 16:(h + 1) * 16], True, True, yw, v, kx1)
                S2.give(cb, kyy)
            if odd:
                while st_["hk"] is None:
                    yield
                po, pw = yield from get(PS)
                for jj in range(8):
                    ko = mm(po[:, jj * 32:(jj + 1) * 32], CT[:, jj, sl], HS[:, jj, :], True, True, pw, kb,
                            st_["hk"])
                a = tt(ys[:, 0:256].rearrange("p (h d) -> p h d", d=16),
                       po[:, 0:256].rearrange("p (h d) -> p h d", d=16), bc16(DOUT), ALU.mult, ko, ysw, kpar)
                PS.give(po, a)
                a = tt(ys[:, 0:256], ys[:, 0:256], py[:, 0:256], ALU.add, a, kyy)
                st_["end"] = [ko, kyy]
            else:
                a = evac(ys[:, 0:256], py[:, 0:256], kyy, ysw)
                bt = []
                for c in range(2):
                    ps, w = yield from get(PS)
                    bb, bw = yield from get(S2)
                    for i in range(4):
                        k = tr(ps[:, i * 128:(i + 1) * 128], BT[:, 4 * c + i, sl], w, kb)
                    v = evac(bb, ps[:, :], k, bw)
                    PS.give(ps, v)
                    bt.append((bb, v))
                yield
                ps, w = yield from get(PS)
                for jj in range(8):
                    bb, v = bt[jj // 4]
                    kst = mm(ps[:, jj * 32:(jj + 1) * 32], bb[:, (jj % 4) * 128:(jj % 4 + 1) * 128],
                             xv[:, 256 + jj * 32:256 + (jj + 1) * 32], True, True, w, v, kx2)
                for bb, v in bt:
                    S2.give(bb, kst)
                st_["hk"] = tt(HS, ps[:, 0:256].rearrange("p (j c) -> p j c", j=8),
                               wv("bm64").unsqueeze(1).to_broadcast([128, 8, 32]), ALU.mult, kst, st_["hw"], d_co)
                PS.give(ps, st_["hk"])
            PS.give(py, a)
            S2.give(xv, kyy, kst)
            yield
            ps, w = yield from get(PS)
            yt, ytw = yield from get(S2)
            for c in range(2):
                k = tr(ps[:, c * 128:(c + 1) * 128], ys[:, c * 128:(c + 1) * 128], w, a)
            S2.give(ys, k)
            ks = []
            for c in range(2):
                v = stt(yt[:, c * 128:(c + 1) * 128], VT[:, c, gl], wv("dpar")[:, c:c + 1],
                        ps[:, c * 128:(c + 1) * 128], ALU.mult, ALU.add, k, ytw)
                ks.append(tt(yt[:, c * 128:(c + 1) * 128], yt[:, c * 128:(c + 1) * 128], GT[:, c, gl],
                             ALU.mult, v, dgat))
            PS.give(ps, ks)
            yield
            ps, w = yield from get(PS)
            for c in range(2):
                k = mm(ps[:, 0:128], yt[:, c * 128:(c + 1) * 128], wv("outp")[:, c * 128:(c + 1) * 128],
                       c == 0, c == 1, w, ks)
            S2.give(yt, k)
            tmp, tw = yield from get(S2)
            a = tt(tmp[:, 0:128], ps[:, 0:128], wv("msc"), ALU.mult, k, tw)
            PS.give(ps, a)
            a = tt(Z[:, t, :], Z[:, t, :], tmp[:, 0:128], ALU.add, a)
            S2.give(tmp, a)
            out.append(a)

        def group23(g, base):
            S = AR[:, base * SLOT:(base + 1) * SLOT]
            X = XG[g]

            def t3(o):
                return S[:, o:o + 512].rearrange("p (t c) -> p t c", c=128)

            XN, O4, Z = t3(0), t3(512), t3(1024)
            XT = S[:, 1536:2048]
            NTm = S[:, 512:1024]
            VT = S[:, 2048:3072].rearrange("p (c n) -> p c n", c=2)
            GT = S[:, 3072:4096].rearrange("p (c n) -> p c n", c=2)
            BT = S[:, 4096:6144].rearrange("p (h n) -> p h n", h=8)
            CT = S[:, 6144:8192].rearrange("p (h n) -> p h n", h=8)
            RAW = S[:, 4096:5120].rearrange("p (c n) -> p c n", c=2)
            YN = t3(7680)
            QT, KT = S[:, 4096:4608], S[:, 4608:5120]
            V9 = S[:, 5120:5696].rearrange("p (t h d) -> p t h d", t=4, d=9)
            QK = S[:, 5696:5696 + 640].rearrange("p (t c) -> p t c", c=160)
            KR = S[:, 6848:7360].rearrange("p (t c) -> p t c", c=128)
            xT = yield from pre(X, XN, XT, dxg[g])
            yield
            sc8 = float(np.float32(8.0 ** -0.25))
            t1 = P.dve(lambda e: e.memset(V9[:, :, :, 8:9], 1.0))
            dq = yield from proj_T(QT, wv("l2q"), XT, [xT, d_wc], scale=sc8)
            dk = yield from proj_T(KT, wv("l2k"), XT, [xT, d_wc], scale=sc8)

            def fin_v(ps, k):
                p4 = v4(ps).rearrange("p t (h d) -> p t h d", d=8)
                return [cp("act", V9[:, t, :, 0:8], p4[:, t, :, :], k) for t in range(4)]

            dv = yield from proj_tok(wv("l2v"), XT, [xT, d_wc], fin_v)
            yield
            ka = yield from attn(QT, KT, lambda t, h: V9[:, t, h, :], 16, 8, wv("hm8"), O4, [dq, dk, dv, t1])
            yield
            oT = yield from to_T(O4, XT, ka)
            yield
            y = yield from proj_tok(wv("l2o"), XT, [oT, d_wc], to(O4))
            yield
            dx = yield from post(X, O4, y)
            xT = yield from pre(X, XN, XT, dx)
            yield
            y = yield from mlp(XT, xT, wv("l2w1"), wv("l2b1"), 4, ACT.Gelu,
                               wv("l2w2").rearrange("p (j c) -> p j c", c=128),
                               lambda ps, k: tt(O4, v4(ps), rep4(wv("l2b2")), ALU.add, k, d_ve), d_wc)
            dx = yield from post(X, O4, y)
            yield
            dn = yield from norm(X, XN, dx)
            dz = yield from mix(Z, XN, wv("rm0"), XN, wv("rm1"), dn)
            yield
            dxm = yield from to_T(Z, XT, dz)
            nn = yield from norm(Z, YN, dz, rms=True, eps=EPS)
            dnT = yield from to_T(YN, NTm, nn)
            yield
            dval, dgat = [], []
            for c in range(2):
                dr = yield from proj_T(RAW[:, c, :], wv("inp")[:, c * 128:(c + 1) * 128], NTm, [dnT, d_wc])
                cw = wv("convw")[:, 4 * c:4 * c + 4]
                cb = wv("convb")[:, c:c + 1]
                r0 = RAW[:, c, :].rearrange("p (b n) -> p b n", n=256)
                o0 = VT[:, c, :].rearrange("p (b n) -> p b n", n=256)
                k = ts(VT[:, c, :], RAW[:, c, :], cw[:, 3:4], cb, ALU.mult, ALU.add, dr, d_ve)
                for s in (1, 2, 3):
                    k = stt(o0[:, :, s:256], r0[:, :, 0:256 - s], cw[:, 3 - s:4 - s], o0[:, :, s:256],
                            ALU.mult, ALU.add, k)
                dval.append([k, act(VT[:, c, :], VT[:, c, :], ACT.Silu, k)])
                yield
            for c in range(2):
                ps, w = yield from get(PS)
                k = mm(ps[:, :], wv("inp")[:, 256 + c * 128:256 + (c + 1) * 128], NTm, True, True, w, dnT, d_wc)
                v = act(GT[:, c, :], ps[:, :], ACT.Silu, k)
                PS.give(ps, v)
                dgat.append(v)
            yield
            H2, hw2 = yield from get(S2)
            HS = H2[:, 0:256].rearrange("p (j c) -> p j c", j=8)
            st_ = {"hw": [hw2], "end": None, "hk": None}
            dy = []
            for b in range(2):
                kb = []
                for h in range(0, 8, 2):
                    for dst, nme in ((BT, "bp"), (CT, "cp")):
                        ps, w = yield from get(PS)
                        for i in range(2):
                            k = mm(ps[:, i * 256:(i + 1) * 256], wv(nme)[:, (h + i) * 128:(h + i + 1) * 128],
                                   XT[:, b * 256:(b + 1) * 256], True, True, w, dxm, d_wc)
                        v = evac(dst[:, h:h + 2, :], ps[:, :].rearrange("p (h n) -> p h n", h=2), k,
                                 st_["end"], dval, dnT)
                        PS.give(ps, v)
                        kb.append(v)
                    yield
                yield from gpipe((scan_tile(2 * b + j, j, VT, GT, BT, CT, HS, kb, dval, dgat, st_, Z, dy)
                                  for j in range(2)), lag=SCLAG)
                st_["hw"], st_["hk"] = [st_["end"]], None
            S2.give(H2, st_["end"])
            def relu_mlp(dz, fc, pj, sc):
                nn = yield from norm(Z, YN, dz, rms=True, eps=EPS)
                nT = yield from to_T(YN, XT, nn)
                yield
                return (yield from mlp(XT, nT, wv(fc), None, 4, "relu2", wv(pj).rearrange("p (j c) -> p j c", c=128),
                                       add_scaled(Z, wv(sc)), d_wm))

            dz = yield from relu_mlp([dy, st_["end"]], "mfc", "mpj", "mmsc")
            dza = yield from mix(Z, Z, wv("ra0"), XN, wv("ra1"), dz)
            yield
            nn = yield from norm(Z, YN, dza, rms=True, eps=EPS)
            nT = yield from to_T(YN, XT, nn)
            yield
            dqk = []
            t2 = P.dve(lambda e: e.memset(V9[:, :, 0:4, 8:9], 1.0), nT)
            for g2 in range(2):
                ps, w = yield from get(PS)
                for j in range(2):
                    t = 2 * g2 + j
                    k = mm(ps[:, j * 192:(j + 1) * 192], XT[:, t * 128:(t + 1) * 128], wv("qkv"), True, True,
                           w, nT, d_wc)
                p3 = ps[:, 0:384].rearrange("p (t c) -> p t c", c=192)
                v = cp("act", QK[:, 2 * g2:2 * g2 + 2, :], p3[:, :, 0:160], k)
                v2 = cp("act", V9[:, 2 * g2:2 * g2 + 2, 0:4, 0:8],
                        p3[:, :, 160:192].rearrange("p t (h d) -> p t h d", d=8), k)
                PS.give(ps, v2)
                dqk += [v, v2]
            yield
            dqr = []
            rb, rw = yield from get(S2)
            sq, sw = yield from get(S2)
            a = []
            for t in range(4):
                b_ = sq[:, 160 * (t % 2):160 * (t % 2) + 160]
                x = tt(b_, QK[:, t, :], QK[:, t, :], ALU.mult, dqk, sw, a[-2:-1])
                a.append(red(rb[:, 20 * t:20 * t + 20], b_.rearrange("p (h d) -> p h d", d=8), ALU.add, x, rw))
            S2.give(sq, a)
            x = ts(rb[:, 0:80], rb[:, 0:80], 0.125, EPS, ALU.mult, ALU.add, a)
            x = act(rb[:, 0:80], rb[:, 0:80], ACT.Sqrt, x)
            yield
            x = rcp(rb[:, 0:80], rb[:, 0:80], x)
            r4 = rb[:, 0:80].rearrange("p (t c) -> p t c", c=20)
            x = stt(r4[:, :, 0:16], r4[:, :, 0:16], float(np.float32(8.0 ** -0.5)),
                    wv("qg").unsqueeze(1).to_broadcast([128, 4, 16]), ALU.mult, ALU.mult, x, d_ve)
            x = tt(QK.rearrange("p t (h d) -> p (t h) d", d=8), QK.rearrange("p t (h d) -> p (t h) d", d=8),
                   rb[:, 0:80].unsqueeze(2).to_broadcast([128, 80, 8]), ALU.mult, x)
            S2.give(rb, x)
            yield
            for t in range(4):
                j = t % 2
                s2, sw = yield from get(S2)
                q3 = QK[:, t, :].rearrange("p (h d) -> p h d", d=8)
                cos = wv("cos")[:, 4 * j:4 * j + 4].unsqueeze(1).to_broadcast([128, 20, 4])
                sin = wv("sin")[:, 4 * j:4 * j + 4].unsqueeze(1).to_broadcast([128, 20, 4])
                xa, xb = q3[:, :, 0:4], q3[:, :, 4:8]
                r3 = s2[:, 0:160].rearrange("p (h d) -> p h d", d=8)
                u3 = s2[:, 160:320].rearrange("p (h d) -> p h d", d=8)
                e1 = tt(r3[:, :, 0:4], xa, cos, ALU.mult, x, sw, d_co)
                e2 = tt(u3[:, :, 0:4], xb, sin, ALU.mult, x)
                e3 = tt(r3[:, :, 4:8], xb, cos, ALU.mult, x)
                e4 = tt(u3[:, :, 4:8], xa, sin, ALU.mult, x)
                o1 = tt(xa, r3[:, :, 0:4], u3[:, :, 0:4], ALU.add, e1, e2, e4)
                o2 = tt(xb, r3[:, :, 4:8], u3[:, :, 4:8], ALU.subtract, e3, e4, e2)
                S2.give(s2, o1, o2)
                kr4 = KR[:, t, :].rearrange("p (g r d) -> p g r d", g=4, d=8)
                k3_ = QK[:, t, 128:160].rearrange("p (g d) -> p g d", d=8)
                dqr += [o1, o2, P.dve(lambda e, kr4=kr4, k3_=k3_: e.tensor_copy(
                    kr4, k3_.unsqueeze(2).to_broadcast([128, 4, 4, 8])), o1, o2)]
                yield
            dq = yield from to_T(QK[:, :, 0:128], QT, dqr)
            dk = yield from to_T(KR, KT, dqr)
            yield
            ka = yield from attn(QT, KT, lambda t, h: V9[:, t, h // 4, :], 16, 8, wv("hm8"), O4, [dq, dk, dqk, t2])
            yield
            oT = yield from to_T(O4, XT, ka)
            yield
            dz = yield from proj_tok(wv("ow"), XT, [oT, d_wc], add_scaled(Z, wv("asc")))
            yield
            dz = yield from relu_mlp(dz, "afc", "apj", "amsc")
            dxg[g] = yield from post(X, Z, dz)

        lent = [(wAB[:, 512 * i:512 * i + 512], []) for i in range(8)]
        S2.lend(lent)
        def first(g, base):
            yield from par(group23(g, base), decay())

        flow(lambda g, base: (first if g == 0 else group23)(g, base), range(8), range(3), STAG1)
        S2.back(lent)
        last = P.fence()

        OA = ZX
        YS = AR[:, 0:8192].rearrange("p (e q d) -> p e q d", e=8, q=8)
        XS = wAB[:, 0:8192].rearrange("p (e b s) -> p e b s", e=8, b=16)
        d_we = [dma(AR[:, 8192 + 1024 * e:9216 + 1024 * e], wd[:, 1024 * e:1024 * (e + 1)], last) for e in range(8)]
        flow(smoe_in, range(8), range(4), 1)
        GM = AR[:, 16384:16640].rearrange("p (m c) -> p m c", m=2)
        ps, w = PS.take()
        for t in range(32):
            k = mm(ps[:, t * 8:(t + 1) * 8], XTA[:, t * 128:(t + 1) * 128], wv("gate"), True, True, w, xTh[t // 4], d_ve)
        PRB = AR[:, 16640:16896]
        PR2 = AR[:, 16896:17152]
        st = AR[:, 17152:17216]
        p3 = ps[:, 0:256].rearrange("p (t e) -> p t e", e=8)
        s3 = PRB.rearrange("p (t e) -> p t e", e=8)
        a = P.dve(lambda e: e.tensor_reduce(st[:, 0:32], p3, X_AX, ALU.max), k)
        a = tt(s3, p3, st[:, 0:32].unsqueeze(2).to_broadcast([128, 32, 8]), ALU.subtract, a)
        PS.give(ps, a)
        a = P.act(lambda e: e.activation(PRB, PRB, ACT.Exp), a)
        a = P.dve(lambda e: e.tensor_reduce(st[:, 32:64], s3, X_AX, ALU.add), a)
        a = P.dve(lambda e: e.reciprocal(st[:, 32:64], st[:, 32:64]), a)
        kp = tt(PR2.rearrange("p (m b e) -> p b m e", m=2, b=16), PRB.rearrange("p (b m e) -> p b m e", m=2, b=16),
                st[:, 32:64].rearrange("p (b m) -> p b m", m=2).unsqueeze(3).to_broadcast([128, 16, 2, 8]),
                ALU.mult, a)
        ps, w = PS.take()
        for m_ in range(2):
            k = tr(ps[:, m_ * 128:(m_ + 1) * 128], PR2[:, m_ * 128:(m_ + 1) * 128], w, kp)
        pp, wk = AR[:, 17216:17472], AR[:, 17472:17728]
        m8 = AR[:, 17728:17736]
        v1 = P.dve(lambda e, s_=ps[:, 0:256]: e.tensor_copy(pp, s_), k)
        a = v2 = P.dve(lambda e, s_=ps[:, 0:256]: e.tensor_copy(wk, s_), k)
        PS.give(ps, v1, v2)
        for r in range(8):
            a = P.dve(lambda e: e.max(m8, wk), a)
            a = P.dve(lambda e: e.match_replace(wk, m8, wk, -1.0), a)
        sel = AR[:, 18304:18560]
        SEL = AR[:, 18560:18816].rearrange("p (m c) -> p m c", m=2)
        RK = AR[:, 18816:19072].rearrange("p (m c) -> p m c", m=2)
        ones = AR[:, 19072:19200]
        on = P.dve(lambda e: e.memset(ones, 1.0))
        a1 = ts(sel, wk, 0.0, None, ALU.is_lt, None, a)
        a = tt(wk, sel, pp, ALU.mult, a1, v1)
        ps, w = PS.take()
        for m_ in range(2):
            k = tr(ps[:, m_ * 128:(m_ + 1) * 128], sel[:, m_ * 128:(m_ + 1) * 128], w, a1)
        ks = P.dve(lambda e, ps=ps: e.tensor_copy(SEL, ps[:, 0:256].rearrange("p (m c) -> p m c", m=2)), k)
        PS.give(ps, ks)
        ps, w = PS.take()
        mm(ps[:, 0:128], wv("tri"), SEL[:, 0, :], True, True, w, ks, d_co)
        mm(ps[:, 128:256], wv("tri"), SEL[:, 1, :], True, False)
        k = mm(ps[:, 128:256], ones, SEL[:, 0, :], False, True, on)
        krk = tt(RK, ps[:, 0:256].rearrange("p (m c) -> p m c", m=2), SEL, ALU.mult, k, ks)
        PS.give(ps, krk)
        ps, w = PS.take()
        for m_ in range(2):
            k = tr(ps[:, m_ * 128:(m_ + 1) * 128], wk[:, m_ * 128:(m_ + 1) * 128], w, a)
        kg = P.dve(lambda e, ps=ps: e.tensor_copy(GM, ps[:, 0:256].rearrange("p (m c) -> p m c", m=2)), k)
        PS.give(ps, kg)
        iota = wv("iota")
        dg = []

        def gather(b, _):
            ps, w = yield from get(PS)
            for m in range(2):
                oh, ow = yield from get(S2)
                a = tt(oh.rearrange("p (e s) -> p e s", s=64), iota.unsqueeze(1).to_broadcast([128, 8, 64]),
                       RK[:, m, 8 * b:8 * b + 8].unsqueeze(2).to_broadcast([128, 8, 64]), ALU.is_equal, ow, krk,
                       d_co)
                yield
                k = mm(ps[:, :], ZX[:, 2 * b + m, :], oh, m == 0, m == 1, w, a, xTh)
                S2.give(oh, k)
            v = evac(XS[:, :, b, :], ps[:, :].rearrange("p (e s) -> p e s", s=64), k)
            PS.give(ps, v)
            dg.append(v)

        flow(gather, range(16), range(3), 1)
        dy = []

        def expert(it, _):
            ex, hf = it
            we = AR[:, 8192 + 1024 * ex:9216 + 1024 * ex]

            def fin(ps, k):
                return evac(YS[:, ex, 4 * hf:4 * hf + 4, :], v4(ps), k)

            o = 1024 * ex + 512 * hf
            dy.append((yield from mlp(wAB[:, o:o + 512], dg, we[:, 0:512], None, 4, ACT.Gelu_apprx_tanh,
                                      we[:, 512:1024].rearrange("p (j c) -> p j c", c=128), fin, d_we[ex])))

        flow(expert, [(ex, hf) for ex in range(8) for hf in range(2)], range(2), 2)
        dyp = []

        def scatter(q, _):
            ot, otw = yield from get(S8)
            o4 = ot.rearrange("p (e m t) -> p e m t", e=8, m=2)
            ko = []
            for m in range(2):
                for eh in range(2):
                    og, ow = yield from get(S2)
                    g4 = og.rearrange("p (e b s) -> p e b s", e=4, b=2)
                    a = []
                    for e_ in range(4):
                        for b2 in range(2):
                            c = 8 * (2 * q + b2) + 4 * eh + e_
                            a.append(ts(g4[:, e_, b2, :], iota, RK[:, m, c:c + 1], GM[:, m, c:c + 1], ALU.is_equal,
                                        ALU.mult, ow, krk, kg, d_co))
                    yield
                    ps, w = yield from get(PS)
                    for e_ in range(4):
                        k = tr(ps[:, e_ * 128:(e_ + 1) * 128], og[:, e_ * 128:(e_ + 1) * 128], w, a)
                    S2.give(og, k)
                    v = cp("act", o4[:, 4 * eh:4 * eh + 4, m, :], v4(ps), k, otw)
                    PS.give(ps, v)
                    ko.append(v)
                    yield
            for b2 in range(2):
                ps, w = yield from get(PS)
                r = slice(64 * b2, 64 * b2 + 64)
                for m in range(2):
                    for ex in range(8):
                        k = mm(ps[:, m * 128:(m + 1) * 128], o4[r, ex, m, :], YS[r, ex, q, :], ex == 0, ex == 7,
                               w, ko, dy)
                t = 2 * (2 * q + b2)
                v = cp("act", OA[:, t:t + 2, :], ps[:, 0:256].rearrange("p (m c) -> p m c", m=2), k, dg)
                PS.give(ps, v)
                dyp.append(v)
                yield
            S8.give(ot, k)

        flow(scatter, range(8), range(2), 3)
        d_outs = []
        YB = AR[:, 0:2048].bitcast(BF16).rearrange("p (t c) -> p t c", c=128)
        SB = AR[:, 19648:19712].bitcast(BF16)
        SF = AR[:, 19200:19584]
        P.fence()
        kf = [P.dve(lambda e, g=g: e.tensor_copy(YB[:, 4 * g:4 * g + 4, :], OA[:, 4 * g:4 * g + 4, :]), dyp)
              for g in range(8)]
        ag = []
        for t in range(32):
            a = P.dve(lambda e, t=t: e.bn_stats(SF[:, 6 * t:6 * t + 6], YB[:, t, :]), kf[t // 4])
            ag.append(P.dve(lambda e, t=t: e.bn_aggr(SF[:, 192 + 2 * t:194 + 2 * t], SF[:, 6 * t:6 * t + 6]), a))
        mv = SF[:, 192:256].rearrange("p (t c) -> p t c", c=2)
        mb_, vb_, eb_, sb_ = SB[:, 0:32], SB[:, 32:64], SB[:, 64:96], SB[:, 96:128]
        a1 = P.dve(lambda e: e.tensor_copy(mb_, mv[:, :, 0]), ag)
        a2 = P.dve(lambda e: e.tensor_copy(vb_, mv[:, :, 1]), ag)
        a3_ = ts(eb_, vb_, EPSB, None, ALU.add, None, a2)
        s_ = P.act(lambda e: e.activation(sb_, eb_, ACT.Sqrt), a3_)
        rr = P.dve(lambda e: e.reciprocal(SF[:, 256:288], sb_), s_)
        mf = P.dve(lambda e: e.tensor_copy(SF[:, 288:320], mb_), a1)
        orows = out.rearrange("b (t p) d -> p (b t) d", p=128)
        outs = []
        for t in range(32):
            a = ts(YB[:, t, :], YB[:, t, :], SF[:, 288 + t:289 + t], None, ALU.subtract, None, mf)
            a = ts(YB[:, t, :], YB[:, t, :], SF[:, 256 + t:257 + t], None, ALU.mult, None, a, rr)
            outs.append(tt(XA[:, t, :], XA[:, t, :], YB[:, t, :], ALU.add, a))
            if t % 8 == 7:
                d_out = dma(orows[:, t - 7:t + 1, :], XA[:, t - 7:t + 1, :], outs[t - 7:t + 1])
                d_outs.append(d_out)
        for d_out in d_outs:
            P.op("sp", lambda e: None, d_out)

        used = {e: set() for e in P.q}
        for e in P.q:
            for deps, _ in P.q[e]:
                for d in deps:
                    if isinstance(d, Tok):
                        used[d.eng].add(d.idx)
        STEP = 4000
        where = {}
        for e in P.q:
            n = 0
            for idx in sorted(used[e]):
                where[(e, idx)] = (n // STEP, n % STEP + 1)
                n += 1
        esem = {}
        for e in P.q:
            if used[e]:
                for c in range((len(used[e]) + STEP - 1) // STEP):
                    esem[(e, c)] = ctx.enter_context(nc.semaphore(f"s_{e}{c}"))

        def stream(name, eng):
            seen = {}
            seen_dma = set()
            for idx, (deps, fn) in enumerate(P.q[name]):
                need = {}
                for d in deps:
                    if isinstance(d, DmaTok):
                        if id(d) not in seen_dma:
                            seen_dma.add(id(d))
                            eng.wait_ge(d.sem, d.val)
                    else:
                        if d.eng == name == "pe":
                            continue
                        need[d.eng] = max(need.get(d.eng, (-1, 0)), where[(d.eng, d.idx)])
                for p, at in need.items():
                    if seen.get(p, (-1, 0)) < at:
                        seen[p] = at
                        eng.wait_ge(esem[(p, at[0])], at[1])
                ins = fn(eng)
                if idx in used[name] and ins is not None:
                    ins.then_inc(esem[(name, where[(name, idx)][0])], 1)

        block = ctx.enter_context(nc.Block())

        @block.sync
        def _(eng):
            stream("sp", eng)

        @block.gpsimd
        def _(eng):
            stream("pool", eng)

        @block.scalar
        def _(eng):
            stream("act", eng)

        @block.tensor
        def _(eng):
            stream("pe", eng)

        @block.vector
        def _(eng):
            stream("dve", eng)


def shape_constants():
    c = np.zeros((128, NCO), np.float32)
    i = np.arange(128)

    def put(name, v):
        o, n = CO[name]
        c[:v.shape[0], o:o + n] = v

    put("ident", np.eye(128, dtype=np.float32))
    put("cmask", np.where(i[None, :] > i[:, None], np.float32(NEG), np.float32(0)))
    put("dif", np.maximum(i[None, :] - i[:, None], 0).astype(np.float32))
    put("tri", (i[None, :] >= i[:, None]).astype(np.float32))
    put("qp1", (i[:, None] + 1).astype(np.float32))
    put("rev", (127 - i[:, None]).astype(np.float32))
    inv = (np.float32(1.0) / np.power(np.float32(10000.0), np.arange(0, 8, 2, dtype=np.float32) / np.float32(8)))
    f = np.outer(np.arange(256, dtype=np.float32), inv.astype(np.float32)).astype(np.float32)
    put("cos", np.cos(f).astype(np.float32).reshape(2, 128, 4).transpose(1, 0, 2).reshape(128, 8))
    put("sin", np.sin(f).astype(np.float32).reshape(2, 128, 4).transpose(1, 0, 2).reshape(128, 8))
    put("iota", np.tile(np.arange(1, 65, dtype=np.float32), (128, 1)))
    put("hm8", (i[:, None] // 8 == np.arange(16)[None, :]).astype(np.float32))
    put("hm16", (i[:, None] // 16 == np.arange(4)[None, :]).astype(np.float32))
    put("bm64", (i[:, None] // 64 == np.arange(32)[None, :] // 16).astype(np.float32))
    put("bm16", (np.arange(64)[:, None] // 16 == np.arange(64)[None, :] // 16).astype(np.float32))
    return c


def step_constant():
    s, i = np.arange(384), np.arange(128)
    return (s[None, :] - 128 <= i[:, None]).astype(np.float32)


def kernel(**inputs):
    import numpy as _np
    import concourse.bacc as _bacc
    from concourse import mybir as _mybir
    from concourse.bass_utils import run_bass_kernel_spmd as _run

    I = {k: _np.asarray(v) for k, v in inputs.items()}

    def pack(tab, n, parts, dt=_np.float32):
        a = _np.zeros((128, n), dt)
        for name, v in parts.items():
            o, w = tab[name]
            assert v.shape[1] == w, (name, v.shape, w)
            a[:v.shape[0], o:o + w] = v
        return a

    def ktiles(w):
        k = w.shape[0] // 128
        return w.reshape(k, 128, -1).transpose(1, 0, 2).reshape(128, -1)

    def rep(v):
        v = v.reshape(1, -1)
        return _np.broadcast_to(v, (128, v.shape[1]))

    pa = {"wq0": I["L0_attn_Wq"], "wk0": I["L0_attn_Wk"], "wvd": I["L0_attn_Wvdown"].T, "wvu": I["L0_attn_Wvup"]}
    for i in range(4):
        q, k, v = I["L1_attn_Wq"][i], I["L1_attn_Wk"][i], I["L1_attn_Wv"][i]
        pa[f"l1q{i}"], pa[f"l1k{i}"] = q, k
        pa[f"l1vqk{i}"] = _np.concatenate([v, q[:, 64:], k[:, 64:]], axis=1)
        pa[f"l1o{i}"] = I["L1_attn_Wo"][i]
        pa[f"l1w1{i}"] = I["L1_attn_W1"][i]
        pa[f"l1w2{i}"] = ktiles(I["L1_attn_W2"][i])
    pb = {"phi": I["L1_ffn_phi"].reshape(128, 2048), "W": I["L1_ffn_W"].transpose(1, 0, 2).reshape(128, 8192)}
    pa["bo"], pa["b2"] = rep(I["L1_attn_bo"]), rep(I["L1_attn_b2"])
    pc = {"l2q": I["L2_attn_Wq"], "l2k": I["L2_attn_Wk"], "l2v": I["L2_attn_Wv"], "l2o": I["L2_attn_Wo"],
          "l2w1": I["L2_ffn_w1"], "l2w2": ktiles(I["L2_ffn_w2"]), "inp": I["L3_attn_in_proj_w"],
          "bp": I["L3_attn_B_proj_w"], "cp": I["L3_attn_C_proj_w"], "outp": ktiles(I["L3_attn_out_proj_w"]),
          "qkv": _np.concatenate([I["L3_attn_q_w"], I["L3_attn_k_w"], I["L3_attn_v_w"]], axis=1),
          "ow": I["L3_attn_o_w"]}
    pd = {}
    for e in range(8):
        pd[f"w1{e}"], pd[f"w2{e}"] = I["L3_ffn_w1"][e], ktiles(I["L3_ffn_w2"][e])
    pm = {"mfc": I["L3_attn_m_fc_w"], "mpj": ktiles(I["L3_attn_m_proj_w"]),
          "afc": I["L3_attn_a_fc_w"], "apj": ktiles(I["L3_attn_a_proj_w"])}
    pi = {"wg": I["L0_ffn_w_gate"].T, "wu": I["L0_ffn_w_up"].T, "wd": ktiles(I["L0_ffn_w_down"].T)}

    pv = {"ln1g": I["L1_attn_ln1_g"].T, "ln1b": I["L1_attn_ln1_b"].T, "ln2g": I["L1_attn_ln2_g"].T,
          "ln2b": I["L1_attn_ln2_b"].T,
          "b1": I["L1_attn_b1"].reshape(4, 4, 128).transpose(2, 0, 1).reshape(128, 16),
          "l2b1": I["L2_ffn_b1"].reshape(4, 128).T,
          "convw": I["L3_attn_conv_w"].reshape(2, 128, 4).transpose(1, 0, 2).reshape(128, 8),
          "convb": I["L3_attn_conv_b"].reshape(2, 128).T,
          "dpar": _np.repeat(I["L3_attn_D_param"], 16).reshape(2, 128).T,
          "mb": I["L1_ffn_b"].T, "dt": rep(I["L3_attn_dt_bias"]), "al": rep(I["L3_attn_A_log"]),
          "qg": rep(I["L3_attn_q_gain"]), "gate": I["L3_ffn_gate_w"], "l2b2": rep(I["L2_ffn_b2"]), "rm0": rep(I["L3_attn_resid_mix_m"][0]),
          "rm1": rep(I["L3_attn_resid_mix_m"][1]), "msc": rep(I["L3_attn_mamba_scale"]),
          "mmsc": rep(I["L3_attn_m_mlp_scale"]), "ra0": rep(I["L3_attn_resid_mix_a"][0]),
          "ra1": rep(I["L3_attn_resid_mix_a"][1]), "asc": rep(I["L3_attn_attn_scale"]),
          "amsc": rep(I["L3_attn_a_mlp_scale"])}
    arrays = {
        "wa": pack(WA, NA, pa), "wb": pack(WB, NB, pb), "wc": pack(WC, NC, pc), "wd": pack(WD, ND, pd), "wm": pack(WM, NM, pm),
        "wi": pack(WI, NI, pi, _np.int32), "ve": pack(VE, NV, pv), "co": shape_constants(), "step": step_constant(),
        "xin": _np.ascontiguousarray(I["L0_attn_inputs"]),
    }
    nc = _bacc.Bacc("TRN2", target_bir_lowering=False, num_devices=1)
    args = [nc.dram_tensor(k, a.shape, _mybir.dt.from_np(a.dtype), kind="ExternalInput").ap()
            for k, a in arrays.items()]
    o = nc.dram_tensor("y", (16, 256, 128), _mybir.dt.float32, kind="ExternalOutput").ap()
    build(nc, *args, o)
    r = _run(nc, [arrays], core_ids=[0])
    return r.results[0]["y"]
```
